# Optimizing a Trainium2 kernel written in Bass

```python
import numpy as np
import jax
import jax.numpy as jnp

def _softmax(x, axis=-1):
    return jax.nn.softmax(x, axis=axis)

def _gelu(x):
    return jax.nn.gelu(x, approximate=True)

def _silu(x):
    return jax.nn.silu(x)

def _sigmoid(x):
    return jax.nn.sigmoid(x)

def _layernorm(x, axis=-1, eps=1e-05):
    m = jnp.mean(x, axis=axis, keepdims=True)
    v = jnp.var(x, axis=axis, keepdims=True)
    return (x - m) / jnp.sqrt(v + eps)

def _scatter_add(tgt, idx, src, axis=0):
    return tgt.at[idx].add(src)

def _segment_sum(src, seg, n):
    return jax.ops.segment_sum(src, seg, n)
kernel_name = 'mk_decoder_preln_d4_seqx_r8_3a02b1'

def setup_inputs(seed: int=0):
    np.random.seed(seed)
    _w = jnp.asarray

    def _rec_inputs():
        import jax
        import jax.numpy as jnp
        _rk = jax.random.key(seed)
        x = -1.394e-06 + 0.9999 * jax.random.normal(jax.random.fold_in(_rk, 1), (16, 64, 128), jnp.float32)
        _lenS = 64 - jax.random.randint(jax.random.fold_in(_rk, 7), (16,), 0, max(1, 64 // 4) + 1, jnp.int32)
        _lenS2 = 64 - jax.random.randint(jax.random.fold_in(_rk, 8), (16,), 0, max(1, 64 // 4) + 1, jnp.int32)
        _ctx_1024P = jax.random.normal(jax.random.fold_in(_rk, 11), (16, 16, 128), jnp.float32)
        _ctx_1024c = jax.random.dirichlet(jax.random.fold_in(_rk, 511), 0.3 * jnp.ones((16,), jnp.float32), (16, 64))
        _ctx_1024t = jnp.einsum('bsk,bkd->bsd', _ctx_1024c, _ctx_1024P)
        _ctx_1024t = _ctx_1024t * jax.lax.rsqrt(jnp.mean(jnp.square(_ctx_1024t)) + 1e-12) * 0.953939
        ctx_1024 = -0.000292821 + 1.00034 * (_ctx_1024t + 0.3 * jax.random.normal(jax.random.fold_in(_rk, 611), (16, 64, 128), jnp.float32))
        _validS = jnp.arange(64)[None, :] < _lenS[:, None]
        _validS2 = jnp.arange(64)[None, :] < _lenS2[:, None]
        _causal = jnp.tril(jnp.ones((64, 64), dtype=bool))
        mask_Bx1x1xS2_ff0 = jnp.where(jnp.ones((16, 1, 1, 64), dtype=bool), 0.0, -1000000000.0).astype(jnp.float32)
        return (x, ctx_1024, mask_Bx1x1xS2_ff0)
    x, ctx_1024, mask_Bx1x1xS2_ff0 = _rec_inputs()

    def _L0_attn_setup():
        import jax, jax.numpy as jnp
        import numpy as np
        DIM = 128
        NUM_HEADS = 16
        HEAD_DIM = DIM // NUM_HEADS
        EPS = 1e-06

        def layer_norm(x, gamma, beta):
            mu = jnp.mean(x, axis=-1, keepdims=True)
            var = jnp.mean(jnp.square(x - mu), axis=-1, keepdims=True)
            return (x - mu) / jnp.sqrt(var + EPS) * gamma + beta

        def apply_rope(q, k):
            seq_len, head_dim = (q.shape[1], q.shape[3])
            half = head_dim // 2
            freq_range = jnp.arange(half, dtype=jnp.float32) / half
            inv_freq = 1.0 / 10000.0 ** freq_range
            t = jnp.arange(seq_len, dtype=jnp.float32)
            freqs = jnp.outer(t, inv_freq)
            emb = jnp.concatenate([freqs, freqs], axis=-1)
            cos = jnp.cos(emb)[None, :, None, :]
            sin = jnp.sin(emb)[None, :, None, :]

            def rotate_half(x):
                x1, x2 = (x[..., :half], x[..., half:])
                return jnp.concatenate([-x2, x1], axis=-1)
            return (q * cos + rotate_half(q) * sin, k * cos + rotate_half(k) * sin)
        key = jax.random.key(seed)
        ks = jax.random.split(key, 4)
        B, S = (2, 256)
        x = jax.random.normal(ks[0], (B, S, DIM), dtype=jnp.float32)
        lim_qkv = float(np.sqrt(6.0 / (DIM + 3 * DIM)))
        w_qkv = jax.random.uniform(ks[1], (3 * DIM, DIM), dtype=jnp.float32, minval=-lim_qkv, maxval=lim_qkv)
        lim_p = float(np.sqrt(6.0 / (DIM + DIM)))
        w_proj = jax.random.uniform(ks[2], (DIM, DIM), dtype=jnp.float32, minval=-lim_p, maxval=lim_p)
        b_proj = jnp.zeros((DIM,), dtype=jnp.float32)
        q_gamma = jnp.ones((HEAD_DIM,), dtype=jnp.float32)
        q_beta = jnp.zeros((HEAD_DIM,), dtype=jnp.float32)
        k_gamma = jnp.ones((HEAD_DIM,), dtype=jnp.float32)
        k_beta = jnp.zeros((HEAD_DIM,), dtype=jnp.float32)
        return {'x': x, 'w_qkv': w_qkv, 'w_proj': w_proj, 'b_proj': b_proj, 'q_gamma': q_gamma, 'q_beta': q_beta, 'k_gamma': k_gamma, 'k_beta': k_beta}
    _L0_attn_all = _L0_attn_setup()
    _L0_attn_in = {k: v for k, v in _L0_attn_all.items() if k in ('w_qkv', 'w_proj', 'b_proj', 'q_gamma', 'q_beta', 'k_gamma', 'k_beta')}
    del _L0_attn_all

    def _L0_xattn_setup():
        import jax, jax.numpy as jnp
        import numpy as np
        import math
        B, S, E = (2, 256, 128)
        H = 16
        DK = E // H
        MAX_DIST = 256

        def _split_heads(x):
            b, s, _ = x.shape
            return x.reshape(b, s, H, DK).transpose(0, 2, 1, 3)
        key = jax.random.key(seed)
        ks = jax.random.split(key, 9)
        sc = 1.0 / math.sqrt(E)
        return {'key': jax.random.normal(ks[0], (B, S, E), jnp.float32), 'query': jax.random.normal(ks[1], (B, S, E), jnp.float32), 'value': jax.random.normal(ks[2], (B, S, E), jnp.float32), 'wq': jax.random.normal(ks[3], (E, E), jnp.float32) * sc, 'wk': jax.random.normal(ks[4], (E, E), jnp.float32) * sc, 'wv': jax.random.normal(ks[5], (E, E), jnp.float32) * sc, 'fc_w': jax.random.normal(ks[6], (E, E), jnp.float32) * sc, 'fc_b': jax.random.normal(ks[7], (E,), jnp.float32) * sc, 'rel_table': jax.random.normal(ks[8], (2 * MAX_DIST - 1, H), jnp.float32) * 0.02}
    _L0_xattn_all = _L0_xattn_setup()
    _L0_xattn_in = {k: v for k, v in _L0_xattn_all.items() if k in ('wq', 'wk', 'wv', 'fc_w', 'fc_b', 'rel_table')}
    del _L0_xattn_all

    def _L0_ffn_setup():
        import jax, jax.numpy as jnp
        import numpy as np
        E, K, H, F = (64, 6, 128, 64)
        SHARED_F = 256
        B, S = (1, 256)
        T = B * S
        CAP = 2 * ((T * K + E - 1) // E)
        key = jax.random.key(seed)
        ks = jax.random.split(key, 6)
        s = 0.05
        return {'hidden_states': jax.random.normal(ks[0], (B, S, H), jnp.float32), 'router_weight': jax.random.normal(ks[1], (E, H), jnp.float32) * s, 'expert_bias': jnp.zeros((E,), jnp.float32), 'w1': jax.random.normal(ks[2], (E, H, F), jnp.float32) * s, 'w2': jax.random.normal(ks[3], (E, F, H), jnp.float32) * s, 'sw1': jax.random.normal(ks[4], (SHARED_F, H), jnp.float32) * s, 'sw2': jax.random.normal(ks[5], (H, SHARED_F), jnp.float32) * s}
    _L0_ffn_all = _L0_ffn_setup()
    _L0_ffn_in = {k: v for k, v in _L0_ffn_all.items() if k in ('router_weight', 'expert_bias', 'w1', 'w2', 'sw1', 'sw2')}
    del _L0_ffn_all

    def _L1_attn_setup():
        import jax, jax.numpy as jnp
        import numpy as np
        B, N, C, H = (8, 128, 128, 16)

        def _masked_softmax(dots, allow):
            neg = jnp.finfo(dots.dtype).min
            logits = jnp.where(allow, dots, neg)
            rowmax = jnp.max(logits, axis=-1, keepdims=True)
            unnorm = jnp.where(allow, jnp.exp(logits - rowmax), 0.0)
            denom = jnp.sum(unnorm, axis=-1, keepdims=True)
            return unnorm / jnp.where(denom == 0, 1.0, denom)
        key = jax.random.key(seed)
        k1, k2, k3 = jax.random.split(key, 3)
        x = jax.random.normal(k1, (B, N, C), dtype=jnp.float32)
        w_qkv = jax.random.normal(k2, (C, 3 * C), dtype=jnp.float32) * (1.0 / np.sqrt(C))
        scale = jnp.ones((H, 1, 1), dtype=jnp.float32)
        w_out = jax.random.normal(k3, (C, C), dtype=jnp.float32) * (1.0 / np.sqrt(C))
        b_out = jnp.zeros((C,), dtype=jnp.float32)
        return {'x': x, 'w_qkv': w_qkv, 'scale': scale, 'w_out': w_out, 'b_out': b_out}
    _L1_attn_all = _L1_attn_setup()
    _L1_attn_in = {k: v for k, v in _L1_attn_all.items() if k in ('w_qkv', 'scale', 'w_out', 'b_out')}
    del _L1_attn_all

    def _L1_xattn_setup():
        import jax, jax.numpy as jnp
        import numpy as np
        B, T, S, H, NH, F = (16, 64, 64, 128, 16, 512)
        HD = H // NH

        def _mha(x, bias, mem, wq, bq, wk, bk, wv, bv, wo, bo):
            b, t, h = x.shape
            q = (x @ wq + bq) * HD ** (-0.5)
            k = mem @ wk + bk
            v = mem @ wv + bv
            split = lambda z: z.reshape(z.shape[0], z.shape[1], NH, HD).transpose(0, 2, 1, 3)
            logits = jnp.einsum('bhqd,bhkd->bhqk', split(q), split(k)) + bias
            w = jax.nn.softmax(logits, axis=-1)
            o = jnp.einsum('bhqk,bhkd->bhqd', w, split(v))
            o = o.transpose(0, 2, 1, 3).reshape(b, t, h)
            return o @ wo + bo

        def _lstm(inp, w, b):
            bsz = inp.shape[0]

            def step(carry, xt):
                c, hdd = carry
                g = jnp.concatenate([xt, hdd], axis=-1) @ w + b
                i, j, f, o = jnp.split(g, 4, axis=-1)
                new_c = jax.nn.sigmoid(f) * c + jax.nn.sigmoid(i) * jnp.tanh(j)
                new_h = jax.nn.sigmoid(o) * jnp.tanh(new_c)
                return ((new_c, new_h), new_h)
            init = (jnp.zeros((bsz, H), inp.dtype), jnp.zeros((bsz, H), inp.dtype))
            _, hs = jax.lax.scan(step, init, inp.transpose(1, 0, 2))
            return hs.transpose(1, 0, 2)
        key = jax.random.key(seed)
        ks = jax.random.split(key, 16)
        d = {}
        d['x'] = jax.random.normal(ks[0], (B, T, H), jnp.float32)
        d['memory'] = jax.random.normal(ks[1], (B, S, H), jnp.float32)
        d['src_bias'] = jnp.zeros((B, 1, 1, S), jnp.float32)
        causal = jnp.triu(jnp.full((T, T), -1000000000.0, jnp.float32), k=1)
        d['tgt_bias'] = causal[None, None]
        sc = 0.02
        names = ['src_wq', 'src_wk', 'src_wv', 'src_wo', 'tgt_wq', 'tgt_wk', 'tgt_wv', 'tgt_wo']
        for i, n in enumerate(names):
            d[n] = jax.random.normal(ks[2 + i], (H, H), jnp.float32) * sc
            d[n.replace('w', 'b')] = jnp.zeros((H,), jnp.float32)
        d['lstm_w'] = jax.random.normal(ks[10], (3 * H, 4 * H), jnp.float32) * sc
        d['lstm_b'] = jnp.zeros((4 * H,), jnp.float32)
        d['ffn_w1'] = jax.random.normal(ks[11], (H, F), jnp.float32) * sc
        d['ffn_b1'] = jnp.zeros((F,), jnp.float32)
        d['ffn_w2'] = jax.random.normal(ks[12], (F, H), jnp.float32) * sc
        d['ffn_b2'] = jnp.zeros((H,), jnp.float32)
        return d
    _L1_xattn_all = _L1_xattn_setup()
    _L1_xattn_in = {k: v for k, v in _L1_xattn_all.items() if k in ('tgt_bias', 'src_wq', 'src_bq', 'src_wk', 'src_bk', 'src_wv', 'src_bv', 'src_wo', 'src_bo', 'tgt_wq', 'tgt_bq', 'tgt_wk', 'tgt_bk', 'tgt_wv', 'tgt_bv', 'tgt_wo', 'tgt_bo', 'lstm_w', 'lstm_b', 'ffn_w1', 'ffn_b1', 'ffn_w2', 'ffn_b2')}
    del _L1_xattn_all

    def _L1_ffn_setup():
        import jax, jax.numpy as jnp
        import numpy as np
        import math
        B, T, D, H, E, TOPK, CAPF = (4, 256, 128, 16, 8, 2, 2.0)
        HD = D // H

        def layernorm(x, g, b, eps=1e-05):
            m = jnp.mean(x, -1, keepdims=True)
            v = jnp.mean(jnp.square(x - m), -1, keepdims=True)
            return (x - m) * jax.lax.rsqrt(v + eps) * g + b

        def block_forward(x, ln1_g, ln1_b, Wqkv, Wproj, ln2_g, ln2_b, Wgate, W1, b1, W2, b2):
            Bb, Tt, d = x.shape
            hd = HD
            half = hd // 2
            h = layernorm(x, ln1_g, ln1_b)
            qkv = (h @ Wqkv).reshape(Bb, Tt, H, 3 * hd)
            q, k, v = (qkv[..., :hd], qkv[..., hd:2 * hd], qkv[..., 2 * hd:])
            inv_freq = 1.0 / 10000.0 ** (jnp.arange(0, hd, 2, dtype=jnp.float32) / hd)
            ang = jnp.arange(Tt, dtype=jnp.float32)[:, None] * inv_freq
            sin = jnp.sin(ang)[None, :, None, :].astype(x.dtype)
            cos = jnp.cos(ang)[None, :, None, :].astype(x.dtype)

            def rope(t):
                t1, t2 = (t[..., :half], t[..., half:])
                return jnp.concatenate([t1 * cos - t2 * sin, t1 * sin + t2 * cos], -1)
            q, k = (rope(q), rope(k))
            scores = jnp.einsum('bqhd,bkhd->bhqk', q, k) / math.sqrt(hd)
            causal = jnp.tril(jnp.ones((Tt, Tt), dtype=bool))
            scores = jnp.where(causal, scores, jnp.asarray(-1000000000.0, scores.dtype))
            probs = jax.nn.softmax(scores, axis=-1)
            attn = jnp.einsum('bhqk,bkhd->bqhd', probs, v).reshape(Bb, Tt, d) @ Wproj
            x = x + attn
            h2 = layernorm(x, ln2_g, ln2_b)
            flat = h2.reshape(-1, d)
            N = flat.shape[0]
            capacity = int(math.ceil(CAPF * N / E))
            gates = jax.nn.softmax((flat @ Wgate).astype(jnp.float32), -1).astype(flat.dtype)
            _, top_inds = jax.lax.top_k(gates, TOPK)
            mask = jnp.zeros((N, E), dtype=bool).at[jnp.arange(N)[:, None], top_inds].set(True)
            pos = jnp.cumsum(mask.astype(jnp.int32), axis=0) * mask - 1
            keep = (pos < capacity) & mask
            t_flat = jnp.repeat(jnp.arange(N), TOPK)
            e_flat = top_inds.reshape(-1)
            p = pos[t_flat, e_flat]
            kp = keep[t_flat, e_flat]
            p_eff = jnp.where(kp, p, capacity)
            exp_in = jnp.zeros((E, capacity, d), flat.dtype).at[e_flat, p_eff].set(flat[t_flat], mode='drop')
            hmid = jax.nn.gelu(jnp.einsum('ecd,edf->ecf', exp_in, W1) + b1[:, None, :], approximate=False)
            exp_out = jnp.einsum('ecf,efd->ecd', hmid, W2) + b2[:, None, :]
            gate = gates[t_flat, e_flat] * kp.astype(flat.dtype)
            p_g = jnp.minimum(p_eff, capacity - 1)
            moe = jnp.zeros((N, d), flat.dtype).at[t_flat].add(exp_out[e_flat, p_g] * gate[:, None])
            return x + moe.reshape(Bb, Tt, d)
        key = jax.random.key(seed)
        ks = jax.random.split(key, 8)
        s = 0.02
        return {'x': jax.random.normal(ks[0], (B, T, D), jnp.float32), 'ln1_g': jnp.ones((D,), jnp.float32), 'ln1_b': jnp.zeros((D,), jnp.float32), 'Wqkv': jax.random.normal(ks[1], (D, 3 * D), jnp.float32) * s, 'Wproj': jax.random.normal(ks[2], (D, D), jnp.float32) * s, 'ln2_g': jnp.ones((D,), jnp.float32), 'ln2_b': jnp.zeros((D,), jnp.float32), 'Wgate': jax.random.normal(ks[3], (D, E), jnp.float32) * s, 'W1': jax.random.normal(ks[4], (E, D, 4 * D), jnp.float32) * s, 'b1': jnp.zeros((E, 4 * D), jnp.float32), 'W2': jax.random.normal(ks[5], (E, 4 * D, D), jnp.float32) * s, 'b2': jnp.zeros((E, D), jnp.float32)}
    _L1_ffn_all = _L1_ffn_setup()
    _L1_ffn_in = {k: v for k, v in _L1_ffn_all.items() if k in ('ln1_g', 'ln1_b', 'Wqkv', 'Wproj', 'ln2_g', 'ln2_b', 'Wgate', 'W1', 'b1', 'W2', 'b2')}
    del _L1_ffn_all

    def _L2_attn_setup():
        import jax, jax.numpy as jnp
        import numpy as np
        B, S, D = (8, 256, 128)
        EPS = 1e-07

        def _loc_weights(steps):
            idx = jnp.arange(steps)
            location = jnp.abs(idx[None, :] - idx[:, None]).astype(jnp.float32)
            lw = 1.0 / (location + EPS) * (location != 0).astype(jnp.float32)
            return lw
        key = jax.random.key(seed)
        kx, kw = jax.random.split(key)
        x = jax.random.normal(kx, (B, S, D), dtype=jnp.float32)
        limit = float(np.sqrt(6.0 / (D + D)))
        W = jax.random.uniform(kw, (D, D), dtype=jnp.float32, minval=-limit, maxval=limit)
        b = jnp.zeros((D,), dtype=jnp.float32)
        return {'x': x, 'W': W, 'b': b}
    _L2_attn_all = _L2_attn_setup()
    _L2_attn_in = {k: v for k, v in _L2_attn_all.items() if k in ('W', 'b')}
    del _L2_attn_all

    def _L2_xattn_setup():
        import jax, jax.numpy as jnp
        import numpy as np
        D_MODEL = 128
        N_HEADS = 16
        HEAD_DIM = D_MODEL // N_HEADS
        key = jax.random.key(seed)
        k1, k2, k3, k4, k5, k6 = jax.random.split(key, 6)
        B, T_q, T_kv = (4, 128, 512)
        s = 1.0 / np.sqrt(D_MODEL)
        return {'query': jax.random.normal(k1, (B, T_q, D_MODEL), dtype=jnp.float32), 'kv_source': jax.random.normal(k2, (B, T_kv, D_MODEL), dtype=jnp.float32), 'w_q': jax.random.normal(k3, (D_MODEL, D_MODEL), dtype=jnp.float32) * s, 'w_k': jax.random.normal(k4, (D_MODEL, D_MODEL), dtype=jnp.float32) * s, 'w_v': jax.random.normal(k5, (D_MODEL, D_MODEL), dtype=jnp.float32) * s, 'w_o': jax.random.normal(k6, (D_MODEL, D_MODEL), dtype=jnp.float32) * s}
    _L2_xattn_all = _L2_xattn_setup()
    _L2_xattn_in = {k: v for k, v in _L2_xattn_all.items() if k in ('w_q', 'w_k', 'w_v', 'w_o')}
    del _L2_xattn_all

    def _L2_ffn_setup():
        import math
        import jax, jax.numpy as jnp
        import numpy as np
        B, T, D, H, E, K, S = (4, 512, 128, 256, 16, 2, 2)
        ROUTE_SCALE = 1.0

        def _swiglu(x, w1, w3, w2):
            return jax.nn.silu(x @ w1) * (x @ w3) @ w2
        key = jax.random.key(seed)
        ks = jax.random.split(key, 9)
        s = 0.02
        return {'x': jax.random.normal(ks[0], (B, T, D), jnp.float32), 'gate_w': jax.random.normal(ks[1], (D, E), jnp.float32) * s, 'gate_b': jnp.zeros((E,), jnp.float32), 'ew1': jax.random.normal(ks[2], (E, D, H), jnp.float32) * s, 'ew3': jax.random.normal(ks[3], (E, D, H), jnp.float32) * s, 'ew2': jax.random.normal(ks[4], (E, H, D), jnp.float32) * s, 'sw1': jax.random.normal(ks[5], (S, D, H), jnp.float32) * s, 'sw3': jax.random.normal(ks[6], (S, D, H), jnp.float32) * s, 'sw2': jax.random.normal(ks[7], (S, H, D), jnp.float32) * s}
    _L2_ffn_all = _L2_ffn_setup()
    _L2_ffn_in = {k: v for k, v in _L2_ffn_all.items() if k in ('gate_w', 'gate_b', 'ew1', 'ew3', 'ew2', 'sw1', 'sw3', 'sw2')}
    del _L2_ffn_all

    def _L3_attn_setup():
        import jax, jax.numpy as jnp
        import numpy as np
        from functools import partial
        B, S, D, H, DK, DV, DFF = (4, 256, 128, 8, 128, 128, 512)
        EPS = 1e-06

        def rms_norm(x):
            return x * jax.lax.rsqrt(jnp.mean(x * x, axis=-1, keepdims=True) + EPS)

        def l2norm(x):
            return x * jax.lax.rsqrt(jnp.sum(x * x, axis=-1, keepdims=True) + EPS)

        def gated_delta_net(h, Wq, Wk, Wv, Wb, Wa, A_log, dt_bias, Wg, o_norm_w, Wo):
            b, s, _ = h.shape
            q = l2norm(jax.nn.silu(h @ Wq).reshape(b, s, H, DK))
            k = l2norm(jax.nn.silu(h @ Wk).reshape(b, s, H, DK))
            v = jax.nn.silu(h @ Wv).reshape(b, s, H, DV)
            beta = jax.nn.sigmoid(h @ Wb)
            g = -jnp.exp(A_log) * jax.nn.softplus(h @ Wa + dt_bias)
            alpha = jnp.exp(g)
            scale = DK ** (-0.5)
            tm = lambda a: jnp.moveaxis(a, 1, 0)
            qs, ks_, vs, als, bts = (tm(q), tm(k), tm(v), tm(alpha), tm(beta))

            def step(Sst, inp):
                q_t, k_t, v_t, a_t, b_t = inp
                Sst = Sst * a_t[..., None, None]
                kv = jnp.einsum('bhd,bhde->bhe', k_t, Sst)
                delta = (v_t - kv) * b_t[..., None]
                Sst = Sst + jnp.einsum('bhd,bhe->bhde', k_t, delta)
                o_t = jnp.einsum('bhd,bhde->bhe', q_t, Sst) * scale
                return (Sst, o_t)
            S0 = jnp.zeros((b, H, DK, DV), dtype=h.dtype)
            _, o = jax.lax.scan(step, S0, (qs, ks_, vs, als, bts))
            o = jnp.moveaxis(o, 0, 1)
            gate = (h @ Wg).reshape(b, s, H, DV)
            o = rms_norm(o) * o_norm_w * jax.nn.silu(gate)
            return o.reshape(b, s, H * DV) @ Wo
        key = jax.random.key(seed)
        ks = jax.random.split(key, 16)
        w = lambda k, shp: jax.random.normal(k, shp, dtype=jnp.float32) * 0.02
        return {'x': jax.random.normal(ks[0], (B, S, D), dtype=jnp.float32), 'Wq': w(ks[1], (D, H * DK)), 'Wk': w(ks[2], (D, H * DK)), 'Wv': w(ks[3], (D, H * DV)), 'Wb': w(ks[4], (D, H)), 'Wa': w(ks[5], (D, H)), 'A_log': jnp.log(jnp.linspace(1.0, 8.0, H).astype(jnp.float32)), 'dt_bias': jax.random.normal(ks[6], (H,), dtype=jnp.float32) * 0.1, 'Wg': w(ks[7], (D, H * DV)), 'o_norm_w': jnp.ones((DV,), dtype=jnp.float32), 'Wo': w(ks[8], (H * DV, D)), 'W_fc': w(ks[9], (D, DFF)), 'W_proj': w(ks[10], (DFF, D))}
    _L3_attn_all = _L3_attn_setup()
    _L3_attn_in = {k: v for k, v in _L3_attn_all.items() if k in ('Wq', 'Wk', 'Wv', 'Wb', 'Wa', 'A_log', 'dt_bias', 'Wg', 'o_norm_w', 'Wo', 'W_fc', 'W_proj')}
    del _L3_attn_all

    def _L3_xattn_setup():
        import jax, jax.numpy as jnp
        import numpy as np
        D_MODEL = 128
        NHEAD = 16
        HEAD_DIM = D_MODEL // NHEAD
        key = jax.random.key(seed)
        ks = jax.random.split(key, 11)
        B, S, D = (4, 256, D_MODEL)
        scale = 1.0 / np.sqrt(D)
        inp = {'q': jax.random.normal(ks[0], (B, S, D), jnp.float32), 'k': jax.random.normal(ks[1], (B, S, D), jnp.float32), 'v': jax.random.normal(ks[2], (B, S, D), jnp.float32), 'Wq': jax.random.normal(ks[3], (D, D), jnp.float32) * scale, 'bq': jnp.zeros((D,), jnp.float32), 'Wk': jax.random.normal(ks[4], (D, D), jnp.float32) * scale, 'bk': jnp.zeros((D,), jnp.float32), 'Wv': jax.random.normal(ks[5], (D, D), jnp.float32) * scale, 'bv': jnp.zeros((D,), jnp.float32), 'Wo': jax.random.normal(ks[6], (D, D), jnp.float32) * scale, 'bo': jnp.zeros((D,), jnp.float32)}
        return inp
    _L3_xattn_all = _L3_xattn_setup()
    _L3_xattn_in = {k: v for k, v in _L3_xattn_all.items() if k in ('Wq', 'bq', 'Wk', 'bk', 'Wv', 'bv', 'Wo', 'bo')}
    del _L3_xattn_all

    def _L3_ffn_setup():
        import jax, jax.numpy as jnp
        import numpy as np
        BLOCK = 32
        W_BITS = 4
        ACT_BITS = 16

        def act_qdq(x):
            qmax = 2.0 ** (ACT_BITS - 1) - 1.0
            scale = jnp.maximum(jnp.max(jnp.abs(x)) / qmax, 1e-12)
            return jnp.clip(jnp.round(x / scale), -qmax - 1.0, qmax) * scale

        def fixed_qdq_u16(x):
            scale = 1.0 / 65536.0
            return jnp.clip(jnp.round(x / scale), 0.0, 65535.0) * scale

        def lpbq_dequant(w):
            O, I = w.shape
            qmax = 2.0 ** (W_BITS - 1) - 1.0
            wb = w.reshape(O, I // BLOCK, BLOCK)
            s = jnp.maximum(jnp.max(jnp.abs(wb), axis=-1, keepdims=True) / qmax, 1e-12)
            wq = jnp.clip(jnp.round(wb / s), -qmax - 1.0, qmax) * s
            return wq.reshape(O, I)
        key = jax.random.key(seed)
        k1, k2, k3, k4 = jax.random.split(key, 4)
        B, S, H, I = (2, 512, 128, 384)
        x = jax.random.normal(k1, (B, S, H), jnp.float32)
        w_gate = jax.random.normal(k2, (I, H), jnp.float32) * 0.02
        w_up = jax.random.normal(k3, (I, H), jnp.float32) * 0.02
        w_down = jax.random.normal(k4, (H, I), jnp.float32) * 0.02
        return {'x': x, 'w_gate': w_gate, 'w_up': w_up, 'w_down': w_down}
    _L3_ffn_all = _L3_ffn_setup()
    _L3_ffn_in = {k: v for k, v in _L3_ffn_all.items() if k in ('w_gate', 'w_up', 'w_down')}
    del _L3_ffn_all
    return {'x': x, 'ctx_1024': ctx_1024, 'mask_Bx1x1xS2_ff0': mask_Bx1x1xS2_ff0, 'L0_attn_w_qkv': _L0_attn_in['w_qkv'], 'L0_attn_w_proj': _L0_attn_in['w_proj'], 'L0_attn_b_proj': _L0_attn_in['b_proj'], 'L0_attn_q_gamma': _L0_attn_in['q_gamma'], 'L0_attn_q_beta': _L0_attn_in['q_beta'], 'L0_attn_k_gamma': _L0_attn_in['k_gamma'], 'L0_attn_k_beta': _L0_attn_in['k_beta'], 'L0_xattn_wq': _L0_xattn_in['wq'], 'L0_xattn_wk': _L0_xattn_in['wk'], 'L0_xattn_wv': _L0_xattn_in['wv'], 'L0_xattn_fc_w': _L0_xattn_in['fc_w'], 'L0_xattn_fc_b': _L0_xattn_in['fc_b'], 'L0_xattn_rel_table': _L0_xattn_in['rel_table'], 'L0_ffn_router_weight': _L0_ffn_in['router_weight'], 'L0_ffn_expert_bias': _L0_ffn_in['expert_bias'], 'L0_ffn_w1': _L0_ffn_in['w1'], 'L0_ffn_w2': _L0_ffn_in['w2'], 'L0_ffn_sw1': _L0_ffn_in['sw1'], 'L0_ffn_sw2': _L0_ffn_in['sw2'], 'L1_attn_w_qkv': _L1_attn_in['w_qkv'], 'L1_attn_scale': _L1_attn_in['scale'], 'L1_attn_w_out': _L1_attn_in['w_out'], 'L1_attn_b_out': _L1_attn_in['b_out'], 'L1_xattn_tgt_bias': _L1_xattn_in['tgt_bias'], 'L1_xattn_src_wq': _L1_xattn_in['src_wq'], 'L1_xattn_src_bq': _L1_xattn_in['src_bq'], 'L1_xattn_src_wk': _L1_xattn_in['src_wk'], 'L1_xattn_src_bk': _L1_xattn_in['src_bk'], 'L1_xattn_src_wv': _L1_xattn_in['src_wv'], 'L1_xattn_src_bv': _L1_xattn_in['src_bv'], 'L1_xattn_src_wo': _L1_xattn_in['src_wo'], 'L1_xattn_src_bo': _L1_xattn_in['src_bo'], 'L1_xattn_tgt_wq': _L1_xattn_in['tgt_wq'], 'L1_xattn_tgt_bq': _L1_xattn_in['tgt_bq'], 'L1_xattn_tgt_wk': _L1_xattn_in['tgt_wk'], 'L1_xattn_tgt_bk': _L1_xattn_in['tgt_bk'], 'L1_xattn_tgt_wv': _L1_xattn_in['tgt_wv'], 'L1_xattn_tgt_bv': _L1_xattn_in['tgt_bv'], 'L1_xattn_tgt_wo': _L1_xattn_in['tgt_wo'], 'L1_xattn_tgt_bo': _L1_xattn_in['tgt_bo'], 'L1_xattn_lstm_w': _L1_xattn_in['lstm_w'], 'L1_xattn_lstm_b': _L1_xattn_in['lstm_b'], 'L1_xattn_ffn_w1': _L1_xattn_in['ffn_w1'], 'L1_xattn_ffn_b1': _L1_xattn_in['ffn_b1'], 'L1_xattn_ffn_w2': _L1_xattn_in['ffn_w2'], 'L1_xattn_ffn_b2': _L1_xattn_in['ffn_b2'], 'L1_ffn_ln1_g': _L1_ffn_in['ln1_g'], 'L1_ffn_ln1_b': _L1_ffn_in['ln1_b'], 'L1_ffn_Wqkv': _L1_ffn_in['Wqkv'], 'L1_ffn_Wproj': _L1_ffn_in['Wproj'], 'L1_ffn_ln2_g': _L1_ffn_in['ln2_g'], 'L1_ffn_ln2_b': _L1_ffn_in['ln2_b'], 'L1_ffn_Wgate': _L1_ffn_in['Wgate'], 'L1_ffn_W1': _L1_ffn_in['W1'], 'L1_ffn_b1': _L1_ffn_in['b1'], 'L1_ffn_W2': _L1_ffn_in['W2'], 'L1_ffn_b2': _L1_ffn_in['b2'], 'L2_attn_W': _L2_attn_in['W'], 'L2_attn_b': _L2_attn_in['b'], 'L2_xattn_w_q': _L2_xattn_in['w_q'], 'L2_xattn_w_k': _L2_xattn_in['w_k'], 'L2_xattn_w_v': _L2_xattn_in['w_v'], 'L2_xattn_w_o': _L2_xattn_in['w_o'], 'L2_ffn_gate_w': _L2_ffn_in['gate_w'], 'L2_ffn_gate_b': _L2_ffn_in['gate_b'], 'L2_ffn_ew1': _L2_ffn_in['ew1'], 'L2_ffn_ew3': _L2_ffn_in['ew3'], 'L2_ffn_ew2': _L2_ffn_in['ew2'], 'L2_ffn_sw1': _L2_ffn_in['sw1'], 'L2_ffn_sw3': _L2_ffn_in['sw3'], 'L2_ffn_sw2': _L2_ffn_in['sw2'], 'L3_attn_Wq': _L3_attn_in['Wq'], 'L3_attn_Wk': _L3_attn_in['Wk'], 'L3_attn_Wv': _L3_attn_in['Wv'], 'L3_attn_Wb': _L3_attn_in['Wb'], 'L3_attn_Wa': _L3_attn_in['Wa'], 'L3_attn_A_log': _L3_attn_in['A_log'], 'L3_attn_dt_bias': _L3_attn_in['dt_bias'], 'L3_attn_Wg': _L3_attn_in['Wg'], 'L3_attn_o_norm_w': _L3_attn_in['o_norm_w'], 'L3_attn_Wo': _L3_attn_in['Wo'], 'L3_attn_W_fc': _L3_attn_in['W_fc'], 'L3_attn_W_proj': _L3_attn_in['W_proj'], 'L3_xattn_Wq': _L3_xattn_in['Wq'], 'L3_xattn_bq': _L3_xattn_in['bq'], 'L3_xattn_Wk': _L3_xattn_in['Wk'], 'L3_xattn_bk': _L3_xattn_in['bk'], 'L3_xattn_Wv': _L3_xattn_in['Wv'], 'L3_xattn_bv': _L3_xattn_in['bv'], 'L3_xattn_Wo': _L3_xattn_in['Wo'], 'L3_xattn_bo': _L3_xattn_in['bo'], 'L3_ffn_w_gate': _L3_ffn_in['w_gate'], 'L3_ffn_w_up': _L3_ffn_in['w_up'], 'L3_ffn_w_down': _L3_ffn_in['w_down']}

def reference(x, ctx_1024, mask_Bx1x1xS2_ff0, L0_attn_w_qkv, L0_attn_w_proj, L0_attn_b_proj, L0_attn_q_gamma, L0_attn_q_beta, L0_attn_k_gamma, L0_attn_k_beta, L0_xattn_wq, L0_xattn_wk, L0_xattn_wv, L0_xattn_fc_w, L0_xattn_fc_b, L0_xattn_rel_table, L0_ffn_router_weight, L0_ffn_expert_bias, L0_ffn_w1, L0_ffn_w2, L0_ffn_sw1, L0_ffn_sw2, L1_attn_w_qkv, L1_attn_scale, L1_attn_w_out, L1_attn_b_out, L1_xattn_tgt_bias, L1_xattn_src_wq, L1_xattn_src_bq, L1_xattn_src_wk, L1_xattn_src_bk, L1_xattn_src_wv, L1_xattn_src_bv, L1_xattn_src_wo, L1_xattn_src_bo, L1_xattn_tgt_wq, L1_xattn_tgt_bq, L1_xattn_tgt_wk, L1_xattn_tgt_bk, L1_xattn_tgt_wv, L1_xattn_tgt_bv, L1_xattn_tgt_wo, L1_xattn_tgt_bo, L1_xattn_lstm_w, L1_xattn_lstm_b, L1_xattn_ffn_w1, L1_xattn_ffn_b1, L1_xattn_ffn_w2, L1_xattn_ffn_b2, L1_ffn_ln1_g, L1_ffn_ln1_b, L1_ffn_Wqkv, L1_ffn_Wproj, L1_ffn_ln2_g, L1_ffn_ln2_b, L1_ffn_Wgate, L1_ffn_W1, L1_ffn_b1, L1_ffn_W2, L1_ffn_b2, L2_attn_W, L2_attn_b, L2_xattn_w_q, L2_xattn_w_k, L2_xattn_w_v, L2_xattn_w_o, L2_ffn_gate_w, L2_ffn_gate_b, L2_ffn_ew1, L2_ffn_ew3, L2_ffn_ew2, L2_ffn_sw1, L2_ffn_sw3, L2_ffn_sw2, L3_attn_Wq, L3_attn_Wk, L3_attn_Wv, L3_attn_Wb, L3_attn_Wa, L3_attn_A_log, L3_attn_dt_bias, L3_attn_Wg, L3_attn_o_norm_w, L3_attn_Wo, L3_attn_W_fc, L3_attn_W_proj, L3_xattn_Wq, L3_xattn_bq, L3_xattn_Wk, L3_xattn_bk, L3_xattn_Wv, L3_xattn_bv, L3_xattn_Wo, L3_xattn_bo, L3_ffn_w_gate, L3_ffn_w_up, L3_ffn_w_down):
    import jax
    import jax.numpy as jnp

    def _L0_attn_ref(x, w_qkv, w_proj, b_proj, q_gamma, q_beta, k_gamma, k_beta):
        import jax, jax.numpy as jnp
        import numpy as np
        DIM = 128
        NUM_HEADS = 16
        HEAD_DIM = DIM // NUM_HEADS
        EPS = 1e-06

        def layer_norm(x, gamma, beta):
            mu = jnp.mean(x, axis=-1, keepdims=True)
            var = jnp.mean(jnp.square(x - mu), axis=-1, keepdims=True)
            return (x - mu) / jnp.sqrt(var + EPS) * gamma + beta

        def apply_rope(q, k):
            seq_len, head_dim = (q.shape[1], q.shape[3])
            half = head_dim // 2
            freq_range = jnp.arange(half, dtype=jnp.float32) / half
            inv_freq = 1.0 / 10000.0 ** freq_range
            t = jnp.arange(seq_len, dtype=jnp.float32)
            freqs = jnp.outer(t, inv_freq)
            emb = jnp.concatenate([freqs, freqs], axis=-1)
            cos = jnp.cos(emb)[None, :, None, :]
            sin = jnp.sin(emb)[None, :, None, :]

            def rotate_half(x):
                x1, x2 = (x[..., :half], x[..., half:])
                return jnp.concatenate([-x2, x1], axis=-1)
            return (q * cos + rotate_half(q) * sin, k * cos + rotate_half(k) * sin)
        B, S, C = x.shape
        H, D = (NUM_HEADS, HEAD_DIM)
        qkv = jnp.einsum('bsc,oc->bso', x, w_qkv).reshape(B, S, 3, H, D)
        q = layer_norm(qkv[:, :, 0], q_gamma, q_beta)
        k = layer_norm(qkv[:, :, 1], k_gamma, k_beta)
        v = qkv[:, :, 2]
        q, k = apply_rope(q, k)
        scale = D ** (-0.5)
        q = q.astype(jnp.float32) * scale
        k = k.astype(jnp.float32)
        v = v.astype(jnp.float32)
        attn = jnp.einsum('bqhd,bkhd->bhqk', q, k)
        attn = jax.nn.softmax(attn, axis=-1)
        out = jnp.einsum('bhqk,bkhd->bqhd', attn, v).reshape(B, S, C)
        out = jnp.einsum('bsc,oc->bso', out, w_proj) + b_proj
        return out

    def _L0_xattn_ref(key, query, value, wq, wk, wv, fc_w, fc_b, rel_table):
        import jax, jax.numpy as jnp
        import numpy as np
        import math
        B, S, E = (2, 256, 128)
        H = 16
        DK = E // H
        MAX_DIST = 256

        def _split_heads(x):
            b, s, _ = x.shape
            return x.reshape(b, s, H, DK).transpose(0, 2, 1, 3)
        b, s, _ = query.shape
        k = _split_heads(key @ wk.T)
        q = _split_heads(query @ wq.T)
        v = _split_heads(value @ wv.T)
        ctx = jnp.arange(s)[:, None]
        mem = jnp.arange(s)[None, :]
        rel = jnp.clip(mem - ctx, -MAX_DIST + 1, MAX_DIST - 1) + MAX_DIST - 1
        bias = rel_table[rel]
        bias = bias.transpose(2, 0, 1)[None]
        scores = jnp.einsum('bhqd,bhkd->bhqk', q, k) / math.sqrt(DK)
        scores = scores + bias
        attn = jax.nn.softmax(scores, axis=-1)
        out = jnp.einsum('bhqk,bhkd->bhqd', attn, v)
        out = out.transpose(0, 2, 1, 3).reshape(b, s, E)
        return out @ fc_w.T + fc_b

    def _L0_ffn_ref(hidden_states, router_weight, expert_bias, w1, w2, sw1, sw2):
        import jax, jax.numpy as jnp
        import numpy as np
        E, K, H, F = (64, 6, 128, 64)
        SHARED_F = 256
        B, S = (1, 256)
        T = B * S
        CAP = 2 * ((T * K + E - 1) // E)
        b, s, h = hidden_states.shape
        x = hidden_states.reshape(-1, h)
        t = x.shape[0]
        logits = x @ router_weight.T
        scores = jax.nn.sigmoid(logits)
        _, top_idx = jax.lax.top_k(scores + expert_bias[None, :], K)
        top_scores = jnp.take_along_axis(scores, top_idx, axis=1)
        probs = top_scores / (jnp.sum(top_scores, axis=-1, keepdims=True) + 1e-20)
        flat_e = top_idx.reshape(-1)
        order = jnp.argsort(flat_e)
        sorted_e = flat_e[order]
        token_of = order // K
        counts = jnp.bincount(flat_e, length=E)
        offsets = jnp.cumsum(counts) - counts
        pos = jnp.arange(t * K) - offsets[sorted_e]
        valid = pos < CAP
        slot = jnp.where(valid, sorted_e * CAP + pos, E * CAP)
        xs = jnp.zeros((E * CAP + 1, h), x.dtype).at[slot].set(x[token_of])
        xs = xs[:-1].reshape(E, CAP, h)
        hmid = jax.nn.gelu(jnp.einsum('ech,ehf->ecf', xs, w1), approximate=True)
        y = jnp.einsum('ecf,efh->ech', hmid, w2).reshape(E * CAP, h)
        pair_w = jnp.where(valid, probs.reshape(-1)[order], 0.0)
        y_pair = y[jnp.minimum(slot, E * CAP - 1)] * pair_w[:, None]
        out = jnp.zeros((t, h), x.dtype).at[token_of].add(y_pair)
        shared = jax.nn.gelu(x @ sw1.T, approximate=True) @ sw2.T
        return (out + shared).reshape(b, s, h)

    def _L1_attn_ref(x, w_qkv, scale, w_out, b_out):
        import jax, jax.numpy as jnp
        import numpy as np
        B, N, C, H = (8, 128, 128, 16)

        def _masked_softmax(dots, allow):
            neg = jnp.finfo(dots.dtype).min
            logits = jnp.where(allow, dots, neg)
            rowmax = jnp.max(logits, axis=-1, keepdims=True)
            unnorm = jnp.where(allow, jnp.exp(logits - rowmax), 0.0)
            denom = jnp.sum(unnorm, axis=-1, keepdims=True)
            return unnorm / jnp.where(denom == 0, 1.0, denom)
        b, n, c = x.shape
        h = scale.shape[0]
        d = c // h
        qkv = x @ w_qkv
        q, k, v = jnp.split(qkv, 3, axis=-1)

        def heads(t):
            return t.reshape(b, n, h, d).transpose(0, 2, 1, 3)
        q, k, v = (heads(q), heads(k), heads(v))
        dots = jnp.einsum('bhnd,bhmd->bhnm', q, k) * scale
        allow = jnp.tril(jnp.ones((n, n), dtype=bool), k=-1)
        attn = _masked_softmax(dots, allow)
        out = jnp.einsum('bhnm,bhmd->bhnd', attn, v)
        out = out.transpose(0, 2, 1, 3).reshape(b, n, c)
        return out @ w_out + b_out

    def _L1_xattn_ref(x, memory, src_bias, tgt_bias, src_wq, src_bq, src_wk, src_bk, src_wv, src_bv, src_wo, src_bo, tgt_wq, tgt_bq, tgt_wk, tgt_bk, tgt_wv, tgt_bv, tgt_wo, tgt_bo, lstm_w, lstm_b, ffn_w1, ffn_b1, ffn_w2, ffn_b2):
        import jax, jax.numpy as jnp
        import numpy as np
        B, T, S, H, NH, F = (16, 64, 64, 128, 16, 512)
        HD = H // NH

        def _mha(x, bias, mem, wq, bq, wk, bk, wv, bv, wo, bo):
            b, t, h = x.shape
            q = (x @ wq + bq) * HD ** (-0.5)
            k = mem @ wk + bk
            v = mem @ wv + bv
            split = lambda z: z.reshape(z.shape[0], z.shape[1], NH, HD).transpose(0, 2, 1, 3)
            logits = jnp.einsum('bhqd,bhkd->bhqk', split(q), split(k)) + bias
            w = jax.nn.softmax(logits, axis=-1)
            o = jnp.einsum('bhqk,bhkd->bhqd', w, split(v))
            o = o.transpose(0, 2, 1, 3).reshape(b, t, h)
            return o @ wo + bo

        def _lstm(inp, w, b):
            bsz = inp.shape[0]

            def step(carry, xt):
                c, hdd = carry
                g = jnp.concatenate([xt, hdd], axis=-1) @ w + b
                i, j, f, o = jnp.split(g, 4, axis=-1)
                new_c = jax.nn.sigmoid(f) * c + jax.nn.sigmoid(i) * jnp.tanh(j)
                new_h = jax.nn.sigmoid(o) * jnp.tanh(new_c)
                return ((new_c, new_h), new_h)
            init = (jnp.zeros((bsz, H), inp.dtype), jnp.zeros((bsz, H), inp.dtype))
            _, hs = jax.lax.scan(step, init, inp.transpose(1, 0, 2))
            return hs.transpose(1, 0, 2)
        c_src = _mha(x, src_bias, memory, src_wq, src_bq, src_wk, src_bk, src_wv, src_bv, src_wo, src_bo)
        c_tgt = _mha(x, tgt_bias, x, tgt_wq, tgt_bq, tgt_wk, tgt_bk, tgt_wv, tgt_bv, tgt_wo, tgt_bo)
        c = c_src + c_tgt
        hiddens = _lstm(jnp.concatenate([x, c], axis=-1), lstm_w, lstm_b)
        hiddens = jax.nn.relu(hiddens @ ffn_w1 + ffn_b1) @ ffn_w2 + ffn_b2
        return hiddens

    def _L1_ffn_ref(x, ln1_g, ln1_b, Wqkv, Wproj, ln2_g, ln2_b, Wgate, W1, b1, W2, b2):
        import jax, jax.numpy as jnp
        import numpy as np
        import math
        B, T, D, H, E, TOPK, CAPF = (4, 256, 128, 16, 8, 2, 2.0)
        HD = D // H

        def layernorm(x, g, b, eps=1e-05):
            m = jnp.mean(x, -1, keepdims=True)
            v = jnp.mean(jnp.square(x - m), -1, keepdims=True)
            return (x - m) * jax.lax.rsqrt(v + eps) * g + b

        def block_forward(x, ln1_g, ln1_b, Wqkv, Wproj, ln2_g, ln2_b, Wgate, W1, b1, W2, b2):
            Bb, Tt, d = x.shape
            hd = HD
            half = hd // 2
            h = layernorm(x, ln1_g, ln1_b)
            qkv = (h @ Wqkv).reshape(Bb, Tt, H, 3 * hd)
            q, k, v = (qkv[..., :hd], qkv[..., hd:2 * hd], qkv[..., 2 * hd:])
            inv_freq = 1.0 / 10000.0 ** (jnp.arange(0, hd, 2, dtype=jnp.float32) / hd)
            ang = jnp.arange(Tt, dtype=jnp.float32)[:, None] * inv_freq
            sin = jnp.sin(ang)[None, :, None, :].astype(x.dtype)
            cos = jnp.cos(ang)[None, :, None, :].astype(x.dtype)

            def rope(t):
                t1, t2 = (t[..., :half], t[..., half:])
                return jnp.concatenate([t1 * cos - t2 * sin, t1 * sin + t2 * cos], -1)
            q, k = (rope(q), rope(k))
            scores = jnp.einsum('bqhd,bkhd->bhqk', q, k) / math.sqrt(hd)
            causal = jnp.tril(jnp.ones((Tt, Tt), dtype=bool))
            scores = jnp.where(causal, scores, jnp.asarray(-1000000000.0, scores.dtype))
            probs = jax.nn.softmax(scores, axis=-1)
            attn = jnp.einsum('bhqk,bkhd->bqhd', probs, v).reshape(Bb, Tt, d) @ Wproj
            x = x + attn
            h2 = layernorm(x, ln2_g, ln2_b)
            flat = h2.reshape(-1, d)
            N = flat.shape[0]
            capacity = int(math.ceil(CAPF * N / E))
            gates = jax.nn.softmax((flat @ Wgate).astype(jnp.float32), -1).astype(flat.dtype)
            _, top_inds = jax.lax.top_k(gates, TOPK)
            mask = jnp.zeros((N, E), dtype=bool).at[jnp.arange(N)[:, None], top_inds].set(True)
            pos = jnp.cumsum(mask.astype(jnp.int32), axis=0) * mask - 1
            keep = (pos < capacity) & mask
            t_flat = jnp.repeat(jnp.arange(N), TOPK)
            e_flat = top_inds.reshape(-1)
            p = pos[t_flat, e_flat]
            kp = keep[t_flat, e_flat]
            p_eff = jnp.where(kp, p, capacity)
            exp_in = jnp.zeros((E, capacity, d), flat.dtype).at[e_flat, p_eff].set(flat[t_flat], mode='drop')
            hmid = jax.nn.gelu(jnp.einsum('ecd,edf->ecf', exp_in, W1) + b1[:, None, :], approximate=False)
            exp_out = jnp.einsum('ecf,efd->ecd', hmid, W2) + b2[:, None, :]
            gate = gates[t_flat, e_flat] * kp.astype(flat.dtype)
            p_g = jnp.minimum(p_eff, capacity - 1)
            moe = jnp.zeros((N, d), flat.dtype).at[t_flat].add(exp_out[e_flat, p_g] * gate[:, None])
            return x + moe.reshape(Bb, Tt, d)
        return block_forward(x, ln1_g, ln1_b, Wqkv, Wproj, ln2_g, ln2_b, Wgate, W1, b1, W2, b2)

    def _L2_attn_ref(x, W, b):
        import jax, jax.numpy as jnp
        import numpy as np
        B, S, D = (8, 256, 128)
        EPS = 1e-07

        def _loc_weights(steps):
            idx = jnp.arange(steps)
            location = jnp.abs(idx[None, :] - idx[:, None]).astype(jnp.float32)
            lw = 1.0 / (location + EPS) * (location != 0).astype(jnp.float32)
            return lw
        steps = x.shape[1]
        x_tran = jnp.matmul(x, W) + b
        weights = jnp.einsum('bsd,btd->bst', x_tran, x)
        lw = _loc_weights(steps)
        weights = jnp.exp(jnp.tanh(weights * lw))
        off_diag = 1.0 - jnp.eye(steps, dtype=weights.dtype)
        weights = weights * off_diag
        weights = weights / (jnp.sum(weights, axis=-1, keepdims=True) + EPS)
        return jnp.matmul(weights, x)

    def _L2_xattn_ref(query, kv_source, w_q, w_k, w_v, w_o):
        import jax, jax.numpy as jnp
        import numpy as np
        D_MODEL = 128
        N_HEADS = 16
        HEAD_DIM = D_MODEL // N_HEADS
        B, T_q, _ = query.shape
        T_kv = kv_source.shape[1]
        q = (query @ w_q.T).reshape(B, T_q, N_HEADS, HEAD_DIM)
        k = (kv_source @ w_k.T).reshape(B, T_kv, N_HEADS, HEAD_DIM)
        v = (kv_source @ w_v.T).reshape(B, T_kv, N_HEADS, HEAD_DIM)
        scale = HEAD_DIM ** (-0.5)
        attn = jax.nn.softmax(jnp.einsum('bqhd,bkhd->bhqk', q, k) * scale, axis=-1)
        out = jnp.einsum('bhqk,bkhd->bqhd', attn, v).reshape(B, T_q, D_MODEL)
        return out @ w_o.T

    def _L2_ffn_ref(x, gate_w, gate_b, ew1, ew3, ew2, sw1, sw3, sw2):
        import math
        import jax, jax.numpy as jnp
        import numpy as np
        B, T, D, H, E, K, S = (4, 512, 128, 256, 16, 2, 2)
        ROUTE_SCALE = 1.0

        def _swiglu(x, w1, w3, w2):
            return jax.nn.silu(x @ w1) * (x @ w3) @ w2
        Bx, Tx, Dx = x.shape
        flat = x.reshape(-1, Dx)
        N = flat.shape[0]
        n_experts = gate_w.shape[1]
        logits = flat @ gate_w
        scores = jax.nn.softmax(logits.astype(jnp.float32), -1) + gate_b
        _, topi = jax.lax.top_k(scores, K)
        weights = jnp.take_along_axis(logits, topi, axis=-1) * ROUTE_SCALE
        weights = weights.astype(flat.dtype)
        capacity = math.ceil(N * K / n_experts * 1.25)

        def per_expert(gid, w1, w3, w2):
            match = topi == gid
            assigned = match.any(-1)
            w_tok = jnp.sum(jnp.where(match, weights, 0.0), -1)
            wm = jnp.where(assigned, w_tok, -jnp.inf)
            vals, idx = jax.lax.top_k(wm, capacity)
            valid = assigned[idx]
            xs = flat[idx]
            y = _swiglu(xs, w1, w3, w2) * jnp.where(valid, vals, 0.0)[:, None]
            return (idx, y)
        idxs, ys = jax.vmap(per_expert)(jnp.arange(n_experts), ew1, ew3, ew2)
        out = jnp.zeros_like(flat).at[idxs.reshape(-1)].add(ys.reshape(-1, Dx))
        shared = jax.vmap(lambda w1, w3, w2: _swiglu(flat, w1, w3, w2))(sw1, sw3, sw2)
        out = out + shared.mean(0)
        return out.reshape(Bx, Tx, Dx)

    def _L3_attn_ref(x, Wq, Wk, Wv, Wb, Wa, A_log, dt_bias, Wg, o_norm_w, Wo, W_fc, W_proj):
        import jax, jax.numpy as jnp
        import numpy as np
        from functools import partial
        B, S, D, H, DK, DV, DFF = (4, 256, 128, 8, 128, 128, 512)
        EPS = 1e-06

        def rms_norm(x):
            return x * jax.lax.rsqrt(jnp.mean(x * x, axis=-1, keepdims=True) + EPS)

        def l2norm(x):
            return x * jax.lax.rsqrt(jnp.sum(x * x, axis=-1, keepdims=True) + EPS)

        def gated_delta_net(h, Wq, Wk, Wv, Wb, Wa, A_log, dt_bias, Wg, o_norm_w, Wo):
            b, s, _ = h.shape
            q = l2norm(jax.nn.silu(h @ Wq).reshape(b, s, H, DK))
            k = l2norm(jax.nn.silu(h @ Wk).reshape(b, s, H, DK))
            v = jax.nn.silu(h @ Wv).reshape(b, s, H, DV)
            beta = jax.nn.sigmoid(h @ Wb)
            g = -jnp.exp(A_log) * jax.nn.softplus(h @ Wa + dt_bias)
            alpha = jnp.exp(g)
            scale = DK ** (-0.5)
            tm = lambda a: jnp.moveaxis(a, 1, 0)
            qs, ks_, vs, als, bts = (tm(q), tm(k), tm(v), tm(alpha), tm(beta))

            def step(Sst, inp):
                q_t, k_t, v_t, a_t, b_t = inp
                Sst = Sst * a_t[..., None, None]
                kv = jnp.einsum('bhd,bhde->bhe', k_t, Sst)
                delta = (v_t - kv) * b_t[..., None]
                Sst = Sst + jnp.einsum('bhd,bhe->bhde', k_t, delta)
                o_t = jnp.einsum('bhd,bhde->bhe', q_t, Sst) * scale
                return (Sst, o_t)
            S0 = jnp.zeros((b, H, DK, DV), dtype=h.dtype)
            _, o = jax.lax.scan(step, S0, (qs, ks_, vs, als, bts))
            o = jnp.moveaxis(o, 0, 1)
            gate = (h @ Wg).reshape(b, s, H, DV)
            o = rms_norm(o) * o_norm_w * jax.nn.silu(gate)
            return o.reshape(b, s, H * DV) @ Wo
        ln_scale = 1.0
        h = gated_delta_net(ln_scale * rms_norm(x), Wq, Wk, Wv, Wb, Wa, A_log, dt_bias, Wg, o_norm_w, Wo)
        x = x + h
        m = ln_scale * rms_norm(x)
        y = jnp.square(jax.nn.relu(m @ W_fc)) @ W_proj
        return x + y

    def _L3_xattn_ref(q, k, v, Wq, bq, Wk, bk, Wv, bv, Wo, bo):
        import jax, jax.numpy as jnp
        import numpy as np
        D_MODEL = 128
        NHEAD = 16
        HEAD_DIM = D_MODEL // NHEAD
        B, S, D = q.shape
        H, Hd = (NHEAD, HEAD_DIM)
        qh = (q @ Wq.T + bq).reshape(B, S, H, Hd).transpose(0, 2, 1, 3)
        kh = (k @ Wk.T + bk).reshape(B, S, H, Hd).transpose(0, 2, 1, 3)
        vh = (v @ Wv.T + bv).reshape(B, S, H, Hd).transpose(0, 2, 1, 3)
        scores = jnp.einsum('bhqd,bhkd->bhqk', qh, kh) / jnp.sqrt(jnp.float32(Hd))
        attn = jax.nn.softmax(scores, axis=-1)
        out = jnp.einsum('bhqk,bhkd->bhqd', attn, vh)
        out = out.transpose(0, 2, 1, 3).reshape(B, S, D)
        return out @ Wo.T + bo

    def _L3_ffn_ref(x, w_gate, w_up, w_down):
        import jax, jax.numpy as jnp
        import numpy as np
        BLOCK = 32
        W_BITS = 4
        ACT_BITS = 16

        def act_qdq(x):
            qmax = 2.0 ** (ACT_BITS - 1) - 1.0
            scale = jnp.maximum(jnp.max(jnp.abs(x)) / qmax, 1e-12)
            return jnp.clip(jnp.round(x / scale), -qmax - 1.0, qmax) * scale

        def fixed_qdq_u16(x):
            scale = 1.0 / 65536.0
            return jnp.clip(jnp.round(x / scale), 0.0, 65535.0) * scale

        def lpbq_dequant(w):
            O, I = w.shape
            qmax = 2.0 ** (W_BITS - 1) - 1.0
            wb = w.reshape(O, I // BLOCK, BLOCK)
            s = jnp.maximum(jnp.max(jnp.abs(wb), axis=-1, keepdims=True) / qmax, 1e-12)
            wq = jnp.clip(jnp.round(wb / s), -qmax - 1.0, qmax) * s
            return wq.reshape(O, I)
        x = act_qdq(x)
        up = act_qdq(x @ lpbq_dequant(w_up).T)
        gate = act_qdq(x @ lpbq_dequant(w_gate).T)
        sig = fixed_qdq_u16(jax.nn.sigmoid(gate))
        gate = act_qdq(gate * sig)
        o = act_qdq(gate * up)
        return o @ lpbq_dequant(w_down).T
    x = x + _L0_attn_ref(_layernorm(x, axis=-1), L0_attn_w_qkv, L0_attn_w_proj, L0_attn_b_proj, L0_attn_q_gamma, L0_attn_q_beta, L0_attn_k_gamma, L0_attn_k_beta)
    x = x + _L0_xattn_ref(ctx_1024, _layernorm(x, axis=-1), ctx_1024, L0_xattn_wq, L0_xattn_wk, L0_xattn_wv, L0_xattn_fc_w, L0_xattn_fc_b, L0_xattn_rel_table)
    x = x + _L0_ffn_ref(_layernorm(x, axis=-1), L0_ffn_router_weight, L0_ffn_expert_bias, L0_ffn_w1, L0_ffn_w2, L0_ffn_sw1, L0_ffn_sw2)
    x = x + _L1_attn_ref(_layernorm(x, axis=-1), L1_attn_w_qkv, L1_attn_scale, L1_attn_w_out, L1_attn_b_out)
    x = x + _L1_xattn_ref(_layernorm(x, axis=-1), ctx_1024, mask_Bx1x1xS2_ff0, L1_xattn_tgt_bias, L1_xattn_src_wq, L1_xattn_src_bq, L1_xattn_src_wk, L1_xattn_src_bk, L1_xattn_src_wv, L1_xattn_src_bv, L1_xattn_src_wo, L1_xattn_src_bo, L1_xattn_tgt_wq, L1_xattn_tgt_bq, L1_xattn_tgt_wk, L1_xattn_tgt_bk, L1_xattn_tgt_wv, L1_xattn_tgt_bv, L1_xattn_tgt_wo, L1_xattn_tgt_bo, L1_xattn_lstm_w, L1_xattn_lstm_b, L1_xattn_ffn_w1, L1_xattn_ffn_b1, L1_xattn_ffn_w2, L1_xattn_ffn_b2)
    x = x + _L1_ffn_ref(_layernorm(x, axis=-1), L1_ffn_ln1_g, L1_ffn_ln1_b, L1_ffn_Wqkv, L1_ffn_Wproj, L1_ffn_ln2_g, L1_ffn_ln2_b, L1_ffn_Wgate, L1_ffn_W1, L1_ffn_b1, L1_ffn_W2, L1_ffn_b2)
    x = x + _L2_attn_ref(_layernorm(x, axis=-1), L2_attn_W, L2_attn_b)
    x = x + _L2_xattn_ref(_layernorm(x, axis=-1), ctx_1024, L2_xattn_w_q, L2_xattn_w_k, L2_xattn_w_v, L2_xattn_w_o)
    x = x + _L2_ffn_ref(_layernorm(x, axis=-1), L2_ffn_gate_w, L2_ffn_gate_b, L2_ffn_ew1, L2_ffn_ew3, L2_ffn_ew2, L2_ffn_sw1, L2_ffn_sw3, L2_ffn_sw2)
    x = x + _L3_attn_ref(_layernorm(x, axis=-1), L3_attn_Wq, L3_attn_Wk, L3_attn_Wv, L3_attn_Wb, L3_attn_Wa, L3_attn_A_log, L3_attn_dt_bias, L3_attn_Wg, L3_attn_o_norm_w, L3_attn_Wo, L3_attn_W_fc, L3_attn_W_proj)
    x = x + _L3_xattn_ref(_layernorm(x, axis=-1), ctx_1024, ctx_1024, L3_xattn_Wq, L3_xattn_bq, L3_xattn_Wk, L3_xattn_bk, L3_xattn_Wv, L3_xattn_bv, L3_xattn_Wo, L3_xattn_bo)
    x = x + _L3_ffn_ref(_layernorm(x, axis=-1), L3_ffn_w_gate, L3_ffn_w_up, L3_ffn_w_down)
    return x

_drawn_inputs = setup_inputs


def setup_inputs(seed=0):
    import zlib

    import numpy as np

    out = dict(_drawn_inputs(seed))
    spreads = {'L0_attn_b_proj': (0.0, 0.1),
     'L0_attn_q_gamma': (1.0, 0.2),
     'L0_attn_q_beta': (0.0, 0.475),
     'L0_attn_k_gamma': (1.0, 0.6),
     'L0_attn_k_beta': (0.0, 0.629),
     'L0_ffn_expert_bias': (0.0, 0.1),
     'L1_attn_scale': (1.0, 0.2),
     'L1_attn_b_out': (0.0, 0.1),
     'L1_xattn_src_bq': (0.0, 0.8),
     'L1_xattn_src_bk': (0.0, 2.0),
     'L1_xattn_src_bv': (0.0, 0.8),
     'L1_xattn_src_bo': (0.0, 0.8),
     'L1_xattn_tgt_bq': (0.0, 0.8),
     'L1_xattn_tgt_bk': (0.0, 2.0),
     'L1_xattn_tgt_bv': (0.0, 0.8),
     'L1_xattn_tgt_bo': (0.0, 0.8),
     'L1_xattn_lstm_b': (0.0, 0.8),
     'L1_xattn_ffn_b1': (0.0, 0.31),
     'L1_xattn_ffn_b2': (0.0, 0.1),
     'L1_ffn_ln1_g': (1.0, 0.6),
     'L1_ffn_ln1_b': (0.0, 0.8),
     'L1_ffn_ln2_g': (1.0, 0.6),
     'L1_ffn_ln2_b': (0.0, 0.8),
     'L1_ffn_b1': (0.0, 0.8),
     'L1_ffn_b2': (0.0, 0.8),
     'L2_attn_b': (0.0, 0.8),
     'L2_ffn_gate_b': (0.0, 0.8),
     'L3_attn_o_norm_w': (1.0, 0.6),
     'L3_xattn_bq': (0.0, 2.0),
     'L3_xattn_bk': (0.0, 2.0),
     'L3_xattn_bv': (0.0, 2.0),
     'L3_xattn_bo': (0.0, 1.779)}
    factors = {'L0_xattn_rel_table': 8.0,
     'L1_xattn_tgt_bias': 8.0,
     'L1_xattn_src_wq': 8.0,
     'L1_xattn_src_wk': 8.0,
     'L1_xattn_src_wv': 8.0,
     'L1_xattn_src_wo': 8.0,
     'L1_xattn_tgt_wq': 8.0,
     'L1_xattn_tgt_wk': 8.0,
     'L1_xattn_tgt_wv': 8.0,
     'L1_xattn_tgt_wo': 8.0,
     'L1_xattn_lstm_w': 8.0,
     'L1_xattn_ffn_w1': 8.0,
     'L1_ffn_Wqkv': 3.995,
     'L1_ffn_Wproj': 3.939,
     'L1_ffn_Wgate': 7.016,
     'L1_ffn_W1': 8.0,
     'L1_ffn_W2': 8.0,
     'L2_ffn_gate_w': 8.0,
     'L2_ffn_ew1': 8.0,
     'L2_ffn_ew3': 8.0,
     'L2_ffn_ew2': 8.0,
     'L2_ffn_sw1': 8.0,
     'L2_ffn_sw3': 8.0,
     'L2_ffn_sw2': 8.0,
     'L3_attn_Wq': 7.962,
     'L3_attn_Wk': 7.954,
     'L3_attn_Wv': 7.921,
     'L3_attn_Wb': 8.0,
     'L3_attn_Wa': 8.0,
     'L3_attn_A_log': 8.0,
     'L3_attn_dt_bias': 8.0,
     'L3_attn_Wg': 7.919,
     'L3_attn_Wo': 7.864,
     'L3_attn_W_fc': 8.0,
     'L3_attn_W_proj': 8.0,
     'L3_ffn_w_gate': 8.0,
     'L3_ffn_w_up': 8.0,
     'L3_ffn_w_down': 8.0,
     'L3_xattn_Wq': 5.18,
     'L3_xattn_Wk': 4.212}
    for name, (base, spread) in spreads.items():
        noise = np.random.default_rng([zlib.crc32(name.encode()), seed]).standard_normal(out[name].shape)
        drawn = base * np.exp(spread * noise) if base else spread * noise
        out[name] = jnp.asarray(drawn.astype(out[name].dtype))
    for name, factor in factors.items():
        out[name] = (out[name] * factor).astype(out[name].dtype)
    return out
```

```python
from contextlib import ExitStack, contextmanager

import numpy as np
import concourse.bass as bass
from concourse import mybir

ALU = mybir.AluOpType
ACT = mybir.ActivationFunctionType
AX = mybir.AxisListType
F32 = mybir.dt.float32
BF16 = mybir.dt.bfloat16

P = 128
SEQ = 64
BATCH = 16
TOK = BATCH * SEQ
TILES = TOK // P
PER = P // SEQ
HEADS = 16
HD = P // HEADS
GROUPS = 4
HALF = 512
SLOT = HD + 1
MAGIC = 12582912.0
NEVER = -3.0e38

WEIGHTS = [
    ("L0a_qkv", 384), ("L0a_o", 128), ("L0x_q", 128), ("L0x_k", 128), ("L0x_v", 128), ("L0x_o", 128),
    ("L0f_router", 64), ("L0f_sw1", 256), ("L0f_sw2", 256),
    ("L1a_q", 128), ("L1a_k", 128), ("L1a_v", 128), ("L1a_o", 128),
    ("L1xs_q", 128), ("L1xs_k", 128), ("L1xs_v", 128), ("L1xs_o", 128),
    ("L1xt_q", 128), ("L1xt_k", 128), ("L1xt_v", 128), ("L1xt_o", 128),
    ("L1x_wx", 512), ("L1x_wc", 512), ("L1x_wh", 512), ("L1x_w1", 512), ("L1x_w2", 512),
    ("L1f_q", 128), ("L1f_k", 128), ("L1f_v", 128), ("L1f_o", 128), ("L1f_gate", 8),
    ("L2a_w", 128), ("L2x_q", 128), ("L2x_k", 128), ("L2x_v", 128), ("L2x_o", 128), ("L2f_gate", 16),
    ("L3a_b", 8), ("L3a_a", 8), ("L3a_fc", 512), ("L3a_proj", 512),
    ("L3x_q", 128), ("L3x_k", 128), ("L3x_v", 128), ("L3x_o", 128),
    ("L3f_w", 1152),
    ("c_L1a_scale", 1), ("c_L1xs_bq", 1), ("c_L1xs_bk", 1), ("c_L1xt_bq", 1), ("c_L1xt_bk", 1),
    ("c_L1x_lstm_b", 4), ("c_L1x_b1", 4), ("c_ln1_g", 1), ("c_ln1_b", 1), ("c_ln2_g", 1), ("c_ln2_b", 1),
    ("c_L1f_b1", 32), ("c_L2a_b", 1), ("c_L3x_bq", 1), ("c_L3x_bk", 1),
    ("c_tgt_bias", 64),
]
ROWS = [
    ("L0a_o", 128), ("L0a_gamma", 16), ("L0a_beta", 16), ("L0x_o", 128), ("L0f_bias", 64), ("L1a_o", 128),
    ("L1xs_v", 128), ("L1xt_v", 128), ("L1xs_o", 128), ("L1xt_o", 128), ("L1x_b2", 128), ("L2f_b", 16),
    ("L3a_Alog", 8), ("L3a_dt", 8), ("L3a_norm", 128), ("L3x_v", 128), ("L3x_o", 128),
]
CONSTS = [
    ("ident", 128), ("gmask", GROUPS), ("emask", HEADS), ("tri_inc", 128), ("tri_str", 128), ("ones", 128),
    ("level", 6 * 128), ("lw", 128), ("off", 128), ("rope_c", 8), ("rope_s", 8), ("causal", 64),
    ("strict", 64), ("notfirst", 1), ("upper", 128), ("pick", 32 * 128), ("two", 128),
]


def offsets(table):
    at, out = 0, {}
    for name, n in table:
        out[name] = (at, n)
        at += n
    return out, at


W_AT, W_COLS = offsets(WEIGHTS)
R_AT, R_COLS = offsets(ROWS)
C_AT, C_COLS = offsets(CONSTS)


def shape_constants():
    p = np.arange(P)
    q = p % SEQ
    same = (p[:, None] // SEQ) == (p[None, :] // SEQ)
    c = {}
    c["ident"] = np.eye(P)
    c["gmask"] = (p[:, None] // HD) % 4 == np.arange(GROUPS)[None, :]
    c["emask"] = (p[:, None] // SEQ) == np.arange(HEADS)[None, :] % 2
    c["tri_inc"] = same & (p[:, None] <= p[None, :])
    c["tri_str"] = same & (p[:, None] > p[None, :])
    c["ones"] = np.ones((P, P))
    levels = []
    for l in range(6):
        m = 2 ** l
        levels.append((p[:, None] // (2 * m) == p[None, :] // (2 * m))
                      & (p[:, None] // m % 2 == 0) & (p[None, :] // m % 2 == 1))
    c["level"] = np.concatenate(levels, 1)
    d = np.abs(q[:, None] - q[None, :]).astype(np.float32)
    c["lw"] = np.where(same & (d != 0), np.float32(1) / (d + np.float32(1e-7)), 0)
    c["off"] = same & (d != 0)
    inv = (1.0 / 10000.0 ** (np.arange(4, dtype=np.float32) / 4)).astype(np.float32)
    ang = (q[:, None].astype(np.float32) * inv[None, :]).astype(np.float32)
    c["rope_c"] = np.concatenate([np.cos(ang), np.cos(ang)], 1)
    c["rope_s"] = np.concatenate([-np.sin(ang), np.sin(ang)], 1)
    k = np.arange(SEQ)
    c["causal"] = np.where(k[None, :] > q[:, None], -1e9, 0)
    c["strict"] = np.where(k[None, :] >= q[:, None], -1e30, 0)
    c["notfirst"] = (q != 0)[:, None]
    c["upper"] = p[:, None] < p[None, :]
    pick = np.zeros((P, 32, P))
    for i in range(32):
        for r in range(P):
            if r % 64 // 2 == i:
                pick[r, i, (r % 2) * 64:(r % 2) * 64 + 64] = 1
    c["pick"] = pick.reshape(P, 32 * P)
    two = np.zeros((P, P))
    two[0, :SEQ] = 1
    two[1, SEQ:] = 1
    c["two"] = two
    return np.concatenate([np.asarray(c[n], np.float32) for n, _ in CONSTS], 1)


class Chain:

    def __init__(self, eng, sem, base=0):
        self.eng, self.sem, self.base, self.n = eng, sem, base, 0

    def mark(self, ins):
        ins.then_inc(self.sem, 1)
        self.n += 1

    def join(self):
        self.eng.wait_ge(self.sem, self.base + self.n)

    def step(self, ins):
        self.mark(ins)
        self.join()


def decoder_kernel(nc, d, out, first=0, last=12):
    ctx = ExitStack()
    uid = [0]

    def sb(name, shape, dt=F32):
        return ctx.enter_context(nc.sbuf_tensor(name, shape, dt))

    @contextmanager
    def phase(*names):
        uid[0] += 1
        sems = [nc.alloc_semaphore(f"{n}_{uid[0]}") for n in names]
        with nc.Block() as block:
            yield block, dict(zip(names, sems))
        nc.clear_and_free_semaphores(sems)
        nc.all_engine_barrier()

    with ctx:
        PS = ctx.enter_context(nc.psum_tensor("PS", [P, 8, HALF], F32))
        WT = sb("WT", [P, W_COLS])
        RW = sb("RW", [P, R_COLS])
        CS = sb("CS", [P, C_COLS])
        X = sb("X", [P, TILES, P])
        XN = sb("XN", [P, TILES, P])
        XR = sb("XR", [P, TILES, P])
        HT = sb("HT", [P, TOK])
        CT = sb("CT", [P, TOK])
        QT = sb("QT", [P, TOK])
        KT = sb("KT", [P, TOK])
        VD = sb("VD", [P, BATCH, HEADS, SLOT])
        identb = sb("identb", [P, P], BF16)
        causalb = sb("causalb", [P, SEQ], BF16)
        strictb = sb("strictb", [P, SEQ], BF16)
        upperb = sb("upperb", [P, P], BF16)
        onesb = sb("onesb", [P, P], BF16)
        pickb = sb("pickb", [P, 32 * P], BF16)
        stats = sb("stats", [P, TILES, 6])
        mv = sb("mv", [P, TILES, 2])
        rstd = sb("rstd", [P, TILES])
        SRC = sb("SRC", [2, TILES, SEQ])
        BIG = [sb(f"BIG{i}", [P, 4096]) for i in range(4)]
        REL = BIG[3][:, 0:1024].rearrange("p (h k) -> p h k", h=HEADS)

        def w(name):
            a, n = W_AT[name]
            return WT[:, a:a + n]

        def row(name):
            a, n = R_AT[name]
            return RW[:, a:a + n]

        def cst(name):
            a, n = C_AT[name]
            return CS[:, a:a + n]

        ident = cst("ident")

        with phase("loaded", "made") as (block, s):
            @block.sync
            def _(sp):
                sp.dma_start(X[:, :, :], d["x"]).then_inc(s["loaded"], 16)
                sp.dma_start(CS[:, :], d["consts"]).then_inc(s["loaded"], 16)
                sp.dma_start(CT[:, :], d["ctxT"]).then_inc(s["loaded"], 16)
                sp.dma_start(SRC[:, :, :], d["src_bias"]).then_inc(s["loaded"], 16)

            @block.scalar
            def _(act):
                act.dma_start(WT[:, :], d["weights"]).then_inc(s["loaded"], 16)
                act.dma_start(RW[:, :], d["rows"][0:1, :].broadcast_to([P, R_COLS])).then_inc(s["loaded"], 16)
                act.wait_ge(s["loaded"], 96)

            @block.vector
            def _(dve):
                dve.wait_ge(s["loaded"], 96)
                for dst, name in ((identb, "ident"), (causalb, "causal"), (strictb, "strict"),
                                  (upperb, "upper"), (onesb, "ones"), (pickb, "pick")):
                    dve.tensor_copy(dst[:, :], cst(name)).then_inc(s["made"], 1)
                dve.tensor_copy(VD[:, :, :, HD],
                                cst("emask").unsqueeze(1).broadcast_to([P, BATCH, HEADS])).then_inc(s["made"], 1)
                dve.wait_ge(s["made"], 7)

        def normalize(src, dst, dstT, eps, gain=None, shift=None, rms=False):
            with phase("stat", "rooted", "normed", "turned", "copied") as (block, s):
                @block.vector
                def _(dve):
                    c = Chain(dve, s["stat"])
                    for t in range(TILES):
                        c.mark(dve.bn_stats(stats[:, t, :], src[:, t, :]))
                    c.join()
                    for t in range(TILES):
                        c.mark(dve.bn_aggr(mv[:, t, :], stats[:, t, :]))
                    c.join()
                    if rms:
                        c.step(dve.tensor_tensor(rstd[:, :], mv[:, :, 0], mv[:, :, 0], ALU.mult))
                        c.step(dve.tensor_tensor(mv[:, :, 1], mv[:, :, 1], rstd[:, :], ALU.add))
                        c.step(dve.memset(mv[:, :, 0], 0.0))
                    c.step(dve.tensor_scalar(rstd[:, :], mv[:, :, 1], eps, None, ALU.add))
                    dve.wait_ge(s["rooted"], 1)
                    c.step(dve.reciprocal(rstd[:, :], rstd[:, :]))
                    for t in range(TILES):
                        dve.tensor_scalar(dst[:, t, :], src[:, t, :], mv[:, t, 0:1], rstd[:, t:t + 1],
                                          ALU.subtract, ALU.mult).then_inc(s["normed"], 1)

                @block.tensor
                def _(pe):
                    for t in range(TILES):
                        pe.wait_ge(s["normed"], t + 1)
                        pe.transpose(PS[:, t // 4, (t % 4) * P:(t % 4 + 1) * P], dst[:, t, :], ident)\
                          .then_inc(s["turned"], 1)

                @block.scalar
                def _(act):
                    act.wait_ge(s["stat"], 2 * TILES + (4 if rms else 1))
                    act.activation(rstd[:, :], rstd[:, :], ACT.Sqrt).then_inc(s["rooted"], 1)
                    for h in range(2):
                        act.wait_ge(s["turned"], 4 * h + 4)
                        o = dstT[:, h * HALF:(h + 1) * HALF]
                        if gain is None:
                            act.activation(o, PS[:, h, :], ACT.Copy).then_inc(s["copied"], 1)
                        else:
                            act.activation(o, PS[:, h, :], ACT.Identity, bias=shift, scale=gain)\
                               .then_inc(s["copied"], 1)
                    act.wait_ge(s["copied"], 2)

        def project(items, values=None):
            twice = BIG[3][:, 1024:3072].rearrange("p (b c k) -> p b c k", b=BATCH, c=2)
            with phase("made", "evac", "twice", "vmade", "vevac") as (block, s):
                @block.scalar
                def _(act):
                    if values:
                        act.activation(twice, values[0][:, :].rearrange("p (b k) -> p b k", b=BATCH).unsqueeze(2)
                                       .broadcast_to([P, BATCH, 2, SEQ]), ACT.Copy).then_inc(s["twice"], 1)

                @block.tensor
                def _(pe):
                    for n, (dst, wt, src, bias, factor) in enumerate(items):
                        if n >= 2:
                            pe.wait_ge(s["evac"], n - 1)
                        for h in range(2):
                            pe.matmul(PS[:, 2 * (n % 2) + h, :], wt, src[:, h * HALF:(h + 1) * HALF],
                                      start=True, stop=True).then_inc(s["made"], 1)
                    if values:
                        src, wv, brow = values
                        pe.wait_ge(s["twice"], 1)
                        for b in range(BATCH):
                            o = PS[:, 4 + b // 4, (b % 4) * P:(b % 4 + 1) * P]
                            keys = BIG[3][:, 1024 + b * P:1024 + (b + 1) * P]
                            mm = pe.matmul(o, keys, wv, start=True, stop=brow is None)
                            if brow is not None:
                                mm = pe.matmul(o, cst("ones")[0:1, :], brow[0:1, :], start=False, stop=True)
                            mm.then_inc(s["vmade"], 1)

                def evacuate(eng, n):
                    dst, wt, src, bias, factor = items[n]
                    eng.wait_ge(s["made"], 2 * n + 2)
                    view = dst[:, :].rearrange("p (a b) -> p a b", a=2)
                    return view, PS[:, 2 * (n % 2):2 * (n % 2) + 2, :], bias, factor

                @block.vector
                def _(dve):
                    for n in range(len(items)):
                        o, i, bias, factor = evacuate(dve, n)
                        dve.tensor_scalar(o, i, 0.0 if bias is None else bias, factor, ALU.add, ALU.mult)\
                           .then_inc(s["evac"], 1)
                    dve.wait_ge(s["evac"], len(items)) if items else None
                    if values:
                        em = cst("emask").unsqueeze(1).unsqueeze(3).broadcast_to([P, 4, HEADS, HD])
                        for g in range(BATCH // 4):
                            dve.wait_ge(s["vmade"], 4 * g + 4)
                            dve.tensor_tensor(VD[:, 4 * g:4 * g + 4, :, 0:HD],
                                              PS[:, 4 + g, :].rearrange("p (b h e) -> p b h e", b=4, h=HEADS),
                                              em, ALU.mult).then_inc(s["vevac"], 1)
                        dve.wait_ge(s["vevac"], BATCH // 4)

        def token_qk(wq, wk, rotate_norm, factor):
            QK = BIG[0][:, 0:2048]
            A = BIG[1][:, 0:2048]
            B = BIG[2][:, 0:2048]
            G = 2 * TILES * HEADS
            grp = lambda a: a.rearrange("p (g e) -> p g e", e=HD)
            sm = BIG[3][:, 0:G]
            va = BIG[3][:, 512:512 + G]
            rs = BIG[3][:, 1024:1024 + G]
            wide = lambda a: a.unsqueeze(2).broadcast_to([P, G, HD])
            with phase("made", "copied", "vec", "rooted", "ready", "turned", "evac") as (block, s):
                @block.tensor
                def _(pe):
                    for t in range(TILES):
                        ht = HT[:, t * P:(t + 1) * P]
                        o = PS[:, t // 2, (t % 2) * 256:(t % 2) * 256 + 256]
                        pe.matmul(o[:, 0:P], ht, wq, start=True, stop=True)
                        pe.matmul(o[:, P:2 * P], ht, wk, start=True, stop=True).then_inc(s["made"], 1)
                    pe.wait_ge(s["ready"], 1)
                    for n in range(2):
                        for t in range(TILES):
                            pe.transpose(PS[:, 4 + 2 * n + t // 4, (t % 4) * P:(t % 4 + 1) * P],
                                         QK[:, (2 * t + n) * P:(2 * t + n + 1) * P], ident).then_inc(s["turned"], 1)

                @block.scalar
                def _(act):
                    act.wait_ge(s["made"], TILES)
                    act.activation(QK.rearrange("p (a b) -> p a b", a=4), PS[:, 0:4, :], ACT.Copy).then_inc(s["copied"], 1)
                    if rotate_norm:
                        act.wait_ge(s["vec"], 6)
                        act.activation(rs, va, ACT.Sqrt).then_inc(s["rooted"], 1)
                    for n in range(2):
                        act.wait_ge(s["turned"], TILES * (n + 1))
                        dst = (QT, KT)[n]
                        act.activation(dst[:, :].rearrange("p (a b) -> p a b", a=2), PS[:, 4 + 2 * n:6 + 2 * n, :],
                                       ACT.Copy, scale=factor if n == 0 else 1.0).then_inc(s["evac"], 1)
                    act.wait_ge(s["evac"], 2)

                @block.vector
                def _(dve):
                    c = Chain(dve, s["vec"])
                    dve.wait_ge(s["copied"], 1)
                    if rotate_norm:
                        c.step(dve.tensor_reduce(sm, grp(QK), AX.X, ALU.add))
                        c.step(dve.tensor_scalar(sm, sm, 1.0 / HD, None, ALU.mult))
                        c.step(dve.tensor_tensor(grp(QK), grp(QK), wide(sm), ALU.subtract))
                        c.step(dve.tensor_tensor(A, QK, QK, ALU.mult))
                        c.step(dve.tensor_reduce(va, grp(A), AX.X, ALU.add))
                        c.step(dve.tensor_scalar(va, va, 1.0 / HD, 1e-6, ALU.mult, ALU.add))
                        dve.wait_ge(s["rooted"], 1)
                        c.step(dve.reciprocal(rs, rs))
                        c.step(dve.tensor_tensor(grp(QK), grp(QK), wide(rs), ALU.mult))
                        four = QK.rearrange("p (t n h e) -> p t n h e", t=TILES, n=2, e=HD)
                        for name, op in (("L0a_gamma", ALU.mult), ("L0a_beta", ALU.add)):
                            for n in range(2):
                                r = row(name)[:, n * HD:(n + 1) * HD].unsqueeze(1).unsqueeze(1)\
                                    .broadcast_to([P, TILES, HEADS, HD])
                                c.mark(dve.tensor_tensor(four[:, :, n], four[:, :, n], r, op))
                            c.join()
                    rc = cst("rope_c").unsqueeze(1).broadcast_to([P, G, HD])
                    h4 = HD // 2
                    c.mark(dve.tensor_tensor(grp(A), grp(QK), rc, ALU.mult))
                    for x in range(2):
                        sn = cst("rope_s")[:, x * h4:(x + 1) * h4].unsqueeze(1).broadcast_to([P, G, h4])
                        c.mark(dve.tensor_tensor(grp(B)[:, :, x * h4:(x + 1) * h4],
                                                 grp(QK)[:, :, (1 - x) * h4:(2 - x) * h4], sn, ALU.mult))
                    c.join()
                    dve.tensor_tensor(QK, A, B, ALU.add).then_inc(s["ready"], 1)

        KM = [BIG[1][:, t * 512:(t + 1) * 512].rearrange("p (r k) -> p r k", r=GROUPS) for t in range(TILES)]
        EX = [BIG[2][:, i * 1024:(i + 1) * 1024] for i in range(2)]
        PT = [BIG[2][:, 2048 + i * 1024:3072 + i * 1024].rearrange("p (j q) -> p j q", j=8) for i in range(2)]
        ON = [BIG[0][:, 2048 + i * 128:2176 + i * 128] for i in range(2)]
        OT = [BIG[0][:, 2304 + i * 128:2432 + i * 128] for i in range(2)]
        MX = [BIG[0][:, 2560 + i * 16:2576 + i * 16] for i in range(2)]
        RI = [BIG[0][:, 2592 + i * 16:2608 + i * 16] for i in range(2)]
        SB = BIG[0][:, 3072:3584].rearrange("p (t k) -> p t k", t=TILES)

        def attend(wo, dst, bias=None, bias_row=None):
            LAST = TILES + 4
            added_bias = bias in ("tgt", "src", "rel")
            with phase("masked", "scored", "vec", "subbed", "exped", "turned",
                       "copied", "mixed", "normed", "oturned", "ocopied", "projected", "added", "based",
                       "rowed", "spread") as (block, s):
                four = lambda a: a.rearrange("p (g r k) -> p g r k", g=4, r=4)

                @block.gpsimd
                def _(pool):
                    for t in range(TILES):
                        pool.tensor_tensor(
                            KM[t], KT[:, t * P:(t + 1) * P].unsqueeze(1).broadcast_to([P, GROUPS, P]),
                            cst("gmask").unsqueeze(2).broadcast_to([P, GROUPS, P]), ALU.mult).then_inc(s["masked"], 1)
                        if t == 1 and bias_row is not None:
                            pool.tensor_tensor(dst[:, :, :], dst[:, :, :],
                                               bias_row.unsqueeze(1).broadcast_to([P, TILES, P]), ALU.add)\
                                .then_inc(s["based"], 1)

                @block.tensor
                def _(pe):
                    if bias == "src":
                        pe.matmul(PS[:, 7, :], cst("two")[0:2, :], SRC[:, :, :], start=True, stop=True)\
                          .then_inc(s["rowed"], 1)

                    def scores(t):
                        pe.wait_ge(s["masked"], t + 1)
                        if t > 0:
                            pe.wait_ge(s["subbed"], t)
                        for g in range(4):
                            if bias in ("causal", "strict"):
                                m = (causalb if bias == "causal" else strictb)[:, :]
                                pe.matmul(PS[:, g, 0:256].rearrange("p (r k) -> p r k", r=4), identb[:, :],
                                          m.unsqueeze(1).broadcast_to([P, 4, SEQ]), start=True, stop=False)
                        for b in range(PER):
                            q = slice(b * SEQ, (b + 1) * SEQ)
                            for g in range(4):
                                rows = slice(32 * g, 32 * g + 32)
                                mm = pe.matmul(PS[q, g, 0:256].rearrange("p (r k) -> p r k", r=4),
                                               QT[rows, t * P + b * SEQ:t * P + (b + 1) * SEQ], KM[t][rows, :, q],
                                               start=bias is None or added_bias, stop=True)
                        mm.then_inc(s["scored"], 1)

                    def turn_probs(t):
                        pe.wait_ge(s["exped"], t + 1)
                        if t > 0:
                            pe.wait_ge(s["copied"], t)
                        for j in range(8):
                            mm = pe.transpose(PS[:, 4 + j // 4, (j % 4) * P:(j % 4 + 1) * P],
                                              EX[t % 2][:, j * P:(j + 1) * P], ident)
                        mm.then_inc(s["turned"], 1)

                    def mix(t):
                        pe.wait_ge(s["copied"], t + 1)
                        if t > 0:
                            pe.wait_ge(s["normed"], t)
                        for b in range(PER):
                            q = slice(b * SEQ, (b + 1) * SEQ)
                            for j in range(8):
                                mm = pe.matmul(PS[q, 6, 2 * SLOT * j:2 * SLOT * (j + 1)], PT[t % 2][:, j, q],
                                               VD[:, PER * t + b, 2 * j:2 * j + 2, :], start=True, stop=True)
                        mm.then_inc(s["mixed"], 1)

                    def turn_out(t):
                        pe.wait_ge(s["normed"], t + 1)
                        if t > 0:
                            pe.wait_ge(s["added"], t)
                        elif bias == "src":
                            pe.wait_ge(s["spread"], 1)
                        pe.transpose(PS[:, 7, 0:P], ON[t % 2], ident).then_inc(s["oturned"], 1)

                    def project_out(t):
                        pe.wait_ge(s["ocopied"], t + 1)
                        pe.matmul(PS[:, 7, P:2 * P], OT[t % 2], wo, start=True, stop=True).then_inc(s["projected"], 1)

                    for step in range(LAST):
                        for stage, lag in ((scores, 0), (project_out, 4), (turn_probs, 1), (mix, 2), (turn_out, 3)):
                            if 0 <= step - lag < TILES:
                                stage(step - lag)

                @block.vector
                def _(dve):
                    c = Chain(dve, s["vec"])
                    if bias == "src":
                        dve.wait_ge(s["rowed"], 1)
                        dve.tensor_copy(SB, PS[:, 7, :].rearrange("p (t k) -> p t k", t=TILES)).then_inc(s["spread"], 1)
                        dve.wait_ge(s["spread"], 1)

                    def shift(t):
                        S = PS[:, 0:4, 0:256].rearrange("p g (r k) -> p g r k", r=4)
                        E = four(EX[t % 2])
                        dve.wait_ge(s["scored"], t + 1)
                        if t > 1:
                            dve.wait_ge(s["turned"], t - 1)
                        m = MX[t % 2].rearrange("p (g r) -> p g r", g=4)
                        if added_bias:
                            if bias == "rel":
                                a = REL.rearrange("p (g r) k -> p g r k", g=4)
                            else:
                                a = w("c_tgt_bias") if bias == "tgt" else SB[:, t, :]
                                a = a.unsqueeze(1).unsqueeze(1).broadcast_to([P, 4, 4, SEQ])
                            c.step(dve.tensor_tensor(E, S, a, ALU.add))
                            S = E
                        c.step(dve.tensor_reduce(m, S, AX.X, ALU.max))
                        dve.tensor_tensor(E, S, m.unsqueeze(3).broadcast_to([P, 4, 4, SEQ]), ALU.subtract)\
                            .then_inc(s["subbed"], 1)

                    def add(t):
                        dve.wait_ge(s["projected"], t + 1)
                        dve.tensor_tensor(dst[:, t, :], dst[:, t, :], PS[:, 7, P:2 * P], ALU.add).then_inc(s["added"], 1)

                    def norm(t):
                        dve.wait_ge(s["mixed"], t + 1)
                        if t > 1:
                            dve.wait_ge(s["oturned"], t - 1)
                        O = PS[:, 6, 0:HEADS * SLOT].rearrange("p (h e) -> p h e", h=HEADS)
                        c.step(dve.reciprocal(RI[t % 2], O[:, :, HD]))
                        if bias == "strict":
                            c.step(dve.tensor_scalar(RI[t % 2], RI[t % 2], cst("notfirst"), None, ALU.mult))
                        dve.tensor_tensor(ON[t % 2].rearrange("p (h e) -> p h e", h=HEADS), O[:, :, 0:HD],
                                          RI[t % 2].unsqueeze(2).broadcast_to([P, HEADS, HD]), ALU.mult)\
                            .then_inc(s["normed"], 1)

                    for step in range(LAST):
                        for stage, lag in ((shift, 0), (add, 4), (norm, 2)):
                            if 0 <= step - lag < TILES:
                                if stage is add and step == lag and bias_row is not None:
                                    dve.wait_ge(s["based"], 1)
                                stage(step - lag)
                    dve.wait_ge(s["added"], TILES)

                @block.scalar
                def _(act):
                    def copy_probs(t):
                        act.wait_ge(s["turned"], t + 1)
                        if t > 1:
                            act.wait_ge(s["mixed"], t - 1)
                        act.activation(PT[t % 2].rearrange("p (a b) q -> p a (b q)", a=2), PS[:, 4:6, :], ACT.Copy)\
                            .then_inc(s["copied"], 1)

                    def exponent(t):
                        act.wait_ge(s["subbed"], t + 1)
                        act.activation(EX[t % 2], EX[t % 2], ACT.Exp).then_inc(s["exped"], 1)

                    def copy_out(t):
                        act.wait_ge(s["oturned"], t + 1)
                        if t > 1:
                            act.wait_ge(s["projected"], t - 1)
                        act.activation(OT[t % 2], PS[:, 7, 0:P], ACT.Copy).then_inc(s["ocopied"], 1)

                    for step in range(LAST):
                        for stage, lag in ((copy_probs, 1), (exponent, 0), (copy_out, 3)):
                            if 0 <= step - lag < TILES:
                                stage(step - lag)

        def turn(src, dstT):
            with phase("turned", "copied") as (block, s):
                @block.tensor
                def _(pe):
                    for t in range(TILES):
                        pe.transpose(PS[:, t // 4, (t % 4) * P:(t % 4 + 1) * P], src[:, t, :], ident)\
                          .then_inc(s["turned"], 1)

                @block.scalar
                def _(act):
                    for h in range(2):
                        act.wait_ge(s["turned"], 4 * h + 4)
                        act.activation(dstT[:, h * HALF:(h + 1) * HALF], PS[:, h, :], ACT.Copy).then_inc(s["copied"], 1)
                    act.wait_ge(s["copied"], 2)

        GATE = sb("GATE", [P, TILES, 64])

        def route(srcT, wg, E, K, kind, capacity):
            V = E + 8 - K
            n = TILES * E
            cut = lambda i, m: BIG[0][:, i * 512:i * 512 + TILES * m].rearrange("p (t e) -> p t e", t=TILES)
            LG, SCORE, MASK, PROB, TOP = cut(0, E), cut(1, E), cut(2, E), cut(3, E), cut(4, 8)
            VAL = BIG[1][:, 0:TILES * V].rearrange("p (t e) -> p t e", t=TILES)
            REP = BIG[1][:, 1024:1024 + TILES * V].rearrange("p (t e) -> p t e", t=TILES)
            RED = BIG[1][:, 2048:2048 + TILES]
            MASKB = BIG[1][:, 2304:2304 + n // 2].bitcast(BF16).rearrange("p (t e) -> p t e", t=TILES)
            WM = BIG[2][0:16, 0:TOK]
            WR = BIG[2][0:16, TOK:2 * TOK]
            KEPT = BIG[2][0:16, 2 * TOK:3 * TOK]
            W8 = BIG[2][0:16, 3 * TOK:3 * TOK + 8]
            TAKEN, LEAST = -3.2e38, NEVER
            wide = lambda a: a.unsqueeze(2).broadcast_to([P, TILES, E])
            logits = PS[:, 0, 0:n].rearrange("p (t e) -> p t e", t=TILES)
            before = PS[:, 1, 0:n].rearrange("p (t e) -> p t e", t=TILES)
            rounds = capacity // 8
            with phase("logits", "scored", "vec", "masked", "counted", "ranked", "turned", "kept", "back") as (block, s):
                @block.tensor
                def _(pe):
                    for t in range(TILES):
                        pe.matmul(logits[:, t, :], srcT[:, t * P:(t + 1) * P], wg, start=True, stop=True)\
                          .then_inc(s["logits"], 1)
                    pe.wait_ge(s["masked"], 1)
                    if kind != "logit":
                        for t in range(TILES):
                            for b in range(t + 1):
                                mm = pe.matmul(before[:, t, :], (upperb if b == t else onesb)[:, :], MASKB[:, b, :],
                                               start=b == 0, stop=b == t)
                        mm.then_inc(s["counted"], 1)
                    else:
                        for t in range(TILES):
                            mm = pe.transpose(PS[0:16, 2 + t // 4, (t % 4) * P:(t % 4 + 1) * P], PROB[:, t, :], ident)
                        mm.then_inc(s["turned"], 1)
                        pe.wait_ge(s["kept"], 1)
                        for t in range(TILES):
                            mm = pe.transpose(before[:, t, :], KEPT[:, t * P:(t + 1) * P], ident[0:16, 0:16])
                        mm.then_inc(s["back"], 1)

                @block.scalar
                def _(act):
                    if kind == "sigmoid":
                        act.wait_ge(s["logits"], TILES)
                        act.activation(SCORE, logits, ACT.Sigmoid).then_inc(s["scored"], 1)
                    else:
                        act.wait_ge(s["vec"], 3)
                        act.activation(SCORE, SCORE, ACT.Exp).then_inc(s["scored"], 1)

                @block.vector
                def _(dve):
                    c = Chain(dve, s["vec"])
                    if kind != "sigmoid":
                        dve.wait_ge(s["logits"], TILES)
                        c.mark(dve.tensor_copy(LG, logits))
                        c.step(dve.tensor_reduce(RED, logits, AX.X, ALU.max))
                        c.step(dve.tensor_tensor(SCORE, LG, wide(RED), ALU.subtract))
                    dve.wait_ge(s["scored"], 1)
                    if kind != "sigmoid":
                        c.step(dve.tensor_reduce(RED, SCORE, AX.X, ALU.add))
                        c.step(dve.reciprocal(RED, RED))
                        c.step(dve.tensor_tensor(SCORE, SCORE, wide(RED), ALU.mult))
                    c.mark(dve.memset(VAL[:, :, E:V], NEVER))
                    if kind == "softmax":
                        c.step(dve.tensor_copy(VAL[:, :, 0:E], SCORE))
                    else:
                        b = row("L0f_bias" if kind == "sigmoid" else "L2f_b")
                        c.step(dve.tensor_tensor(VAL[:, :, 0:E], SCORE,
                                                 b.unsqueeze(1).broadcast_to([P, TILES, E]), ALU.add))
                    for t in range(TILES):
                        c.mark(dve.max(TOP[:, t, :], VAL[:, t, :]))
                    c.join()
                    c.step(dve.memset(TOP[:, :, K:8], NEVER))
                    for t in range(TILES):
                        c.mark(dve.match_replace(REP[:, t, :], TOP[:, t, :], VAL[:, t, :], -2.0e38))
                    c.join()
                    c.step(dve.tensor_tensor(MASK, REP[:, :, 0:E], VAL[:, :, 0:E], ALU.not_equal))
                    if kind == "logit":
                        c.step(dve.tensor_tensor(PROB, LG, MASK, ALU.mult))
                        c.step(dve.tensor_scalar(SCORE, MASK, -NEVER, NEVER, ALU.mult, ALU.add))
                        c.mark(dve.tensor_tensor(PROB, PROB, SCORE, ALU.add))
                        c.join()
                        dve.sem_inc(s["masked"], 1)
                        dve.wait_ge(s["turned"], 1)
                        c.mark(dve.tensor_copy(WM, PS[0:16, 2:4, :].rearrange("p a b -> p (a b)")))
                        c.step(dve.tensor_copy(WR, PS[0:16, 2:4, :].rearrange("p a b -> p (a b)")))
                        for r in range(rounds):
                            c.step(dve.max(W8, WR))
                            c.step(dve.match_replace(WR, W8, WR, TAKEN))
                        c.mark(dve.tensor_tensor(KEPT, WR, WM, ALU.not_equal))
                        c.join()
                        dve.sem_inc(s["kept"], 1)
                        dve.wait_ge(s["back"], 1)
                        c.step(dve.tensor_tensor(MASK, MASK, before, ALU.mult))
                        c.mark(dve.tensor_tensor(GATE[:, :, 0:E], LG, MASK, ALU.mult))
                        c.mark(dve.memset(GATE[:, :, E:E + 2], 0.5))
                        c.join()
                        return
                    dve.tensor_copy(MASKB, MASK).then_inc(s["masked"], 1)
                    if kind == "sigmoid":
                        c.step(dve.tensor_tensor(PROB, SCORE, MASK, ALU.mult))
                        c.step(dve.tensor_reduce(RED, PROB, AX.X, ALU.add))
                        c.step(dve.tensor_scalar(RED, RED, 1e-20, None, ALU.add))
                        c.step(dve.reciprocal(RED, RED))
                        c.step(dve.tensor_tensor(PROB, PROB, wide(RED), ALU.mult))
                    else:
                        c.step(dve.tensor_tensor(PROB, SCORE, MASK, ALU.mult))
                    dve.wait_ge(s["counted"], 1)
                    c.step(dve.scalar_tensor_tensor(out=GATE[:, :, 0:E], in0=before, scalar=float(capacity), in1=PROB,
                                                    op0=ALU.is_lt, op1=ALU.mult))

        def experts(srcT, names, units, chunks, func, bias, dst):
            n = chunks * P
            W1 = [BIG[0][:, u * 512:u * 512 + n] for u in range(2)]
            W3 = [BIG[0][:, 1024 + u * 512:1024 + u * 512 + n] for u in range(2)]
            W2 = [BIG[0][:, 2048 + u * 512:2048 + u * 512 + n] for u in range(2)]
            HID = [[BIG[2 + u][:, c * TOK:(c + 1) * TOK] for c in range(chunks)] for u in range(2)]
            gated = len(names) == 3
            bufs = {names[0]: W1, names[-1]: W2}
            if gated:
                bufs[names[1]] = W3
            with phase("loaded_even", "loaded_odd", "wfree", "made", "hfree", "acted", "ready", "ymade", "added", "vec") as (block, s):
                loaded = (s["loaded_even"], s["loaded_odd"])

                @block.sync
                def _(sp):
                    with sp.Fori(0, units // 2) as i:
                        for u in range(2):
                            e = i * 2 + u
                            sp.wait_ge(s["wfree"], e + 1)
                            for name, buf in bufs.items():
                                sp.dma_start(buf[u], d[name][:, bass.ts(e, n)]).then_inc(loaded[u], 16)

                @block.tensor
                def _(pe):
                    pe.sem_inc(s["wfree"], 2)
                    with pe.Fori(0, units // 2) as i:
                        for u in range(2):
                            e = i * 2 + u
                            pe.wait_ge(loaded[u], (i + 1) * (16 * len(names)))
                            for c in range(chunks):
                                pe.wait_ge(s["hfree"], e * chunks + c + 1)
                                for k, W in enumerate((W1, W3) if gated else (W1,)):
                                    b = 2 * k if gated else 2 * (c % 2)
                                    for h in range(2):
                                        mm = pe.matmul(PS[:, b + h, :], W[u][:, c * P:(c + 1) * P],
                                                       srcT[:, h * HALF:(h + 1) * HALF], start=True, stop=True)
                                mm.then_inc(s["made"], 1)
                            pe.wait_ge(s["ready"], (e + 1) * chunks)
                            for h in range(2):
                                pe.wait_ge(s["added"], e * 2 + h + 1)
                                for t in range(4 * h, 4 * h + 4):
                                    for c in range(chunks):
                                        mm = pe.matmul(PS[:, 4 + h, (t % 4) * P:(t % 4 + 1) * P],
                                                       HID[u][c][:, t * P:(t + 1) * P], W2[u][:, c * P:(c + 1) * P],
                                                       start=c == 0, stop=c == chunks - 1)
                                mm.then_inc(s["ymade"], 1)
                            pe.wait_ge(s["ymade"], (e + 1) * 2)
                            pe.sem_inc(s["wfree"], 1)

                @block.scalar
                def _(act):
                    if not gated:
                        act.sem_inc(s["hfree"], 2)
                    with act.Fori(0, units // 2) as i:
                        for u in range(2):
                            e = i * 2 + u
                            act.wait_ge(s["wfree"], e + 1)
                            for c in range(chunks):
                                act.wait_ge(s["made"], e * chunks + c + 1)
                                b = 0 if gated else 2 * (c % 2)
                                o = HID[u][c].rearrange("p (a b) -> p a b", a=2)
                                if bias is None:
                                    ins = act.activation(o, PS[:, b:b + 2, :], func)
                                else:
                                    ins = act.activation(o, PS[:, b:b + 2, :], func,
                                                         bias=bias[:, bass.ds(e * chunks + c, 1)])
                                ins.then_inc(s["acted"] if gated else s["ready"], 1)
                                if not gated:
                                    act.wait_ge(s["ready"], e * chunks + c + 1)
                                    act.sem_inc(s["hfree"], 1)

                @block.vector
                def _(dve):
                    dve.sem_inc(s["added"], 2)
                    if gated:
                        dve.sem_inc(s["hfree"], 1)
                    with dve.Fori(0, units // 2) as i:
                        v = Chain(dve, s["vec"], i * 16)
                        for u in range(2):
                            e = i * 2 + u
                            if gated:
                                for c in range(chunks):
                                    dve.wait_ge(s["acted"], e * chunks + c + 1)
                                    o = HID[u][c].rearrange("p (a b) -> p a b", a=2)
                                    dve.tensor_tensor(o, o, PS[:, 2:4, :], ALU.mult).then_inc(s["ready"], 1)
                                    dve.wait_ge(s["ready"], e * chunks + c + 1)
                                    dve.sem_inc(s["hfree"], 1)
                            for h in range(2):
                                dve.wait_ge(s["ymade"], e * 2 + h + 1)
                                for t in range(4 * h, 4 * h + 4):
                                    v.mark(dve.scalar_tensor_tensor(
                                        out=dst[:, t, :], in0=PS[:, 4 + h, (t % 4) * P:(t % 4 + 1) * P],
                                        scalar=GATE[:, t, bass.ds(e, 1)], in1=dst[:, t, :],
                                        op0=ALU.mult, op1=ALU.add))
                                v.join()
                                dve.sem_inc(s["added"], 1)
                        assert v.n == 16

        def l1_ffn():
            normalize(X, XR, HT, 1e-5)
            normalize(XR, XN, HT, 1e-5, w("c_ln1_g"), w("c_ln1_b"))
            token_qk(w("L1f_q"), w("L1f_k"), False, HD ** -0.5)
            project([], (HT, w("L1f_v"), None))
            attend(w("L1f_o"), XR, "causal")
            normalize(XR, XN, HT, 1e-5, w("c_ln2_g"), w("c_ln2_b"))
            route(HT, w("L1f_gate"), 8, 2, "softmax", 256)
            B2 = BIG[1][0:8, 0:P]
            GT = BIG[1][0:8, P:P + TOK]
            with phase("loaded", "turned", "copied", "made", "vec") as (block, s):
                @block.sync
                def _(sp):
                    sp.dma_start(B2, d["L1f_b2"]).then_inc(s["loaded"], 16)

                @block.tensor
                def _(pe):
                    for t in range(TILES):
                        mm = pe.transpose(PS[0:8, t // 4, (t % 4) * P:(t % 4 + 1) * P], GATE[:, t, 0:8], ident)
                    mm.then_inc(s["turned"], 1)
                    pe.wait_ge(s["loaded"], 16)
                    pe.wait_ge(s["copied"], 1)
                    for t in range(TILES):
                        mm = pe.matmul(PS[:, 2 + t // 4, (t % 4) * P:(t % 4 + 1) * P], GT[:, t * P:(t + 1) * P], B2,
                                       start=True, stop=True)
                    mm.then_inc(s["made"], 1)

                @block.scalar
                def _(act):
                    act.wait_ge(s["turned"], 1)
                    act.activation(GT.rearrange("p (a b) -> p a b", a=2), PS[0:8, 0:2, :], ACT.Copy).then_inc(s["copied"], 1)

                @block.vector
                def _(dve):
                    c = Chain(dve, s["vec"])
                    both = lambda a: a[:, :, :].rearrange("p (a t) f -> p a (t f)", a=2)
                    c.step(dve.tensor_tensor(both(X), both(X), both(XR), ALU.add))
                    dve.wait_ge(s["made"], 1)
                    c.step(dve.tensor_tensor(both(X), both(X), PS[:, 2:4, :], ALU.add))
            experts(HT, ("L1f_w1", "L1f_w2"), 8, 4, ACT.Gelu, w("c_L1f_b1"), X)

        def l2_ffn():
            normalize(X, XN, HT, 1e-5)
            route(HT, w("L2f_gate"), 16, 2, "logit", 160)
            experts(HT, ("L2f_w1", "L2f_w3", "L2f_w2"), 18, 2, ACT.Silu, None, X)

        def l2_attn():
            normalize(X, XN, HT, 1e-5)
            project([(QT, w("L2a_w"), HT, w("c_L2a_b"), 1.0)])
            WW = BIG[0][:, 0:TOK]
            SM = BIG[0][:, TOK:TOK + TILES]
            ww = WW.rearrange("p (t k) -> p t k", t=TILES)
            two = lambda a: a.rearrange("p (a b) -> p a b", a=2)
            quad = lambda a: a.unsqueeze(1).broadcast_to([P, 4, P])
            with phase("scored", "vec", "exped", "weighed", "mixed") as (block, s):
                @block.tensor
                def _(pe):
                    for t in range(TILES):
                        cols = slice(t * P, (t + 1) * P)
                        mm = pe.matmul(PS[:, t // 4, (t % 4) * P:(t % 4 + 1) * P], HT[:, cols], QT[:, cols],
                                       start=True, stop=True)
                    mm.then_inc(s["scored"], 1)
                    pe.wait_ge(s["weighed"], 1)
                    for t in range(TILES):
                        pe.matmul(PS[:, 2 + t // 4, (t % 4) * P:(t % 4 + 1) * P], ww[:, t, :], XN[:, t, :],
                                  start=True, stop=True)
                        mm = pe.matmul(PS[:, 4, t:t + 1], ww[:, t, :], cst("ones")[:, 0:1], start=True, stop=True)
                    mm.then_inc(s["mixed"], 1)

                @block.scalar
                def _(act):
                    act.wait_ge(s["vec"], 2)
                    act.activation(WW, WW, ACT.Tanh).then_inc(s["exped"], 1)
                    act.wait_ge(s["exped"], 1)
                    act.activation(WW, WW, ACT.Exp).then_inc(s["exped"], 1)

                @block.vector
                def _(dve):
                    c = Chain(dve, s["vec"])
                    dve.wait_ge(s["scored"], 1)
                    for h in range(2):
                        c.mark(dve.tensor_tensor(ww[:, 4 * h:4 * h + 4, :], PS[:, h, :].rearrange("p (t k) -> p t k", t=4),
                                                 quad(cst("lw")), ALU.mult))
                    dve.wait_ge(s["exped"], 2)
                    dve.tensor_tensor(ww, ww, cst("off").unsqueeze(1).broadcast_to([P, TILES, P]), ALU.mult)\
                        .then_inc(s["weighed"], 1)
                    dve.wait_ge(s["mixed"], 1)
                    c.step(dve.tensor_scalar(SM, PS[:, 4, 0:TILES], 1e-7, None, ALU.add))
                    c.step(dve.reciprocal(SM, SM))
                    for t in range(TILES):
                        c.mark(dve.scalar_tensor_tensor(out=X[:, t, :], in0=PS[:, 2 + t // 4, (t % 4) * P:(t % 4 + 1) * P],
                                                        scalar=SM[:, t:t + 1], in1=X[:, t, :], op0=ALU.mult, op1=ALU.add))
                    c.join()

        def l0_ffn():
            normalize(X, XN, HT, 1e-5)
            route(HT, w("L0f_router"), 64, 6, "sigmoid", 48)
            G2 = BIG[1][:, 0:TOK]
            GA = BIG[0][:, 3072:3584].bitcast(BF16)
            GB = BIG[0][:, 3584:4096].bitcast(BF16)
            GF = BIG[1][:, TOK:2 * TOK]
            R1 = BIG[1][:, 2 * TOK:3 * TOK]
            T3 = BIG[1][:, 3 * TOK:3 * TOK + 512].bitcast(BF16)
            T1 = BIG[1][:, 3 * TOK + 512:4 * TOK].bitcast(BF16)
            with phase("vec", "turned", "pool") as (block, s):
                @block.tensor
                def _(pe):
                    pe.wait_ge(s["vec"], 2)
                    for t in range(TILES):
                        mm = pe.transpose(PS[:, t // 4, (t % 4) * P:(t % 4 + 1) * P], G2[:, t * P:(t + 1) * P], ident)
                    mm.then_inc(s["turned"], 1)

                @block.vector
                def _(dve):
                    c = Chain(dve, s["vec"])
                    g2 = G2.rearrange("p (t c e) -> p t c e", t=TILES, c=2)
                    for k in range(2):
                        c.mark(dve.tensor_copy(g2[:, :, k, :], GATE[:, :, :]))
                    dve.wait_ge(s["turned"], 1)
                    c.step(dve.tensor_copy(GF, PS[:, 0:2, :].rearrange("p a b -> p (a b)")))
                    c.step(dve.tensor_copy(T1, GF))
                    c.step(dve.tensor_tensor(R1, GF, T1, ALU.subtract))
                    c.step(dve.tensor_copy(T3, R1))
                    c.step(dve.tensor_tensor(R1, R1, T3, ALU.subtract))
                    c.mark(dve.memset(GB[:, :], 0.0))
                    c.mark(dve.tensor_copy(GA[0:64, :], T1[0:64, :]))
                    c.mark(dve.tensor_copy(GA[64:128, :], T3[64:128, :]))
                    c.join()
                    c.step(dve.tensor_copy(GB[0:64, :], R1[0:64, :]))

            n = 4 * P
            W1 = [BIG[0][:, u * 512:u * 512 + n] for u in range(2)]
            W2 = [BIG[0][:, 1024 + u * 512:1024 + u * 512 + n] for u in range(2)]
            HID = [BIG[2][:, c * TOK:(c + 1) * TOK] for c in range(2)]
            SH = [BIG[3][:, c * TOK:(c + 1) * TOK] for c in range(2)]
            YT = BIG[1][:, 0:TOK]
            halves = lambda a: a.rearrange("p (a b) -> p a b", a=2)
            with phase("loaded_even", "loaded_odd", "wfree", "made", "hfree", "acted", "picked", "ready", "ymade", "shared",
                       "copied", "turned", "added") as (block, s):
                loaded = (s["loaded_even"], s["loaded_odd"])

                @block.sync
                def _(sp):
                    with sp.Fori(0, 4) as i:
                        for u in range(2):
                            e = i * 2 + u
                            sp.wait_ge(s["wfree"], e + 1)
                            for name, buf in (("L0f_w1", W1), ("L0f_w2", W2)):
                                sp.dma_start(buf[u], d[name][:, bass.ts(e, n)]).then_inc(loaded[u], 16)

                @block.tensor
                def _(pe):
                    pe.sem_inc(s["wfree"], 2)
                    for c in range(2):
                        for h in range(2):
                            mm = pe.matmul(PS[:, 2 * c + h, :], w("L0f_sw1")[:, c * P:(c + 1) * P],
                                           HT[:, h * HALF:(h + 1) * HALF], start=True, stop=True)
                        mm.then_inc(s["made"], 1)
                    pe.wait_ge(s["shared"], 2)
                    for c in range(2):
                        for h in range(2):
                            pe.matmul(PS[:, 6 + h, :], w("L0f_sw2")[:, c * P:(c + 1) * P], SH[c][:, h * HALF:(h + 1) * HALF],
                                      start=c == 0, stop=False, skip_group_check=True)
                    with pe.Fori(0, 4) as i:
                        for u in range(2):
                            e = i * 2 + u
                            pe.wait_ge(loaded[u], (i + 1) * 32)
                            for c in range(4):
                                pair = e * 4 + c
                                pe.wait_ge(s["hfree"], pair + 1)
                                for h in range(2):
                                    mm = pe.matmul(PS[:, 2 * (c % 2) + h, :], W1[u][:, c * P:(c + 1) * P],
                                                   HT[:, h * HALF:(h + 1) * HALF], start=True, stop=True)
                                mm.then_inc(s["made"], 1)
                                pe.wait_ge(s["ready"], pair + 1)
                                if c > 0:
                                    for h in range(2):
                                        pe.matmul(PS[:, 6 + h, :], W2[u][:, (c - 1) * P:c * P],
                                                  HID[(c - 1) % 2][:, h * HALF:(h + 1) * HALF],
                                                  start=False, stop=False, skip_group_check=True).then_inc(s["ymade"], 1)
                                for h in range(2):
                                    for k, G in enumerate((GA, GB)):
                                        mm = pe.matmul(PS[:, 4 + h, :], pickb[:, bass.ts(pair, P)],
                                                       G[:, h * HALF:(h + 1) * HALF], start=k == 0, stop=k == 1)
                                mm.then_inc(s["picked"], 1)
                            pe.wait_ge(s["ready"], e * 4 + 5)
                            for h in range(2):
                                pe.matmul(PS[:, 6 + h, :], W2[u][:, 3 * P:4 * P], HID[1][:, h * HALF:(h + 1) * HALF],
                                          start=False, stop=False, skip_group_check=True).then_inc(s["ymade"], 1)
                            pe.wait_ge(s["ymade"], (e + 1) * 8)
                            pe.sem_inc(s["wfree"], 1)
                    for t in range(TILES):
                        if t == 0:
                            pe.wait_ge(s["copied"], 1)
                        mm = pe.transpose(PS[:, t // 4, (t % 4) * P:(t % 4 + 1) * P], YT[:, t * P:(t + 1) * P], ident)
                    mm.then_inc(s["turned"], 1)

                @block.scalar
                def _(act):
                    for c in range(2):
                        act.wait_ge(s["made"], c + 1)
                        act.activation(halves(SH[c]), PS[:, 2 * c:2 * c + 2, :], ACT.Gelu_apprx_tanh).then_inc(s["shared"], 1)
                        act.wait_ge(s["shared"], c + 1)
                        act.sem_inc(s["hfree"], 1)
                    with act.Fori(0, 16) as i:
                        for c in range(2):
                            pair = i * 2 + c
                            act.wait_ge(s["made"], pair + 3)
                            act.wait_ge(s["picked"], pair + 1)
                            act.activation(halves(HID[c]), PS[:, 2 * c:2 * c + 2, :], ACT.Gelu_apprx_tanh)\
                               .then_inc(s["acted"], 1)
                            act.wait_ge(s["acted"], pair + 1)
                            act.sem_inc(s["hfree"], 1)

                @block.vector
                def _(dve):
                    dve.sem_inc(s["ready"], 1)
                    with dve.Fori(0, 16) as i:
                        for c in range(2):
                            pair = i * 2 + c
                            dve.wait_ge(s["acted"], pair + 1)
                            dve.wait_ge(s["picked"], pair + 1)
                            dve.tensor_tensor(halves(HID[c]), halves(HID[c]), PS[:, 4:6, :], ALU.mult)\
                                .then_inc(s["ready"], 1)
                    dve.wait_ge(s["ymade"], 64)
                    dve.tensor_copy(halves(YT), PS[:, 6:8, :]).then_inc(s["copied"], 1)
                    dve.wait_ge(s["turned"], 1)
                    x = X[:, :, :].rearrange("p (a t) f -> p a (t f)", a=2)
                    dve.tensor_tensor(x, x, PS[:, 0:2, :], ALU.add).then_inc(s["added"], 1)
                    dve.wait_ge(s["added"], 1)

        def l1_xattn():
            normalize(X, XN, HT, 1e-5)
            with phase("zeroed") as (block, s):
                @block.gpsimd
                def _(pool):
                    pool.memset(XR[:, :, :], 0.0).then_inc(s["zeroed"], 1)
            project([(QT, w("L1xs_q"), HT, w("c_L1xs_bq"), HD ** -0.5), (KT, w("L1xs_k"), CT, w("c_L1xs_bk"), 1.0)],
                    (CT, w("L1xs_v"), row("L1xs_v")))
            attend(w("L1xs_o"), XR, "src", row("L1xs_o"))
            project([(QT, w("L1xt_q"), HT, w("c_L1xt_bq"), HD ** -0.5), (KT, w("L1xt_k"), HT, w("c_L1xt_bk"), 1.0)],
                    (HT, w("L1xt_v"), row("L1xt_v")))
            attend(w("L1xt_o"), XR, "tgt", row("L1xt_o"))
            turn(XR, QT)
            N = 4 * BATCH
            GX = BIG[0]
            gx = GX[:, :].rearrange("p (s g b) -> p g b s", s=SEQ, g=4)
            HS = BIG[1][:, 0:(SEQ + 1) * BATCH]
            G = [BIG[1][:, 1280 + i * 128:1280 + i * 128 + 5 * BATCH] for i in range(2)]
            T = BIG[1][:, 1600:1600 + 2 * BATCH]
            TC = BIG[1][:, 1664:1664 + BATCH]
            WH = BIG[1][:, 2048:2560]
            with phase("made", "evac", "zeroed") as (block, s):
                @block.tensor
                def _(pe):
                    for g in range(4):
                        for h in range(2):
                            cols = slice(h * HALF, (h + 1) * HALF)
                            o = PS[:, 2 * g + h, :]
                            pe.matmul(o, w("L1x_wx")[:, g * P:(g + 1) * P], HT[:, cols], start=True, stop=False)
                            pe.matmul(o, w("L1x_wc")[:, g * P:(g + 1) * P], QT[:, cols], start=False, stop=True)\
                              .then_inc(s["made"], 1)

                @block.gpsimd
                def _(pool):
                    pool.memset(HS[:, 0:BATCH], 0.0).then_inc(s["zeroed"], 1)
                    pool.memset(G[0][:, 64:80], 0.0).then_inc(s["zeroed"], 1)
                    pool.tensor_scalar(WH[:, 0:3 * P], w("L1x_wh")[:, 0:3 * P], 0.5, None, ALU.mult).then_inc(s["zeroed"], 1)
                    pool.tensor_copy(WH[:, 3 * P:4 * P], w("L1x_wh")[:, 3 * P:4 * P]).then_inc(s["zeroed"], 1)

                @block.vector
                def _(dve):
                    for g in range(4):
                        for h in range(2):
                            dve.wait_ge(s["made"], 2 * g + h + 1)
                            dve.tensor_scalar(gx[:, g, h * 8:h * 8 + 8, :],
                                              PS[:, 2 * g + h, :].rearrange("p (b s) -> p b s", b=8),
                                              w("c_L1x_lstm_b")[:, g:g + 1], 2.0 if g == 3 else 1.0, ALU.add, ALU.mult)\
                                .then_inc(s["evac"], 1)
                    dve.wait_ge(s["evac"], 8)

            with phase("gates", "gfree", "acted", "cell", "tanhed", "hidden") as (block, s):
                @block.tensor
                def _(pe):
                    with pe.Fori(0, SEQ // 2) as i:
                        for u in range(2):
                            step = i * 2 + u
                            o = PS[:, u, 0:N]
                            pe.wait_ge(s["gfree"], step + 1)
                            pe.matmul(o, ident, GX[:, bass.ts(step, N)], start=True, stop=False, skip_group_check=True)
                            pe.wait_ge(s["hidden"], step + 1)
                            for g in range(4):
                                mm = pe.matmul(o[:, g * BATCH:(g + 1) * BATCH], WH[:, g * P:(g + 1) * P],
                                               HS[:, bass.ts(step, BATCH)], start=False, stop=g == 3,
                                               skip_group_check=True)
                            mm.then_inc(s["gates"], 1)

                @block.scalar
                def _(act):
                    act.sem_inc(s["gfree"], 2)
                    with act.Fori(0, SEQ // 2) as i:
                        for u in range(2):
                            step = i * 2 + u
                            act.wait_ge(s["gates"], step + 1)
                            act.activation(G[u][:, 0:64], PS[:, u, 0:64], ACT.Tanh, scale=0.5).then_inc(s["acted"], 1)
                            act.wait_ge(s["acted"], step + 1)
                            act.sem_inc(s["gfree"], 1)
                            act.wait_ge(s["cell"], step * 2 + 2)
                            act.activation(TC, G[1 - u][:, 64:80], ACT.Tanh, scale=0.5).then_inc(s["tanhed"], 1)

                @block.vector
                def _(dve):
                    dve.sem_inc(s["hidden"], 1)
                    with dve.Fori(0, SEQ // 2) as i:
                        for u in range(2):
                            step = i * 2 + u
                            dve.wait_ge(s["acted"], step + 1)
                            dve.scalar_tensor_tensor(out=T, in0=G[u][:, 0:32], scalar=1.0, in1=G[u][:, 48:80],
                                                     op0=ALU.add, op1=ALU.mult).then_inc(s["cell"], 1)
                            dve.wait_ge(s["cell"], step * 2 + 1)
                            dve.scalar_tensor_tensor(out=G[1 - u][:, 64:80], in0=T[:, BATCH:2 * BATCH], scalar=0.5,
                                                     in1=T[:, 0:BATCH], op0=ALU.mult, op1=ALU.add)\
                                .then_inc(s["cell"], 1)
                            dve.wait_ge(s["tanhed"], step + 1)
                            dve.scalar_tensor_tensor(out=HS[:, bass.ts(step + 1, BATCH)], in0=G[u][:, 32:48],
                                                     scalar=1.0, in1=TC, op0=ALU.add, op1=ALU.mult)\
                                .then_inc(s["hidden"], 1)

            RR = [BIG[2][:, c * TOK:(c + 1) * TOK] for c in range(4)]
            with phase("made", "evac", "ymade", "based", "added") as (block, s):
                @block.tensor
                def _(pe):
                    for c in range(4):
                        if c >= 2:
                            pe.wait_ge(s["evac"], 2 * (c - 1))
                        for h in range(2):
                            pe.matmul(PS[:, 2 * (c % 2) + h, :], w("L1x_w1")[:, c * P:(c + 1) * P],
                                      HS[:, BATCH + h * HALF:BATCH + (h + 1) * HALF], start=True, stop=True)\
                              .then_inc(s["made"], 1)
                    pe.wait_ge(s["evac"], 8)
                    for t in range(TILES):
                        for c in range(4):
                            mm = pe.matmul(PS[:, 4 + t // 4, (t % 4) * P:(t % 4 + 1) * P], RR[c][:, t * P:(t + 1) * P],
                                           w("L1x_w2")[:, c * P:(c + 1) * P], start=c == 0, stop=c == 3)
                        mm.then_inc(s["ymade"], 1)

                @block.scalar
                def _(act):
                    for c in range(4):
                        for h in range(2):
                            act.wait_ge(s["made"], 2 * c + h + 1)
                            o = RR[c].rearrange("p (b s) -> p s b", b=BATCH)[:, h * 32:(h + 1) * 32, :]
                            act.activation(o, PS[:, 2 * (c % 2) + h, :].rearrange("p (s b) -> p s b", b=BATCH), ACT.Relu,
                                           scale=0.5, bias=w("c_L1x_b1")[:, c:c + 1]).then_inc(s["evac"], 1)

                @block.gpsimd
                def _(pool):
                    pool.tensor_tensor(X[:, :, :], X[:, :, :],
                                       row("L1x_b2").unsqueeze(1).broadcast_to([P, TILES, P]), ALU.add)\
                        .then_inc(s["based"], 1)

                @block.vector
                def _(dve):
                    dve.wait_ge(s["based"], 1)
                    for h in range(2):
                        dve.wait_ge(s["ymade"], 4 * h + 4)
                        x = X[:, 4 * h:4 * h + 4, :].rearrange("p t f -> p (t f)")
                        dve.tensor_tensor(x, x, PS[:, 4 + h, :], ALU.add).then_inc(s["added"], 1)
                    dve.wait_ge(s["added"], 2)


        EXTRA = sb("EXTRA", [P, 6 * TOK])
        tiles = lambda a: a.rearrange("p (t f) -> p t f", t=TILES)
        halves = lambda a: a.rearrange("p (a b) -> p a b", a=2)
        half = lambda a, g: a[:, g * HALF:(g + 1) * HALF]
        square = lambda g, t: PS[:, g, (t % 4) * P:(t % 4 + 1) * P]
        each = lambda a: a.unsqueeze(1).broadcast_to([P, TILES, P])

        def delta_heads():
            H, LV = 8, 5
            W4 = BIG[3]
            part = lambda buf, i: buf[:, i * TOK:(i + 1) * TOK]
            SIL = BIG[0][:, :].rearrange("p (t n f) -> p t n f", t=TILES, n=4)
            QH, KH, KBH, GAM = (part(BIG[1], i) for i in range(4))
            LT, AT, XX, XXT = (part(BIG[2], i) for i in range(4))
            WO, YY, CC, KB, GU, GW = (part(EXTRA, i) for i in range(6))
            OO = XN[:, :, :]
            small = CS[:, C_AT["pick"][0]:C_AT["pick"][0] + 4096]
            steps = lambda a: a.rearrange("p (t h) -> p t h", t=TILES)
            LG = small[:, 0:128].rearrange("p (t n) -> p t n", t=TILES)
            BETA, G, Z, E1, NA, U, SP, T1 = (steps(small[:, 128 + 64 * i:192 + 64 * i]) for i in range(8))
            RS = small[:, 700:716].rearrange("p (t n) -> p t n", t=TILES)
            RO = small[:, 720:728]
            EA = small[:, 730:738]
            SQ2 = small[:, 1024:3072].rearrange("p (t n f) -> p t n f", t=TILES, n=2)
            with phase("loaded", "made", "vec", "acted") as (block, s):
                @block.sync
                def _(sp):
                    sp.dma_start(W4[:, :], d["L3a_w"]).then_inc(s["loaded"], 16)
                    sp.dma_start(WO, d["L3a_wo"]).then_inc(s["loaded"], 16)
                    sp.wait_ge(s["loaded"], 32)

                @block.tensor
                def _(pe):
                    for t in range(TILES):
                        a = W_AT["L3a_b"][0]
                        mm = pe.matmul(PS[:, 0, t * 16:(t + 1) * 16], HT[:, t * P:(t + 1) * P], WT[:, a:a + 16],
                                       start=True, stop=True)
                    mm.then_inc(s["made"], 1)

                @block.scalar
                def _(act):
                    act.wait_ge(s["made"], 1)
                    act.activation(LG, PS[:, 0, 0:128].rearrange("p (t n) -> p t n", t=TILES), ACT.Copy).then_inc(s["acted"], 1)
                    act.wait_ge(s["acted"], 1)
                    act.activation(BETA, LG[:, :, 0:8], ACT.Sigmoid).then_inc(s["acted"], 1)
                    act.activation(EA, row("L3a_Alog"), ACT.Exp).then_inc(s["acted"], 1)
                    act.wait_ge(s["vec"], 2)
                    act.activation(E1, NA, ACT.Exp).then_inc(s["acted"], 1)
                    act.wait_ge(s["vec"], 3)
                    act.activation(SP, U, ACT.Ln).then_inc(s["acted"], 1)

                @block.vector
                def _(dve):
                    c = Chain(dve, s["vec"])
                    wide = lambda a: a.unsqueeze(1).broadcast_to([P, TILES, 8])
                    dve.wait_ge(s["acted"], 1)
                    c.step(dve.tensor_tensor(Z, LG[:, :, 8:16], wide(row("L3a_dt")), ALU.add))
                    c.step(dve.scalar_tensor_tensor(out=NA, in0=Z, scalar=-1.0, in1=Z, op0=ALU.mult, op1=ALU.min))
                    dve.wait_ge(s["acted"], 4)
                    c.step(dve.tensor_scalar(U, E1, 1.0, None, ALU.add))
                    dve.wait_ge(s["acted"], 5)
                    c.step(dve.tensor_scalar(T1, E1, -0.25, 1.0 / 3.0, ALU.mult, ALU.add))
                    c.step(dve.tensor_tensor(T1, T1, E1, ALU.mult))
                    c.step(dve.tensor_scalar(T1, T1, -0.5, None, ALU.add))
                    c.step(dve.tensor_tensor(T1, T1, E1, ALU.mult))
                    c.step(dve.scalar_tensor_tensor(out=T1, in0=T1, scalar=1.0, in1=E1, op0=ALU.add, op1=ALU.mult))
                    c.step(dve.tensor_scalar(U, E1, 0.01, None, ALU.is_lt))
                    c.step(dve.tensor_tensor(T1, T1, U, ALU.mult))
                    c.step(dve.tensor_scalar(U, U, -1.0, 1.0, ALU.mult, ALU.add))
                    c.step(dve.tensor_tensor(SP, SP, U, ALU.mult))
                    c.step(dve.tensor_tensor(SP, SP, T1, ALU.add))
                    c.step(dve.scalar_tensor_tensor(out=SP, in0=Z, scalar=0.0, in1=SP, op0=ALU.max, op1=ALU.add))
                    c.step(dve.scalar_tensor_tensor(out=G, in0=SP, scalar=-1.0, in1=wide(EA), op0=ALU.mult, op1=ALU.mult))

            per = dict(projected=8, silued=8, squared=1, rooted=2, scaled=1, beta_k=1, spread=1, pairs=1, decayed=1,
                       turned=3, tcopied=3, inner=2, lower=1, level0=1, other=1, xcopied=1, attn=1, masked=LV,
                       ymade=8, ycopied=8, corrected=8, subbed=8, zmade=2, zcopied=2, wmade=2, wcopied=2, vmade=2,
                       delta=2, mixed=2, gated=1, summed=1, onormed=2, oturned=2, ocopied=2, out=2, added=2, vec=33)
            with phase(*per) as (block, s):
                def waits(eng, h):
                    return lambda name, n: eng.wait_ge(s[name], h * per[name] + n)

                @block.tensor
                def _(pe):
                    with pe.Fori(0, H) as h:
                        at = waits(pe, h)
                        for t in range(TILES):
                            at("silued", t + 1)
                            pe.matmul(PS[:, t % 4, :], HT[:, t * P:(t + 1) * P], W4[:, bass.ts(h, HALF)],
                                      start=True, stop=True).then_inc(s["projected"], 1)
                        at("spread", 1)
                        for g in range(2):
                            mm = pe.matmul(PS[:, 6 + g, :], cst("tri_str"), half(GU, g), start=True, stop=True)
                        mm.then_inc(s["pairs"], 1)
                        at("scaled", 1)
                        at("silued", TILES + 4)
                        for n in range(3):
                            if n == 2:
                                at("beta_k", 1)
                            for t in range(TILES):
                                src = tiles(KB)[:, t, :] if n == 2 else SIL[:, t, n, :]
                                mm = pe.transpose(square(2 * n + t // 4, t), src, ident)
                            mm.then_inc(s["turned"], 1)
                        at("tcopied", 3)
                        at("decayed", 1)
                        for bank, o in ((6, KBH), (0, QH)):
                            for t in range(TILES):
                                c = slice(t * P, (t + 1) * P)
                                mm = pe.matmul(square(bank + t // 4, t), KH[:, c], o[:, c], start=True, stop=True)
                            mm.then_inc(s["inner"], 1)
                        at("level0", 1)
                        for t in range(TILES):
                            mm = pe.transpose(square(2 + t // 4, t), tiles(XXT)[:, t, :], ident)
                        mm.then_inc(s["other"], 1)
                        at("xcopied", 1)
                        at("attn", 1)
                        for l in range(1, LV):
                            at("masked", l)
                            for g in range(2):
                                if l > 1:
                                    at("subbed", 2 * (l - 2) + g + 1)
                                for t in range(4 * g, 4 * g + 4):
                                    mm = pe.matmul(square(g, t), tiles(CC)[:, t, :], tiles(XX)[:, t, :],
                                                   start=True, stop=True)
                                mm.then_inc(s["ymade"], 1)
                            for g in range(2):
                                at("ycopied", 2 * (l - 1) + g + 1)
                                for t in range(4 * g, 4 * g + 4):
                                    pe.matmul(square(2 + g, t), tiles(XXT)[:, t, :], tiles(YY)[:, t, :],
                                              start=True, stop=True)
                                    mm = pe.matmul(square(4 + g, t), tiles(YY)[:, t, :], tiles(XXT)[:, t, :],
                                                   start=True, stop=True)
                                mm.then_inc(s["corrected"], 1)
                        at("masked", LV)
                        for g in range(2):
                            at("subbed", 2 * (LV - 2) + g + 1)
                            for t in range(4 * g, 4 * g + 4):
                                mm = pe.matmul(square(g, t), tiles(XXT)[:, t, :], SIL[:, t, 2, :], start=True, stop=True)
                            mm.then_inc(s["zmade"], 1)
                        for g in range(2):
                            at("zcopied", g + 1)
                            for t in range(4 * g, 4 * g + 4):
                                mm = pe.matmul(square(2 + g, t), tiles(CC)[:, t, :], tiles(YY)[:, t, :],
                                               start=True, stop=True)
                            mm.then_inc(s["wmade"], 1)
                        for g in range(2):
                            at("wcopied", g + 1)
                            for t in range(4 * g, 4 * g + 4):
                                mm = pe.matmul(square(4 + g, t), tiles(XXT)[:, t, :], tiles(XX)[:, t, :],
                                               start=True, stop=True)
                            mm.then_inc(s["vmade"], 1)
                        for g in range(2):
                            at("delta", g + 1)
                            for t in range(4 * g, 4 * g + 4):
                                mm = pe.matmul(square(g, t), tiles(AT)[:, t, :], tiles(YY)[:, t, :], start=True, stop=True)
                            mm.then_inc(s["mixed"], 1)
                        for g in range(2):
                            at("onormed", g + 3)
                            for t in range(4 * g, 4 * g + 4):
                                mm = pe.transpose(square(2 + g, t), OO[:, t, :], ident)
                            mm.then_inc(s["oturned"], 1)
                        for g in range(2):
                            at("ocopied", g + 1)
                            for t in range(4 * g, 4 * g + 4):
                                mm = pe.matmul(square(4 + g, t), tiles(XX)[:, t, :], WO[:, bass.ts(h, P)],
                                               start=True, stop=True)
                            mm.then_inc(s["out"], 1)

                @block.scalar
                def _(act):
                    act.sem_inc(s["silued"], 4)
                    with act.Fori(0, H) as h:
                        at = waits(act, h)
                        for t in range(TILES):
                            at("projected", t + 1)
                            act.activation(BIG[0][:, t * HALF:(t + 1) * HALF], PS[:, t % 4, :], ACT.Silu)\
                                .then_inc(s["silued"], 1)
                        at("summed", 1)
                        act.activation(RS, RS, ACT.Sqrt).then_inc(s["rooted"], 1)
                        at("pairs", 1)
                        act.activation(halves(GAM), PS[:, 6:8, :], ACT.Exp).then_inc(s["decayed"], 1)
                        for n, o in enumerate((QH, KH, KBH)):
                            at("turned", n + 1)
                            act.activation(halves(o), PS[:, 2 * n:2 * n + 2, :], ACT.Copy).then_inc(s["tcopied"], 1)
                        at("other", 1)
                        act.activation(halves(XX), PS[:, 2:4, :], ACT.Copy).then_inc(s["xcopied"], 1)
                        for l in range(1, LV):
                            for g in range(2):
                                at("ymade", 2 * (l - 1) + g + 1)
                                act.activation(half(YY, g), PS[:, g, :], ACT.Copy).then_inc(s["ycopied"], 1)
                        for g in range(2):
                            at("zmade", g + 1)
                            act.activation(half(YY, g), PS[:, g, :], ACT.Copy).then_inc(s["zcopied"], 1)
                        for g in range(2):
                            at("wmade", g + 1)
                            act.activation(half(XX, g), PS[:, 2 + g, :], ACT.Copy).then_inc(s["wcopied"], 1)
                        at("vec", per["vec"] - 1)
                        act.activation(RO, RO, ACT.Sqrt).then_inc(s["rooted"], 1)
                        for g in range(2):
                            at("oturned", g + 1)
                            act.activation(half(XX, g), PS[:, 2 + g, :], ACT.Copy).then_inc(s["ocopied"], 1)

                @block.gpsimd
                def _(pool):
                    with pool.Fori(0, H) as h:
                        at = waits(pool, h)
                        pool.tensor_tensor(tiles(GU), each(cst("tri_inc")),
                                           G[:, :, bass.ds(h, 1)].broadcast_to([P, TILES, P]), ALU.mult)\
                            .then_inc(s["spread"], 1)
                        at("silued", TILES + 4)
                        pool.tensor_tensor(SQ2, SIL[:, :, 0:2, :], SIL[:, :, 0:2, :], ALU.mult).then_inc(s["squared"], 1)
                        at("onormed", 2)
                        pool.tensor_tensor(tiles(GW), SIL[:, :, 3, :], each(row("L3a_norm")), ALU.mult)\
                            .then_inc(s["gated"], 1)
                        for l in range(1, LV + 1):
                            if l == 1:
                                at("lower", 1)
                            else:
                                at("ymade", 2 * (l - 1))
                            a = C_AT["level"][0] + l * P
                            pool.tensor_tensor(tiles(CC), tiles(LT), each(CS[:, a:a + P]), ALU.mult)\
                                .then_inc(s["masked"], 1)

                @block.vector
                def _(dve):
                    dve.sem_inc(s["onormed"], 2)
                    with dve.Fori(0, H) as h:
                        at = waits(dve, h)
                        c = Chain(dve, s["vec"], h * per["vec"])
                        col = lambda a: a.broadcast_to([P, TILES, P])
                        at("squared", 1)
                        c.step(dve.tensor_reduce(RS, SQ2, AX.X, ALU.add))
                        dve.tensor_scalar(RS, RS, 1e-6, None, ALU.add).then_inc(s["summed"], 1)
                        at("rooted", 1)
                        c.step(dve.reciprocal(RS, RS))
                        c.mark(dve.scalar_tensor_tensor(out=SIL[:, :, 0, :], in0=SIL[:, :, 0, :], scalar=float(P) ** -0.5,
                                                        in1=col(RS[:, :, 0:1]), op0=ALU.mult, op1=ALU.mult))
                        dve.tensor_tensor(SIL[:, :, 1, :], SIL[:, :, 1, :], col(RS[:, :, 1:2]), ALU.mult)\
                            .then_inc(s["scaled"], 1)
                        at("scaled", 1)
                        b = col(BETA[:, :, bass.ds(h, 1)])
                        dve.tensor_tensor(tiles(KB), SIL[:, :, 1, :], b, ALU.mult).then_inc(s["beta_k"], 1)
                        c.mark(dve.tensor_tensor(SIL[:, :, 2, :], SIL[:, :, 2, :], b, ALU.mult))
                        at("decayed", 1)
                        c.step(dve.tensor_tensor(tiles(GAM), tiles(GAM), each(cst("tri_inc")), ALU.mult))
                        at("inner", 1)
                        dve.tensor_tensor(halves(LT), PS[:, 6:8, :], halves(GAM), ALU.mult).then_inc(s["lower"], 1)
                        at("lower", 1)
                        a = C_AT["level"][0]
                        c.step(dve.tensor_tensor(tiles(XXT), tiles(LT), each(CS[:, a:a + P]), ALU.mult))
                        dve.tensor_tensor(tiles(XXT), each(ident), tiles(XXT), ALU.subtract).then_inc(s["level0"], 1)
                        at("inner", 2)
                        dve.tensor_tensor(halves(AT), PS[:, 0:2, :], halves(GAM), ALU.mult).then_inc(s["attn"], 1)
                        at("level0", 1)
                        at("xcopied", 1)
                        for l in range(1, LV):
                            for g in range(2):
                                at("corrected", 2 * (l - 1) + g + 1)
                                c.mark(dve.tensor_tensor(half(XX, g), half(XX, g), PS[:, 2 + g, :], ALU.subtract))
                                dve.tensor_tensor(half(XXT, g), half(XXT, g), PS[:, 4 + g, :], ALU.subtract)\
                                    .then_inc(s["subbed"], 1)
                                at("subbed", 2 * (l - 1) + g + 1)
                        for g in range(2):
                            at("vmade", g + 1)
                            dve.tensor_tensor(half(YY, g), half(YY, g), PS[:, 4 + g, :], ALU.subtract).then_inc(s["delta"], 1)
                        at("mixed", 2)
                        for t in range(TILES):
                            c.mark(dve.bn_stats(stats[:, t, :], square(t // 4, t)))
                        c.join()
                        dve.memset(small[:, 740:741], 0.0)
                        for t in range(TILES):
                            c.mark(dve.bn_aggr(mv[:, t, :], stats[:, t, :]))
                        c.join()
                        c.step(dve.tensor_tensor(RO, mv[:, :, 0], mv[:, :, 0], ALU.mult))
                        c.step(dve.scalar_tensor_tensor(out=RO, in0=mv[:, :, 1], scalar=1e-6, in1=RO,
                                                        op0=ALU.add, op1=ALU.add))
                        at("rooted", 2)
                        c.step(dve.reciprocal(RO, RO))
                        at("gated", 1)
                        for g in range(2):
                            for t in range(4 * g, 4 * g + 4):
                                ins = dve.scalar_tensor_tensor(out=OO[:, t, :], in0=square(g, t), scalar=RO[:, t:t + 1],
                                                               in1=tiles(GW)[:, t, :], op0=ALU.mult, op1=ALU.mult)
                            ins.then_inc(s["onormed"], 1)
                        for g in range(2):
                            at("out", g + 1)
                            x = XR[:, 4 * g:4 * g + 4, :].rearrange("p t f -> p (t f)")
                            dve.tensor_tensor(x, x, PS[:, 4 + g, :], ALU.add).then_inc(s["added"], 1)
                        at("added", 2)
                        assert c.n == per["vec"]

        def l3_attn():
            normalize(X, XR, HT, 1e-5)
            normalize(XR, XN, HT, 1e-6, rms=True)
            delta_heads()
            normalize(XR, XN, HT, 1e-6, rms=True)
            RR = [BIG[2][:, c * TOK:(c + 1) * TOK] for c in range(4)]
            with phase("made", "rect", "evac", "ymade", "added") as (block, s):
                @block.tensor
                def _(pe):
                    for c in range(4):
                        if c >= 2:
                            pe.wait_ge(s["rect"], c - 1)
                        for h in range(2):
                            mm = pe.matmul(PS[:, 2 * (c % 2) + h, :], w("L3a_fc")[:, c * P:(c + 1) * P],
                                           HT[:, h * HALF:(h + 1) * HALF], start=True, stop=True)
                        mm.then_inc(s["made"], 1)
                    pe.wait_ge(s["evac"], 4)
                    for t in range(TILES):
                        for c in range(4):
                            mm = pe.matmul(square(4 + t // 4, t), RR[c][:, t * P:(t + 1) * P],
                                           w("L3a_proj")[:, c * P:(c + 1) * P], start=c == 0, stop=c == 3)
                        mm.then_inc(s["ymade"], 1)

                @block.scalar
                def _(act):
                    for c in range(4):
                        act.wait_ge(s["made"], c + 1)
                        act.activation(halves(RR[c]), PS[:, 2 * (c % 2):2 * (c % 2) + 2, :], ACT.Relu).then_inc(s["rect"], 1)
                        act.wait_ge(s["rect"], c + 1)
                        act.activation(RR[c], RR[c], ACT.Square).then_inc(s["evac"], 1)

                @block.vector
                def _(dve):
                    whole = lambda a: a[:, :, :].rearrange("p t f -> p (t f)")
                    dve.tensor_tensor(whole(X), whole(X), whole(XR), ALU.add).then_inc(s["added"], 1)
                    dve.wait_ge(s["added"], 1)
                    for h in range(2):
                        dve.wait_ge(s["ymade"], 4 * h + 4)
                        x = X[:, 4 * h:4 * h + 4, :].rearrange("p t f -> p (t f)")
                        dve.tensor_tensor(x, x, PS[:, 4 + h, :], ALU.add).then_inc(s["added"], 1)
                    dve.wait_ge(s["added"], 3)

        def l3_ffn():
            normalize(X, XN, HT, 1e-5)
            QMAX = 32767.0
            inv_q = float(np.float32(1.0) / np.float32(QMAX))
            WQ = EXTRA[:, 0:1152].rearrange("p (n i) -> p n i", n=36)
            WF = EXTRA[:, 0:1152]
            WD = EXTRA[:, 1152:2304]
            MB = EXTRA[:, 2304:2340]
            IB = EXTRA[:, 2340:2376]
            SC = EXTRA[:, 2400:2412]
            UP, GT, SG = BIG[0][:, 0:3072], BIG[1][:, 0:3072], BIG[2][:, 0:3072]
            blocks32 = lambda a: a.unsqueeze(2).broadcast_to([P, 36, 32])
            with phase("vec", "turned", "copied") as (block, s):
                @block.vector
                def _(dve):
                    c = Chain(dve, s["vec"])
                    src = w("L3f_w").rearrange("p (n i) -> p n i", n=36)
                    c.step(dve.tensor_reduce(MB, src, AX.X, ALU.max, apply_absolute_value=True))
                    c.step(dve.tensor_scalar(MB, MB, float(np.float32(1) / np.float32(7)), 1e-12, ALU.mult, ALU.max))
                    c.step(dve.reciprocal(IB, MB))
                    c.step(dve.tensor_tensor(WQ, src, blocks32(IB), ALU.mult))
                    c.step(dve.tensor_scalar(WF, WF, MAGIC, None, ALU.add))
                    c.step(dve.tensor_scalar(WF, WF, -MAGIC, -8.0, ALU.add, ALU.max))
                    c.step(dve.tensor_scalar(WF, WF, 7.0, None, ALU.min))
                    c.step(dve.tensor_tensor(WQ, WQ, blocks32(MB), ALU.mult))

                @block.tensor
                def _(pe):
                    pe.wait_ge(s["vec"], 8)
                    for n in range(9):
                        mm = pe.transpose(PS[:, n // 4, (n % 4) * P:(n % 4 + 1) * P], WF[:, n * P:(n + 1) * P], ident)
                    mm.then_inc(s["turned"], 1)

                @block.scalar
                def _(act):
                    act.wait_ge(s["turned"], 1)
                    act.activation(WD[:, 0:1024].rearrange("p (a b) -> p a b", a=2), PS[:, 0:2, :], ACT.Copy)\
                        .then_inc(s["copied"], 1)
                    act.activation(WD[:, 1024:1152], PS[:, 2, 0:P], ACT.Copy).then_inc(s["copied"], 1)

            def quantize(items, after=None):
                with phase("vec", "pooled") as (block, s):
                    @block.gpsimd
                    def _(pool):
                        pool.wait_ge(s["vec"], 1)
                        n = len(items)
                        a = items[0][2]
                        pool.partition_all_reduce(SC[:, 6:6 + n], SC[:, a:a + n], P, bass.bass_isa.ReduceOp.max)\
                            .then_inc(s["pooled"], 1)

                    @block.vector
                    def _(dve):
                        c = Chain(dve, s["vec"])
                        n = len(items)
                        a = items[0][2]
                        for k, (src, dst, col) in enumerate(items):
                            ins = dve.tensor_reduce(SC[:, col:col + 1], src, AX.X, ALU.max, apply_absolute_value=True)
                            if k == n - 1:
                                c.mark(ins)
                        dve.wait_ge(s["pooled"], 1)
                        c.step(dve.tensor_scalar(SC[:, a:a + n], SC[:, 6:6 + n], inv_q, 1e-12, ALU.mult, ALU.max))
                        c.step(dve.reciprocal(SC[:, 8:8 + n], SC[:, a:a + n]))
                        for k, (src, dst, col) in enumerate(items):
                            c.step(dve.tensor_scalar(dst, src, SC[:, 8 + k:9 + k], MAGIC, ALU.mult, ALU.add))
                            c.step(dve.tensor_scalar(dst, dst, -MAGIC, -QMAX - 1.0, ALU.add, ALU.max))
                            c.step(dve.tensor_scalar(dst, dst, QMAX, SC[:, col:col + 1], ALU.min, ALU.mult))

            quantize([(HT[:, :], QT[:, :], 0)])
            with phase("made", "copied") as (block, s):
                @block.tensor
                def _(pe):
                    for n in range(6):
                        if n >= 4:
                            pe.wait_ge(s["copied"], n - 3)
                        for h in range(2):
                            mm = pe.matmul(PS[:, 2 * (n % 4) + h, :], WD[:, n * P:(n + 1) * P],
                                           QT[:, h * HALF:(h + 1) * HALF], start=True, stop=True)
                        mm.then_inc(s["made"], 1)

                @block.scalar
                def _(act):
                    for n in range(6):
                        act.wait_ge(s["made"], n + 1)
                        o = (GT if n < 3 else UP)[:, (n % 3) * TOK:(n % 3 + 1) * TOK]
                        act.activation(halves(o), PS[:, 2 * (n % 4):2 * (n % 4) + 2, :], ACT.Copy).then_inc(s["copied"], 1)
            quantize([(GT, GT, 0), (UP, UP, 1)])
            with phase("signed", "vec") as (block, s):
                @block.scalar
                def _(act):
                    act.activation(SG, GT, ACT.Sigmoid).then_inc(s["signed"], 1)

                @block.vector
                def _(dve):
                    c = Chain(dve, s["vec"])
                    dve.wait_ge(s["signed"], 1)
                    c.step(dve.tensor_scalar(SG, SG, 65536.0, MAGIC, ALU.mult, ALU.add))
                    c.step(dve.tensor_scalar(SG, SG, -MAGIC, 0.0, ALU.add, ALU.max))
                    c.step(dve.tensor_scalar(SG, SG, 65535.0, 1.0 / 65536.0, ALU.min, ALU.mult))
                    c.step(dve.tensor_tensor(GT, GT, SG, ALU.mult))
            quantize([(GT, GT, 0)])
            with phase("vec") as (block, s):
                @block.vector
                def _(dve):
                    dve.tensor_tensor(UP, UP, GT, ALU.mult).then_inc(s["vec"], 1)
            quantize([(UP, UP, 0)])
            with phase("ymade", "added") as (block, s):
                @block.tensor
                def _(pe):
                    for t in range(TILES):
                        for c in range(3):
                            mm = pe.matmul(square(t // 4, t), UP[:, c * TOK + t * P:c * TOK + (t + 1) * P],
                                           WD[:, (6 + c) * P:(7 + c) * P], start=c == 0, stop=c == 2)
                    mm.then_inc(s["ymade"], 1)

                @block.vector
                def _(dve):
                    dve.wait_ge(s["ymade"], 1)
                    x = X[:, :, :].rearrange("p (a t) f -> p a (t f)", a=2)
                    dve.tensor_tensor(x, x, PS[:, 0:2, :], ALU.add).then_inc(s["added"], 1)

        def store():
            with phase("stored") as (block, s):
                @block.sync
                def _(sp):
                    sp.dma_start(out, X[:, :, :]).then_inc(s["stored"], 16)
                    sp.wait_ge(s["stored"], 16)

        def l0_attn():
            normalize(X, XN, HT, 1e-5)
            qkv = w("L0a_qkv")
            token_qk(qkv[:, 0:P], qkv[:, P:2 * P], True, HD ** -0.5)
            project([], (HT, qkv[:, 2 * P:3 * P], None))
            attend(w("L0a_o"), X, None, row("L0a_o"))

        def l0_xattn():
            normalize(X, XN, HT, 1e-5)
            project([(QT, w("L0x_q"), HT, None, HD ** -0.5), (KT, w("L0x_k"), CT, None, 1.0)],
                    (CT, w("L0x_v"), None))
            with phase("rel") as (block, s):
                @block.sync
                def _(sp):
                    for b in range(PER):
                        sp.dma_start(REL[b * SEQ:(b + 1) * SEQ, :, :], d["rel"]).then_inc(s["rel"], 16)
                    sp.wait_ge(s["rel"], 32)
            attend(w("L0x_o"), X, "rel", row("L0x_o"))

        def l1_attn():
            normalize(X, XN, HT, 1e-5)
            project([(QT, w("L1a_q"), HT, None, w("c_L1a_scale")), (KT, w("L1a_k"), HT, None, 1.0)],
                    (HT, w("L1a_v"), None))
            attend(w("L1a_o"), X, "strict", row("L1a_o"))

        def l2_xattn():
            normalize(X, XN, HT, 1e-5)
            project([(QT, w("L2x_q"), HT, None, HD ** -0.5), (KT, w("L2x_k"), CT, None, 1.0)],
                    (CT, w("L2x_v"), None))
            attend(w("L2x_o"), X)

        def l3_xattn():
            normalize(X, XN, HT, 1e-5)
            project([(QT, w("L3x_q"), HT, w("c_L3x_bq"), HD ** -0.5), (KT, w("L3x_k"), CT, w("c_L3x_bk"), 1.0)],
                    (CT, w("L3x_v"), row("L3x_v")))
            attend(w("L3x_o"), X, None, row("L3x_o"))

        blocks = [l0_attn, l0_xattn, l0_ffn, l1_attn, l1_xattn, l1_ffn, l2_attn, l2_xattn, l2_ffn, l3_attn, l3_xattn, l3_ffn]
        for f in blocks[first:last]:
            f()
        store()


def pack(inputs):
    g = {k: np.asarray(v) for k, v in inputs.items()}
    W = {}
    W["L0a_qkv"] = g["L0_attn_w_qkv"].T
    W["L0a_o"] = g["L0_attn_w_proj"].T
    W["L0x_q"], W["L0x_k"], W["L0x_v"], W["L0x_o"] = (g["L0_xattn_" + n].T for n in ("wq", "wk", "wv", "fc_w"))
    W["L0f_router"] = g["L0_ffn_router_weight"].T
    W["L0f_sw1"] = g["L0_ffn_sw1"].T
    W["L0f_sw2"] = g["L0_ffn_sw2"].T.reshape(2, P, P).transpose(1, 0, 2)
    q3 = g["L1_attn_w_qkv"]
    W["L1a_q"], W["L1a_k"], W["L1a_v"] = q3[:, 0:P], q3[:, P:2 * P], q3[:, 2 * P:]
    W["L1a_o"] = g["L1_attn_w_out"]
    for a, b in (("L1xs_", "L1_xattn_src_w"), ("L1xt_", "L1_xattn_tgt_w")):
        for n in "qkvo":
            W[a + n] = g[b + n]
    lw = g["L1_xattn_lstm_w"].reshape(3, P, 4, P)[:, :, [0, 2, 3, 1], :]
    W["L1x_wx"], W["L1x_wc"], W["L1x_wh"] = lw[0], lw[1], lw[2]
    W["L1x_w1"] = g["L1_xattn_ffn_w1"]
    W["L1x_w2"] = g["L1_xattn_ffn_w2"].reshape(4, P, P).transpose(1, 0, 2)
    q3 = g["L1_ffn_Wqkv"].reshape(P, HEADS, 3, HD)
    W["L1f_q"], W["L1f_k"], W["L1f_v"] = q3[:, :, 0], q3[:, :, 1], q3[:, :, 2]
    W["L1f_o"], W["L1f_gate"] = g["L1_ffn_Wproj"], g["L1_ffn_Wgate"]
    W["L2a_w"] = g["L2_attn_W"]
    W["L2x_q"], W["L2x_k"], W["L2x_v"], W["L2x_o"] = (g["L2_xattn_w_" + n].T for n in "qkvo")
    W["L2f_gate"] = g["L2_ffn_gate_w"]
    W["L3a_b"], W["L3a_a"], W["L3a_fc"] = g["L3_attn_Wb"], g["L3_attn_Wa"], g["L3_attn_W_fc"]
    W["L3a_proj"] = g["L3_attn_W_proj"].reshape(4, P, P).transpose(1, 0, 2)
    W["L3x_q"], W["L3x_k"], W["L3x_v"], W["L3x_o"] = (g["L3_xattn_W" + n].T for n in "qkvo")
    W["L3f_w"] = np.concatenate([g["L3_ffn_w_gate"].reshape(3, P, P), g["L3_ffn_w_up"].reshape(3, P, P),
                                 g["L3_ffn_w_down"].reshape(P, 3, P).transpose(1, 0, 2)]).transpose(1, 0, 2)
    W["c_L1a_scale"] = np.repeat(g["L1_attn_scale"].reshape(-1), HD)
    for a, b in (("L1xs_b", "L1_xattn_src_b"), ("L1xt_b", "L1_xattn_tgt_b"), ("L3x_b", "L3_xattn_b")):
        for n in "qk":
            W["c_" + a + n] = g[b + n]
    W["c_L1x_lstm_b"] = g["L1_xattn_lstm_b"].reshape(4, P)[[0, 2, 3, 1]].T
    W["c_L1x_b1"] = g["L1_xattn_ffn_b1"].reshape(4, P).T
    for n in ("ln1_g", "ln1_b", "ln2_g", "ln2_b"):
        W["c_" + n] = g["L1_ffn_" + n]
    W["c_L1f_b1"] = g["L1_ffn_b1"].reshape(32, P).T
    W["c_L2a_b"] = g["L2_attn_b"]
    W["c_tgt_bias"] = np.concatenate([g["L1_xattn_tgt_bias"].reshape(SEQ, SEQ)] * 2)
    R = {"L0a_o": g["L0_attn_b_proj"], "L0a_gamma": np.concatenate([g["L0_attn_q_gamma"], g["L0_attn_k_gamma"]]),
         "L0a_beta": np.concatenate([g["L0_attn_q_beta"], g["L0_attn_k_beta"]]), "L0x_o": g["L0_xattn_fc_b"],
         "L0f_bias": g["L0_ffn_expert_bias"], "L1a_o": g["L1_attn_b_out"], "L1xs_v": g["L1_xattn_src_bv"],
         "L1xt_v": g["L1_xattn_tgt_bv"], "L1xs_o": g["L1_xattn_src_bo"], "L1xt_o": g["L1_xattn_tgt_bo"],
         "L1x_b2": g["L1_xattn_ffn_b2"], "L2f_b": g["L2_ffn_gate_b"], "L3a_Alog": g["L3_attn_A_log"],
         "L3a_dt": g["L3_attn_dt_bias"], "L3a_norm": g["L3_attn_o_norm_w"], "L3x_v": g["L3_xattn_bv"],
         "L3x_o": g["L3_xattn_bo"]}
    a = {}
    a["x"] = g["x"].reshape(TILES, P, P).transpose(1, 0, 2)
    a["ctxT"] = g["ctx_1024"].reshape(TOK, P).T
    a["weights"] = np.concatenate([W[n].reshape(P, m) for n, m in WEIGHTS], 1)
    a["rows"] = np.concatenate([R[n].reshape(1, m) for n, m in ROWS], 1)
    a["consts"] = shape_constants()
    a["src_bias"] = g["mask_Bx1x1xS2_ff0"].reshape(TILES, PER, SEQ).transpose(1, 0, 2)
    q, k = np.arange(SEQ)[:, None], np.arange(SEQ)[None, :]
    a["rel"] = g["L0_xattn_rel_table"][k - q + 255].transpose(0, 2, 1)
    a["L0f_w1"] = g["L0_ffn_w1"].transpose(1, 0, 2).reshape(P, 4096)
    a["L0f_w2"] = g["L0_ffn_w2"].reshape(32, P, P).transpose(1, 0, 2).reshape(P, 4096)
    a["L1f_w1"] = g["L1_ffn_W1"].transpose(1, 0, 2).reshape(P, 4096)
    a["L1f_w2"] = g["L1_ffn_W2"].reshape(32, P, P).transpose(1, 0, 2).reshape(P, 4096)
    a["L1f_b2"] = g["L1_ffn_b2"]
    both = lambda e, s: np.concatenate([g["L2_ffn_" + e], g["L2_ffn_" + s]])
    a["L2f_w1"] = both("ew1", "sw1").transpose(1, 0, 2).reshape(P, 18 * 256)
    a["L2f_w3"] = both("ew3", "sw3").transpose(1, 0, 2).reshape(P, 18 * 256)
    a["L2f_w2"] = both("ew2", "sw2").reshape(36, P, P).transpose(1, 0, 2).reshape(P, 36 * P)
    a["L3a_w"] = np.concatenate([g["L3_attn_W" + n].reshape(P, 8, 1, P) for n in "qkvg"], 2).reshape(P, 4096)
    a["L3a_wo"] = g["L3_attn_Wo"].reshape(8, P, P).transpose(1, 0, 2).reshape(P, 1024)
    return {k: np.ascontiguousarray(v) for k, v in a.items()}


def kernel(**inputs):
    import concourse.bacc as _bacc
    from concourse.bass_utils import run_bass_kernel_spmd as _run

    nc = _bacc.Bacc("TRN2", target_bir_lowering=False, num_devices=1)
    arrays = pack(inputs)
    d = {k: nc.dram_tensor(k + "_dram", v.shape, F32, kind="ExternalInput").ap() for k, v in arrays.items()}
    out = nc.dram_tensor("out_dram", (P, TILES, P), F32, kind="ExternalOutput").ap()
    decoder_kernel(nc, d, out)
    r = _run(nc, [{k + "_dram": v for k, v in arrays.items()}], core_ids=[0])
    return r.results[0]["out_dram"].transpose(1, 0, 2).reshape(BATCH, SEQ, P)
```

```python
from contextlib import ExitStack, contextmanager

import numpy as np
import concourse.bass as bass
from concourse import mybir

ALU = mybir.AluOpType
ACT = mybir.ActivationFunctionType
AX = mybir.AxisListType
F32 = mybir.dt.float32
BF16 = mybir.dt.bfloat16

P = 128
SEQ = 64
BATCH = 16
TOK = BATCH * SEQ
TILES = TOK // P
PER = P // SEQ
HEADS = 16
HD = P // HEADS
GROUPS = 4
HALF = 512
SLOT = HD + 1
MAGIC = 12582912.0
NEVER = -3.0e38

WEIGHTS = [
    ("L0a_qkv", 384), ("L0a_o", 128), ("L0x_q", 128), ("L0x_k", 128), ("L0x_v", 128), ("L0x_o", 128),
    ("L0f_router", 64), ("L0f_sw1", 256), ("L0f_sw2", 256),
    ("L1a_q", 128), ("L1a_k", 128), ("L1a_v", 128), ("L1a_o", 128),
    ("L1xs_q", 128), ("L1xs_k", 128), ("L1xs_v", 128), ("L1xs_o", 128),
    ("L1xt_q", 128), ("L1xt_k", 128), ("L1xt_v", 128), ("L1xt_o", 128),
    ("L1x_wx", 512), ("L1x_wc", 512), ("L1x_wh", 512), ("L1x_w1", 512), ("L1x_w2", 512),
    ("L1f_q", 128), ("L1f_k", 128), ("L1f_v", 128), ("L1f_o", 128), ("L1f_gate", 8),
    ("L2a_w", 128), ("L2x_q", 128), ("L2x_k", 128), ("L2x_v", 128), ("L2x_o", 128), ("L2f_gate", 16),
    ("L3a_b", 8), ("L3a_a", 8), ("L3a_fc", 512), ("L3a_proj", 512),
    ("L3x_q", 128), ("L3x_k", 128), ("L3x_v", 128), ("L3x_o", 128),
    ("L3f_w", 1152),
    ("c_L1a_scale", 1), ("c_L1xs_bq", 1), ("c_L1xs_bk", 1), ("c_L1xt_bq", 1), ("c_L1xt_bk", 1),
    ("c_L1x_lstm_b", 4), ("c_L1x_b1", 4), ("c_ln1_g", 1), ("c_ln1_b", 1), ("c_ln2_g", 1), ("c_ln2_b", 1),
    ("c_L1f_b1", 32), ("c_L2a_b", 1), ("c_L3x_bq", 1), ("c_L3x_bk", 1),
    ("c_tgt_bias", 64),
]
ROWS = [
    ("L0a_o", 128), ("L0a_gamma", 16), ("L0a_beta", 16), ("L0x_o", 128), ("L0f_bias", 64), ("L1a_o", 128),
    ("L1xs_v", 128), ("L1xt_v", 128), ("L1xs_o", 128), ("L1xt_o", 128), ("L1x_b2", 128), ("L2f_b", 16),
    ("L3a_Alog", 8), ("L3a_dt", 8), ("L3a_norm", 128), ("L3x_v", 128), ("L3x_o", 128),
]
CONSTS = [
    ("ident", 128), ("gmask", GROUPS), ("emask", HEADS), ("tri_inc", 128), ("tri_str", 128), ("ones", 128),
    ("level", 6 * 128), ("lw", 128), ("off", 128), ("rope_c", 8), ("rope_s", 8), ("causal", 64),
    ("strict", 64), ("notfirst", 1), ("upper", 128), ("pick", 32 * 128), ("two", 128),
]


def offsets(table):
    at, out = 0, {}
    for name, n in table:
        out[name] = (at, n)
        at += n
    return out, at


W_AT, W_COLS = offsets(WEIGHTS)
R_AT, R_COLS = offsets(ROWS)
C_AT, C_COLS = offsets(CONSTS)


def shape_constants():
    p = np.arange(P)
    q = p % SEQ
    same = (p[:, None] // SEQ) == (p[None, :] // SEQ)
    c = {}
    c["ident"] = np.eye(P)
    c["gmask"] = (p[:, None] // HD) % 4 == np.arange(GROUPS)[None, :]
    c["emask"] = (p[:, None] // SEQ) == np.arange(HEADS)[None, :] % 2
    c["tri_inc"] = same & (p[:, None] <= p[None, :])
    c["tri_str"] = same & (p[:, None] > p[None, :])
    c["ones"] = np.ones((P, P))
    levels = []
    for l in range(6):
        m = 2 ** l
        levels.append((p[:, None] // (2 * m) == p[None, :] // (2 * m))
                      & (p[:, None] // m % 2 == 0) & (p[None, :] // m % 2 == 1))
    c["level"] = np.concatenate(levels, 1)
    d = np.abs(q[:, None] - q[None, :]).astype(np.float32)
    c["lw"] = np.where(same & (d != 0), np.float32(1) / (d + np.float32(1e-7)), 0)
    c["off"] = same & (d != 0)
    inv = (1.0 / 10000.0 ** (np.arange(4, dtype=np.float32) / 4)).astype(np.float32)
    ang = (q[:, None].astype(np.float32) * inv[None, :]).astype(np.float32)
    c["rope_c"] = np.concatenate([np.cos(ang), np.cos(ang)], 1)
    c["rope_s"] = np.concatenate([-np.sin(ang), np.sin(ang)], 1)
    k = np.arange(SEQ)
    c["causal"] = np.where(k[None, :] > q[:, None], -1e9, 0)
    c["strict"] = np.where(k[None, :] >= q[:, None], -1e30, 0)
    c["notfirst"] = (q != 0)[:, None]
    c["upper"] = p[:, None] < p[None, :]
    pick = np.zeros((P, 32, P))
    for i in range(32):
        for r in range(P):
            if r % 64 // 2 == i:
                pick[r, i, (r % 2) * 64:(r % 2) * 64 + 64] = 1
    c["pick"] = pick.reshape(P, 32 * P)
    two = np.zeros((P, P))
    two[0, :SEQ] = 1
    two[1, SEQ:] = 1
    c["two"] = two
    return np.concatenate([np.asarray(c[n], np.float32) for n, _ in CONSTS], 1)


class Chain:

    def __init__(self, eng, sem, base=0):
        self.eng, self.sem, self.base, self.n = eng, sem, base, 0

    def mark(self, ins):
        ins.then_inc(self.sem, 1)
        self.n += 1

    def join(self):
        self.eng.wait_ge(self.sem, self.base + self.n)

    def step(self, ins):
        self.mark(ins)
        self.join()


def decoder_kernel(nc, d, out, first=0, last=12):
    ctx = ExitStack()
    uid = [0]
    used = []

    def sb(name, shape, dt=F32):
        return ctx.enter_context(nc.sbuf_tensor(name, shape, dt))

    @contextmanager
    def phase(*names):
        uid[0] += 1
        sems = [nc.alloc_semaphore(f"{n}_{uid[0]}") for n in names]
        if used:
            nc.clear_and_free_semaphores(used.pop())
        with nc.Block() as block:
            yield block, dict(zip(names, sems))
        used.append(sems)

    with ctx:
        PS = ctx.enter_context(nc.psum_tensor("PS", [P, 8, HALF], F32))
        WT = sb("WT", [P, W_COLS])
        RW = sb("RW", [P, R_COLS])
        CS = sb("CS", [P, C_COLS])
        X = sb("X", [P, TILES, P])
        XN = sb("XN", [P, TILES, P])
        XR = sb("XR", [P, TILES, P])
        HT = sb("HT", [P, TOK])
        CT = sb("CT", [P, TOK])
        QT = sb("QT", [P, TOK])
        KT = sb("KT", [P, TOK])
        VD = sb("VD", [P, BATCH, HEADS, SLOT])
        identb = sb("identb", [P, P], BF16)
        causalb = sb("causalb", [P, SEQ], BF16)
        strictb = sb("strictb", [P, SEQ], BF16)
        upperb = sb("upperb", [P, P], BF16)
        onesb = sb("onesb", [P, P], BF16)
        pickb = sb("pickb", [P, 32 * P], BF16)
        stats = sb("stats", [P, TILES, 6])
        mv = sb("mv", [P, TILES, 2])
        rstd = sb("rstd", [P, TILES])
        idle = sb("idle", [P, 1])
        SRC = sb("SRC", [2, TILES, SEQ])
        BIG = [sb(f"BIG{i}", [P, 4096]) for i in range(4)]
        REL = BIG[3][:, 0:1024].rearrange("p (h k) -> p h k", h=HEADS)

        def w(name):
            a, n = W_AT[name]
            return WT[:, a:a + n]

        def row(name):
            a, n = R_AT[name]
            return RW[:, a:a + n]

        def cst(name):
            a, n = C_AT[name]
            return CS[:, a:a + n]

        ident = cst("ident")

        with phase("loaded", "made") as (block, s):
            @block.sync
            def _(sp):
                sp.dma_start(X[:, :, :], d["x"]).then_inc(s["loaded"], 16)
                sp.dma_start(CS[:, :], d["consts"]).then_inc(s["loaded"], 16)
                sp.dma_start(CT[:, :], d["ctxT"]).then_inc(s["loaded"], 16)
                sp.dma_start(SRC[:, :, :], d["src_bias"]).then_inc(s["loaded"], 16)

            @block.scalar
            def _(act):
                act.dma_start(WT[:, :], d["weights"]).then_inc(s["loaded"], 16)
                act.dma_start(RW[:, :], d["rows"][0:1, :].broadcast_to([P, R_COLS])).then_inc(s["loaded"], 16)
                act.wait_ge(s["loaded"], 96)

            @block.vector
            def _(dve):
                dve.wait_ge(s["loaded"], 96)
                for dst, name in ((identb, "ident"), (causalb, "causal"), (strictb, "strict"),
                                  (upperb, "upper"), (onesb, "ones"), (pickb, "pick")):
                    dve.tensor_copy(dst[:, :], cst(name)).then_inc(s["made"], 1)
                dve.tensor_copy(VD[:, :, :, HD],
                                cst("emask").unsqueeze(1).broadcast_to([P, BATCH, HEADS])).then_inc(s["made"], 1)
                dve.memset(idle[:, :], 0.0).then_inc(s["made"], 1)
                dve.wait_ge(s["made"], 8)

        def normalize(src, dst, dstT, eps, gain=None, shift=None, rms=False):
            with phase("stat", "rooted", "normed", "turned", "copied") as (block, s):
                @block.vector
                def _(dve):
                    c = Chain(dve, s["stat"])
                    for t in range(TILES):
                        c.mark(dve.bn_stats(stats[:, t, :], src[:, t, :]))
                    c.join()
                    for t in range(TILES):
                        c.mark(dve.bn_aggr(mv[:, t, :], stats[:, t, :]))
                    c.join()
                    if rms:
                        c.step(dve.tensor_tensor(rstd[:, :], mv[:, :, 0], mv[:, :, 0], ALU.mult))
                        c.step(dve.tensor_tensor(mv[:, :, 1], mv[:, :, 1], rstd[:, :], ALU.add))
                        c.step(dve.memset(mv[:, :, 0], 0.0))
                    c.step(dve.tensor_scalar(rstd[:, :], mv[:, :, 1], eps, None, ALU.add))
                    dve.wait_ge(s["rooted"], 1)
                    c.step(dve.reciprocal(rstd[:, :], rstd[:, :]))
                    for t in range(TILES):
                        dve.tensor_scalar(dst[:, t, :], src[:, t, :], mv[:, t, 0:1], rstd[:, t:t + 1],
                                          ALU.subtract, ALU.mult).then_inc(s["normed"], 1)

                @block.tensor
                def _(pe):
                    for t in range(TILES):
                        pe.wait_ge(s["normed"], t + 1)
                        pe.transpose(PS[:, t // 4, (t % 4) * P:(t % 4 + 1) * P], dst[:, t, :], ident)\
                          .then_inc(s["turned"], 1)

                @block.scalar
                def _(act):
                    act.activation(idle[:, :], idle[:, :], ACT.Sqrt)
                    act.wait_ge(s["stat"], 2 * TILES + (4 if rms else 1))
                    act.activation(rstd[:, :], rstd[:, :], ACT.Sqrt).then_inc(s["rooted"], 1)
                    for h in range(2):
                        act.wait_ge(s["turned"], 4 * h + 4)
                        o = dstT[:, h * HALF:(h + 1) * HALF]
                        if gain is None:
                            act.activation(o, PS[:, h, :], ACT.Copy).then_inc(s["copied"], 1)
                        else:
                            act.activation(o, PS[:, h, :], ACT.Identity, bias=shift, scale=gain)\
                               .then_inc(s["copied"], 1)
                    act.wait_ge(s["copied"], 2)

        def project(items, values=None):
            twice = BIG[3][:, 1024:3072].rearrange("p (b c k) -> p b c k", b=BATCH, c=2)
            with phase("made", "evac", "twice", "vmade", "vevac") as (block, s):
                @block.scalar
                def _(act):
                    if values:
                        act.activation(twice, values[0][:, :].rearrange("p (b k) -> p b k", b=BATCH).unsqueeze(2)
                                       .broadcast_to([P, BATCH, 2, SEQ]), ACT.Copy).then_inc(s["twice"], 1)

                @block.tensor
                def _(pe):
                    for n, (dst, wt, src, bias, factor) in enumerate(items):
                        if n >= 2:
                            pe.wait_ge(s["evac"], n - 1)
                        for h in range(2):
                            pe.matmul(PS[:, 2 * (n % 2) + h, :], wt, src[:, h * HALF:(h + 1) * HALF],
                                      start=True, stop=True).then_inc(s["made"], 1)
                    if values:
                        src, wv, brow = values
                        pe.wait_ge(s["twice"], 1)
                        for b in range(BATCH):
                            o = PS[:, 4 + b // 4, (b % 4) * P:(b % 4 + 1) * P]
                            keys = BIG[3][:, 1024 + b * P:1024 + (b + 1) * P]
                            mm = pe.matmul(o, keys, wv, start=True, stop=brow is None)
                            if brow is not None:
                                mm = pe.matmul(o, cst("ones")[0:1, :], brow[0:1, :], start=False, stop=True)
                            mm.then_inc(s["vmade"], 1)

                def evacuate(eng, n):
                    dst, wt, src, bias, factor = items[n]
                    eng.wait_ge(s["made"], 2 * n + 2)
                    view = dst[:, :].rearrange("p (a b) -> p a b", a=2)
                    return view, PS[:, 2 * (n % 2):2 * (n % 2) + 2, :], bias, factor

                @block.vector
                def _(dve):
                    for n in range(len(items)):
                        o, i, bias, factor = evacuate(dve, n)
                        dve.tensor_scalar(o, i, 0.0 if bias is None else bias, factor, ALU.add, ALU.mult)\
                           .then_inc(s["evac"], 1)
                    dve.wait_ge(s["evac"], len(items)) if items else None
                    if values:
                        em = cst("emask").unsqueeze(1).unsqueeze(3).broadcast_to([P, 4, HEADS, HD])
                        for g in range(BATCH // 4):
                            dve.wait_ge(s["vmade"], 4 * g + 4)
                            dve.tensor_tensor(VD[:, 4 * g:4 * g + 4, :, 0:HD],
                                              PS[:, 4 + g, :].rearrange("p (b h e) -> p b h e", b=4, h=HEADS),
                                              em, ALU.mult).then_inc(s["vevac"], 1)
                        dve.wait_ge(s["vevac"], BATCH // 4)

        def token_qk(wq, wk, rotate_norm, factor):
            QK = BIG[0][:, 0:2048]
            A = BIG[1][:, 0:2048]
            B = BIG[2][:, 0:2048]
            G = 2 * TILES * HEADS
            grp = lambda a: a.rearrange("p (g e) -> p g e", e=HD)
            sm = BIG[3][:, 0:G]
            va = BIG[3][:, 512:512 + G]
            rs = BIG[3][:, 1024:1024 + G]
            wide = lambda a: a.unsqueeze(2).broadcast_to([P, G, HD])
            with phase("made", "copied", "vec", "rooted", "ready", "turned", "evac") as (block, s):
                @block.tensor
                def _(pe):
                    for t in range(TILES):
                        ht = HT[:, t * P:(t + 1) * P]
                        o = PS[:, t // 2, (t % 2) * 256:(t % 2) * 256 + 256]
                        pe.matmul(o[:, 0:P], ht, wq, start=True, stop=True)
                        pe.matmul(o[:, P:2 * P], ht, wk, start=True, stop=True).then_inc(s["made"], 1)
                    pe.wait_ge(s["ready"], 1)
                    for n in range(2):
                        for t in range(TILES):
                            pe.transpose(PS[:, 4 + 2 * n + t // 4, (t % 4) * P:(t % 4 + 1) * P],
                                         QK[:, (2 * t + n) * P:(2 * t + n + 1) * P], ident).then_inc(s["turned"], 1)

                @block.scalar
                def _(act):
                    act.wait_ge(s["made"], TILES)
                    act.activation(QK.rearrange("p (a b) -> p a b", a=4), PS[:, 0:4, :], ACT.Copy).then_inc(s["copied"], 1)
                    if rotate_norm:
                        act.wait_ge(s["vec"], 6)
                        act.activation(rs, va, ACT.Sqrt).then_inc(s["rooted"], 1)
                    for n in range(2):
                        act.wait_ge(s["turned"], TILES * (n + 1))
                        dst = (QT, KT)[n]
                        act.activation(dst[:, :].rearrange("p (a b) -> p a b", a=2), PS[:, 4 + 2 * n:6 + 2 * n, :],
                                       ACT.Copy, scale=factor if n == 0 else 1.0).then_inc(s["evac"], 1)
                    act.wait_ge(s["evac"], 2)

                @block.vector
                def _(dve):
                    c = Chain(dve, s["vec"])
                    dve.wait_ge(s["copied"], 1)
                    if rotate_norm:
                        c.step(dve.tensor_reduce(sm, grp(QK), AX.X, ALU.add))
                        c.step(dve.tensor_scalar(sm, sm, 1.0 / HD, None, ALU.mult))
                        c.step(dve.tensor_tensor(grp(QK), grp(QK), wide(sm), ALU.subtract))
                        c.step(dve.tensor_tensor(A, QK, QK, ALU.mult))
                        c.step(dve.tensor_reduce(va, grp(A), AX.X, ALU.add))
                        c.step(dve.tensor_scalar(va, va, 1.0 / HD, 1e-6, ALU.mult, ALU.add))
                        dve.wait_ge(s["rooted"], 1)
                        c.step(dve.reciprocal(rs, rs))
                        c.step(dve.tensor_tensor(grp(QK), grp(QK), wide(rs), ALU.mult))
                        four = QK.rearrange("p (t n h e) -> p t n h e", t=TILES, n=2, e=HD)
                        for name, op in (("L0a_gamma", ALU.mult), ("L0a_beta", ALU.add)):
                            for n in range(2):
                                r = row(name)[:, n * HD:(n + 1) * HD].unsqueeze(1).unsqueeze(1)\
                                    .broadcast_to([P, TILES, HEADS, HD])
                                c.mark(dve.tensor_tensor(four[:, :, n], four[:, :, n], r, op))
                            c.join()
                    rc = cst("rope_c").unsqueeze(1).broadcast_to([P, G, HD])
                    h4 = HD // 2
                    c.mark(dve.tensor_tensor(grp(A), grp(QK), rc, ALU.mult))
                    for x in range(2):
                        sn = cst("rope_s")[:, x * h4:(x + 1) * h4].unsqueeze(1).broadcast_to([P, G, h4])
                        c.mark(dve.tensor_tensor(grp(B)[:, :, x * h4:(x + 1) * h4],
                                                 grp(QK)[:, :, (1 - x) * h4:(2 - x) * h4], sn, ALU.mult))
                    c.join()
                    dve.tensor_tensor(QK, A, B, ALU.add).then_inc(s["ready"], 1)

        KM = [BIG[1][:, t * 512:(t + 1) * 512].rearrange("p (r k) -> p r k", r=GROUPS) for t in range(TILES)]
        EX = [BIG[2][:, i * 1024:(i + 1) * 1024] for i in range(2)]
        PT = [BIG[2][:, 2048 + i * 1024:3072 + i * 1024].rearrange("p (j q) -> p j q", j=8) for i in range(2)]
        ON = [BIG[0][:, 2048 + i * 128:2176 + i * 128] for i in range(2)]
        OT = [BIG[0][:, 2304 + i * 128:2432 + i * 128] for i in range(2)]
        MX = [BIG[0][:, 2560 + i * 16:2576 + i * 16] for i in range(2)]
        RI = [BIG[0][:, 2592 + i * 16:2608 + i * 16] for i in range(2)]
        SB = BIG[0][:, 3072:3584].rearrange("p (t k) -> p t k", t=TILES)

        def attend(wo, dst, bias=None, bias_row=None):
            LAST = TILES + 4
            added_bias = bias in ("tgt", "src", "rel")
            with phase("masked", "scored", "vec", "subbed", "exped", "turned",
                       "copied", "mixed", "normed", "oturned", "ocopied", "projected", "added", "based",
                       "rowed", "spread") as (block, s):
                four = lambda a: a.rearrange("p (g r k) -> p g r k", g=4, r=4)

                @block.gpsimd
                def _(pool):
                    for t in range(TILES):
                        pool.tensor_tensor(
                            KM[t], KT[:, t * P:(t + 1) * P].unsqueeze(1).broadcast_to([P, GROUPS, P]),
                            cst("gmask").unsqueeze(2).broadcast_to([P, GROUPS, P]), ALU.mult).then_inc(s["masked"], 1)
                        if t == 1 and bias_row is not None:
                            pool.tensor_tensor(dst[:, :, :], dst[:, :, :],
                                               bias_row.unsqueeze(1).broadcast_to([P, TILES, P]), ALU.add)\
                                .then_inc(s["based"], 1)

                @block.tensor
                def _(pe):
                    if bias == "src":
                        pe.matmul(PS[:, 7, :], cst("two")[0:2, :], SRC[:, :, :], start=True, stop=True)\
                          .then_inc(s["rowed"], 1)

                    def scores(t):
                        pe.wait_ge(s["masked"], t + 1)
                        if t > 0:
                            pe.wait_ge(s["subbed"], t)
                        for g in range(4):
                            if bias in ("causal", "strict"):
                                m = (causalb if bias == "causal" else strictb)[:, :]
                                pe.matmul(PS[:, g, 0:256].rearrange("p (r k) -> p r k", r=4), identb[:, :],
                                          m.unsqueeze(1).broadcast_to([P, 4, SEQ]), start=True, stop=False)
                        for b in range(PER):
                            q = slice(b * SEQ, (b + 1) * SEQ)
                            for g in range(4):
                                rows = slice(32 * g, 32 * g + 32)
                                mm = pe.matmul(PS[q, g, 0:256].rearrange("p (r k) -> p r k", r=4),
                                               QT[rows, t * P + b * SEQ:t * P + (b + 1) * SEQ], KM[t][rows, :, q],
                                               start=bias is None or added_bias, stop=True)
                        mm.then_inc(s["scored"], 1)

                    def turn_probs(t):
                        pe.wait_ge(s["exped"], t + 1)
                        if t > 0:
                            pe.wait_ge(s["copied"], t)
                        for j in range(8):
                            mm = pe.transpose(PS[:, 4 + j // 4, (j % 4) * P:(j % 4 + 1) * P],
                                              EX[t % 2][:, j * P:(j + 1) * P], ident)
                        mm.then_inc(s["turned"], 1)

                    def mix(t):
                        pe.wait_ge(s["copied"], t + 1)
                        if t > 0:
                            pe.wait_ge(s["normed"], t)
                        for b in range(PER):
                            q = slice(b * SEQ, (b + 1) * SEQ)
                            for j in range(8):
                                mm = pe.matmul(PS[q, 6, 2 * SLOT * j:2 * SLOT * (j + 1)], PT[t % 2][:, j, q],
                                               VD[:, PER * t + b, 2 * j:2 * j + 2, :], start=True, stop=True)
                        mm.then_inc(s["mixed"], 1)

                    def turn_out(t):
                        pe.wait_ge(s["normed"], t + 1)
                        if t > 0:
                            pe.wait_ge(s["added"], t)
                        elif bias == "src":
                            pe.wait_ge(s["spread"], 1)
                        pe.transpose(PS[:, 7, 0:P], ON[t % 2], ident).then_inc(s["oturned"], 1)

                    def project_out(t):
                        pe.wait_ge(s["ocopied"], t + 1)
                        pe.matmul(PS[:, 7, P:2 * P], OT[t % 2], wo, start=True, stop=True).then_inc(s["projected"], 1)

                    for step in range(LAST):
                        for stage, lag in ((scores, 0), (project_out, 4), (turn_probs, 1), (mix, 2), (turn_out, 3)):
                            if 0 <= step - lag < TILES:
                                stage(step - lag)

                @block.vector
                def _(dve):
                    c = Chain(dve, s["vec"])
                    if bias == "src":
                        dve.wait_ge(s["rowed"], 1)
                        dve.tensor_copy(SB, PS[:, 7, :].rearrange("p (t k) -> p t k", t=TILES)).then_inc(s["spread"], 1)
                        dve.wait_ge(s["spread"], 1)

                    def shift(t):
                        S = PS[:, 0:4, 0:256].rearrange("p g (r k) -> p g r k", r=4)
                        E = four(EX[t % 2])
                        dve.wait_ge(s["scored"], t + 1)
                        if t > 1:
                            dve.wait_ge(s["turned"], t - 1)
                        m = MX[t % 2].rearrange("p (g r) -> p g r", g=4)
                        if added_bias:
                            if bias == "rel":
                                a = REL.rearrange("p (g r) k -> p g r k", g=4)
                            else:
                                a = w("c_tgt_bias") if bias == "tgt" else SB[:, t, :]
                                a = a.unsqueeze(1).unsqueeze(1).broadcast_to([P, 4, 4, SEQ])
                            c.step(dve.tensor_tensor(E, S, a, ALU.add))
                            S = E
                        c.step(dve.tensor_reduce(m, S, AX.X, ALU.max))
                        dve.tensor_tensor(E, S, m.unsqueeze(3).broadcast_to([P, 4, 4, SEQ]), ALU.subtract)\
                            .then_inc(s["subbed"], 1)

                    def add(t):
                        dve.wait_ge(s["projected"], t + 1)
                        dve.tensor_tensor(dst[:, t, :], dst[:, t, :], PS[:, 7, P:2 * P], ALU.add).then_inc(s["added"], 1)

                    def norm(t):
                        dve.wait_ge(s["mixed"], t + 1)
                        if t > 1:
                            dve.wait_ge(s["oturned"], t - 1)
                        O = PS[:, 6, 0:HEADS * SLOT].rearrange("p (h e) -> p h e", h=HEADS)
                        c.step(dve.reciprocal(RI[t % 2], O[:, :, HD]))
                        if bias == "strict":
                            c.step(dve.tensor_scalar(RI[t % 2], RI[t % 2], cst("notfirst"), None, ALU.mult))
                        dve.tensor_tensor(ON[t % 2].rearrange("p (h e) -> p h e", h=HEADS), O[:, :, 0:HD],
                                          RI[t % 2].unsqueeze(2).broadcast_to([P, HEADS, HD]), ALU.mult)\
                            .then_inc(s["normed"], 1)

                    for step in range(LAST):
                        for stage, lag in ((shift, 0), (add, 4), (norm, 2)):
                            if 0 <= step - lag < TILES:
                                if stage is add and step == lag and bias_row is not None:
                                    dve.wait_ge(s["based"], 1)
                                stage(step - lag)
                    dve.wait_ge(s["added"], TILES)

                @block.scalar
                def _(act):
                    def copy_probs(t):
                        act.wait_ge(s["turned"], t + 1)
                        if t > 1:
                            act.wait_ge(s["mixed"], t - 1)
                        act.activation(PT[t % 2].rearrange("p (a b) q -> p a (b q)", a=2), PS[:, 4:6, :], ACT.Copy)\
                            .then_inc(s["copied"], 1)

                    def exponent(t):
                        act.wait_ge(s["subbed"], t + 1)
                        act.activation(EX[t % 2], EX[t % 2], ACT.Exp).then_inc(s["exped"], 1)

                    def copy_out(t):
                        act.wait_ge(s["oturned"], t + 1)
                        if t > 1:
                            act.wait_ge(s["projected"], t - 1)
                        act.activation(OT[t % 2], PS[:, 7, 0:P], ACT.Copy).then_inc(s["ocopied"], 1)

                    for step in range(LAST):
                        for stage, lag in ((copy_probs, 1), (exponent, 0), (copy_out, 3)):
                            if 0 <= step - lag < TILES:
                                stage(step - lag)

        def turn(src, dstT):
            with phase("turned", "copied") as (block, s):
                @block.tensor
                def _(pe):
                    for t in range(TILES):
                        pe.transpose(PS[:, t // 4, (t % 4) * P:(t % 4 + 1) * P], src[:, t, :], ident)\
                          .then_inc(s["turned"], 1)

                @block.scalar
                def _(act):
                    for h in range(2):
                        act.wait_ge(s["turned"], 4 * h + 4)
                        act.activation(dstT[:, h * HALF:(h + 1) * HALF], PS[:, h, :], ACT.Copy).then_inc(s["copied"], 1)
                    act.wait_ge(s["copied"], 2)

        GATE = sb("GATE", [P, TILES, 64])

        def route(srcT, wg, E, K, kind, capacity):
            V = E + 8 - K
            n = TILES * E
            cut = lambda i, m: BIG[0][:, i * 512:i * 512 + TILES * m].rearrange("p (t e) -> p t e", t=TILES)
            LG, SCORE, MASK, PROB, TOP = cut(0, E), cut(1, E), cut(2, E), cut(3, E), cut(4, 8)
            VAL = BIG[1][:, 0:TILES * V].rearrange("p (t e) -> p t e", t=TILES)
            REP = BIG[1][:, 1024:1024 + TILES * V].rearrange("p (t e) -> p t e", t=TILES)
            RED = BIG[1][:, 2048:2048 + TILES]
            MASKB = BIG[1][:, 2304:2304 + n // 2].bitcast(BF16).rearrange("p (t e) -> p t e", t=TILES)
            WM = BIG[2][0:16, 0:TOK]
            WR = BIG[2][0:16, TOK:2 * TOK]
            KEPT = BIG[2][0:16, 2 * TOK:3 * TOK]
            W8 = BIG[2][0:16, 3 * TOK:3 * TOK + 8]
            TAKEN, LEAST = -3.2e38, NEVER
            wide = lambda a: a.unsqueeze(2).broadcast_to([P, TILES, E])
            logits = PS[:, 0, 0:n].rearrange("p (t e) -> p t e", t=TILES)
            before = PS[:, 1, 0:n].rearrange("p (t e) -> p t e", t=TILES)
            rounds = capacity // 8
            with phase("logits", "scored", "vec", "masked", "counted", "ranked", "turned", "kept", "back") as (block, s):
                @block.tensor
                def _(pe):
                    for t in range(TILES):
                        pe.matmul(logits[:, t, :], srcT[:, t * P:(t + 1) * P], wg, start=True, stop=True)\
                          .then_inc(s["logits"], 1)
                    pe.wait_ge(s["masked"], 1)
                    if kind != "logit":
                        for t in range(TILES):
                            for b in range(t + 1):
                                mm = pe.matmul(before[:, t, :], (upperb if b == t else onesb)[:, :], MASKB[:, b, :],
                                               start=b == 0, stop=b == t)
                        mm.then_inc(s["counted"], 1)
                    else:
                        for t in range(TILES):
                            mm = pe.transpose(PS[0:16, 2 + t // 4, (t % 4) * P:(t % 4 + 1) * P], PROB[:, t, :], ident)
                        mm.then_inc(s["turned"], 1)
                        pe.wait_ge(s["kept"], 1)
                        for t in range(TILES):
                            mm = pe.transpose(before[:, t, :], KEPT[:, t * P:(t + 1) * P], ident[0:16, 0:16])
                        mm.then_inc(s["back"], 1)

                @block.scalar
                def _(act):
                    if kind == "sigmoid":
                        act.wait_ge(s["logits"], TILES)
                        act.activation(SCORE, logits, ACT.Sigmoid).then_inc(s["scored"], 1)
                    else:
                        act.wait_ge(s["vec"], 3)
                        act.activation(SCORE, SCORE, ACT.Exp).then_inc(s["scored"], 1)

                @block.vector
                def _(dve):
                    c = Chain(dve, s["vec"])
                    if kind != "sigmoid":
                        dve.wait_ge(s["logits"], TILES)
                        c.mark(dve.tensor_copy(LG, logits))
                        c.step(dve.tensor_reduce(RED, logits, AX.X, ALU.max))
                        c.step(dve.tensor_tensor(SCORE, LG, wide(RED), ALU.subtract))
                    dve.wait_ge(s["scored"], 1)
                    if kind != "sigmoid":
                        c.step(dve.tensor_reduce(RED, SCORE, AX.X, ALU.add))
                        c.step(dve.reciprocal(RED, RED))
                        c.step(dve.tensor_tensor(SCORE, SCORE, wide(RED), ALU.mult))
                    c.mark(dve.memset(VAL[:, :, E:V], NEVER))
                    if kind == "softmax":
                        c.step(dve.tensor_copy(VAL[:, :, 0:E], SCORE))
                    else:
                        b = row("L0f_bias" if kind == "sigmoid" else "L2f_b")
                        c.step(dve.tensor_tensor(VAL[:, :, 0:E], SCORE,
                                                 b.unsqueeze(1).broadcast_to([P, TILES, E]), ALU.add))
                    for t in range(TILES):
                        c.mark(dve.max(TOP[:, t, :], VAL[:, t, :]))
                    c.join()
                    c.step(dve.memset(TOP[:, :, K:8], NEVER))
                    for t in range(TILES):
                        c.mark(dve.match_replace(REP[:, t, :], TOP[:, t, :], VAL[:, t, :], -2.0e38))
                    c.join()
                    c.step(dve.tensor_tensor(MASK, REP[:, :, 0:E], VAL[:, :, 0:E], ALU.not_equal))
                    if kind == "logit":
                        c.step(dve.tensor_tensor(PROB, LG, MASK, ALU.mult))
                        c.step(dve.tensor_scalar(SCORE, MASK, -NEVER, NEVER, ALU.mult, ALU.add))
                        c.mark(dve.tensor_tensor(PROB, PROB, SCORE, ALU.add))
                        c.join()
                        dve.sem_inc(s["masked"], 1)
                        dve.wait_ge(s["turned"], 1)
                        c.mark(dve.tensor_copy(WM, PS[0:16, 2:4, :].rearrange("p a b -> p (a b)")))
                        c.step(dve.tensor_copy(WR, PS[0:16, 2:4, :].rearrange("p a b -> p (a b)")))
                        for r in range(rounds):
                            c.step(dve.max(W8, WR))
                            c.step(dve.match_replace(WR, W8, WR, TAKEN))
                        c.mark(dve.tensor_tensor(KEPT, WR, WM, ALU.not_equal))
                        c.join()
                        dve.sem_inc(s["kept"], 1)
                        dve.wait_ge(s["back"], 1)
                        c.step(dve.tensor_tensor(MASK, MASK, before, ALU.mult))
                        c.mark(dve.tensor_tensor(GATE[:, :, 0:E], LG, MASK, ALU.mult))
                        c.mark(dve.memset(GATE[:, :, E:E + 2], 0.5))
                        c.join()
                        return
                    dve.tensor_copy(MASKB, MASK).then_inc(s["masked"], 1)
                    if kind == "sigmoid":
                        c.step(dve.tensor_tensor(PROB, SCORE, MASK, ALU.mult))
                        c.step(dve.tensor_reduce(RED, PROB, AX.X, ALU.add))
                        c.step(dve.tensor_scalar(RED, RED, 1e-20, None, ALU.add))
                        c.step(dve.reciprocal(RED, RED))
                        c.step(dve.tensor_tensor(PROB, PROB, wide(RED), ALU.mult))
                    else:
                        c.step(dve.tensor_tensor(PROB, SCORE, MASK, ALU.mult))
                    dve.wait_ge(s["counted"], 1)
                    c.step(dve.scalar_tensor_tensor(out=GATE[:, :, 0:E], in0=before, scalar=float(capacity), in1=PROB,
                                                    op0=ALU.is_lt, op1=ALU.mult))

        def experts(srcT, names, units, chunks, func, bias, dst):
            n = chunks * P
            W1 = [BIG[0][:, u * 512:u * 512 + n] for u in range(2)]
            W3 = [BIG[0][:, 1024 + u * 512:1024 + u * 512 + n] for u in range(2)]
            W2 = [BIG[0][:, 2048 + u * 512:2048 + u * 512 + n] for u in range(2)]
            HID = [[BIG[2 + u][:, c * TOK:(c + 1) * TOK] for c in range(chunks)] for u in range(2)]
            gated = len(names) == 3
            STEPS = 4
            assert chunks * (2 if gated else 1) == STEPS

            def where(step, u):
                c = step // 2 if gated else step
                o = HID[u][c].rearrange("p (a b) -> p a b", a=2)
                return c, (o[:, step % 2, :] if gated else o)

            def pipeline(eng, hidden, output):
                def both(h, y):
                    for n in range(2):
                        if h is not None:
                            for step in (2 * n, 2 * n + 1):
                                hidden(*h, step)
                        if y is not None:
                            output(*y, n)
                both((0, 0), None)
                with eng.Fori(0, units // 2 - 1) as i:
                    both((i, 1), (i, 0))
                    both((i + 1, 0), (i, 1))
                last = units // 2 - 1
                both((last, 1), (last, 0))
                both(None, (last, 1))

            with phase("w1_even", "w1_odd", "w2_even", "w2_odd", "made", "acted", "ready", "ymade", "added") as (block, s):
                w1_loaded, w2_loaded = (s["w1_even"], s["w1_odd"]), (s["w2_even"], s["w2_odd"])

                @block.sync
                def _(sp):
                    with sp.Fori(0, units // 2) as i:
                        for u in range(2):
                            e = i * 2 + u
                            sp.wait_ge(s["made"], e * STEPS + STEPS)
                            sp.dma_start(W1[u], d[names[0]][:, bass.ts(e, n)]).then_inc(w1_loaded[u], 16)
                            if gated:
                                sp.dma_start(W3[u], d[names[1]][:, bass.ts(e, n)]).then_inc(w1_loaded[u], 16)
                            sp.wait_ge(s["ymade"], e * 2 + 2)
                            sp.dma_start(W2[u], d[names[-1]][:, bass.ts(e, n)]).then_inc(w2_loaded[u], 16)

                @block.tensor
                def _(pe):
                    pe.sem_inc(s["made"], 2 * STEPS)
                    pe.sem_inc(s["ymade"], 4)

                    def hidden(i, u, step):
                        e = i * 2 + u
                        c, _ = where(step, u)
                        if step == 0:
                            pe.wait_ge(w1_loaded[u], (i + 1) * (16 * (len(names) - 1)))
                        pe.wait_ge(s["ready"], e * STEPS + (step + 1))
                        wc = slice(c * P, (c + 1) * P)
                        for k in range(2):
                            W, h = ((W1, W3)[k], step % 2) if gated else (W1, k)
                            mm = pe.matmul(PS[:, 2 * (step % 2) + k, :], W[u][:, wc], srcT[:, h * HALF:(h + 1) * HALF],
                                           start=True, stop=True)
                        mm.then_inc(s["made"], 1)

                    def output(i, u, h):
                        e = i * 2 + u
                        if h == 0:
                            pe.wait_ge(s["ready"], e * STEPS + (STEPS + 2))
                            pe.wait_ge(w2_loaded[u], i * 16 + 16)
                        pe.wait_ge(s["added"], e * 2 + (h + 1))
                        for t in range(4 * h, 4 * h + 4):
                            for c in range(chunks):
                                mm = pe.matmul(PS[:, 4 + h, (t % 4) * P:(t % 4 + 1) * P],
                                               HID[u][c][:, t * P:(t + 1) * P], W2[u][:, c * P:(c + 1) * P],
                                               start=c == 0, stop=c == chunks - 1)
                        mm.then_inc(s["ymade"], 1)

                    pipeline(pe, hidden, output)

                @block.scalar
                def _(act):
                    if not gated:
                        act.sem_inc(s["ready"], 2)
                    with act.Fori(0, units // 2) as i:
                        for u in range(2):
                            e = i * 2 + u
                            act.wait_ge(s["ymade"], e * 2 + 2)
                            for step in range(STEPS):
                                act.wait_ge(s["made"], e * STEPS + (2 * STEPS + step + 1))
                                c, o = where(step, u)
                                b = 2 * (step % 2)
                                src = PS[:, b, :] if gated else PS[:, b:b + 2, :]
                                if bias is None:
                                    ins = act.activation(o, src, func)
                                else:
                                    ins = act.activation(o, src, func, bias=bias[:, bass.ds(e * chunks + c, 1)])
                                ins.then_inc(s["acted"] if gated else s["ready"], 1)

                @block.vector
                def _(dve):
                    dve.sem_inc(s["added"], 2)
                    if gated:
                        dve.sem_inc(s["ready"], 2)

                    def hidden(i, u, step):
                        if gated:
                            dve.wait_ge(s["acted"], (i * 2 + u) * STEPS + (step + 1))
                            _, o = where(step, u)
                            dve.tensor_tensor(o, o, PS[:, 2 * (step % 2) + 1, :], ALU.mult).then_inc(s["ready"], 1)

                    def output(i, u, h):
                        e = i * 2 + u
                        dve.wait_ge(s["ymade"], e * 2 + (h + 5))
                        dve.wait_ge(s["added"], e * 2 + (h + 1))
                        for t in range(4 * h, 4 * h + 4):
                            ins = dve.scalar_tensor_tensor(
                                out=dst[:, t, :], in0=PS[:, 4 + h, (t % 4) * P:(t % 4 + 1) * P],
                                scalar=GATE[:, t, bass.ds(e, 1)], in1=dst[:, t, :], op0=ALU.mult, op1=ALU.add)
                        ins.then_inc(s["added"], 1)

                    pipeline(dve, hidden, output)
                    dve.wait_ge(s["added"], 2 * units + 2)

        def l1_ffn():
            normalize(X, XR, HT, 1e-5)
            normalize(XR, XN, HT, 1e-5, w("c_ln1_g"), w("c_ln1_b"))
            token_qk(w("L1f_q"), w("L1f_k"), False, HD ** -0.5)
            project([], (HT, w("L1f_v"), None))
            attend(w("L1f_o"), XR, "causal")
            normalize(XR, XN, HT, 1e-5, w("c_ln2_g"), w("c_ln2_b"))
            route(HT, w("L1f_gate"), 8, 2, "softmax", 256)
            B2 = BIG[1][0:8, 0:P]
            GT = BIG[1][0:8, P:P + TOK]
            with phase("loaded", "turned", "copied", "made", "vec") as (block, s):
                @block.sync
                def _(sp):
                    sp.dma_start(B2, d["L1f_b2"]).then_inc(s["loaded"], 16)

                @block.tensor
                def _(pe):
                    for t in range(TILES):
                        mm = pe.transpose(PS[0:8, t // 4, (t % 4) * P:(t % 4 + 1) * P], GATE[:, t, 0:8], ident)
                    mm.then_inc(s["turned"], 1)
                    pe.wait_ge(s["loaded"], 16)
                    pe.wait_ge(s["copied"], 1)
                    for t in range(TILES):
                        mm = pe.matmul(PS[:, 2 + t // 4, (t % 4) * P:(t % 4 + 1) * P], GT[:, t * P:(t + 1) * P], B2,
                                       start=True, stop=True)
                    mm.then_inc(s["made"], 1)

                @block.scalar
                def _(act):
                    act.wait_ge(s["turned"], 1)
                    act.activation(GT.rearrange("p (a b) -> p a b", a=2), PS[0:8, 0:2, :], ACT.Copy).then_inc(s["copied"], 1)

                @block.vector
                def _(dve):
                    c = Chain(dve, s["vec"])
                    both = lambda a: a[:, :, :].rearrange("p (a t) f -> p a (t f)", a=2)
                    c.step(dve.tensor_tensor(both(X), both(X), both(XR), ALU.add))
                    dve.wait_ge(s["made"], 1)
                    c.step(dve.tensor_tensor(both(X), both(X), PS[:, 2:4, :], ALU.add))
            experts(HT, ("L1f_w1", "L1f_w2"), 8, 4, ACT.Gelu, w("c_L1f_b1"), X)

        def l2_ffn():
            normalize(X, XN, HT, 1e-5)
            route(HT, w("L2f_gate"), 16, 2, "logit", 160)
            experts(HT, ("L2f_w1", "L2f_w3", "L2f_w2"), 18, 2, ACT.Silu, None, X)

        def l2_attn():
            normalize(X, XN, HT, 1e-5)
            project([(QT, w("L2a_w"), HT, w("c_L2a_b"), 1.0)])
            WW = BIG[0][:, 0:TOK]
            SM = BIG[0][:, TOK:TOK + TILES]
            ww = WW.rearrange("p (t k) -> p t k", t=TILES)
            two = lambda a: a.rearrange("p (a b) -> p a b", a=2)
            quad = lambda a: a.unsqueeze(1).broadcast_to([P, 4, P])
            with phase("scored", "vec", "exped", "weighed", "mixed") as (block, s):
                @block.tensor
                def _(pe):
                    for t in range(TILES):
                        cols = slice(t * P, (t + 1) * P)
                        mm = pe.matmul(PS[:, t // 4, (t % 4) * P:(t % 4 + 1) * P], HT[:, cols], QT[:, cols],
                                       start=True, stop=True)
                    mm.then_inc(s["scored"], 1)
                    pe.wait_ge(s["weighed"], 1)
                    for t in range(TILES):
                        pe.matmul(PS[:, 2 + t // 4, (t % 4) * P:(t % 4 + 1) * P], ww[:, t, :], XN[:, t, :],
                                  start=True, stop=True)
                        mm = pe.matmul(PS[:, 4, t:t + 1], ww[:, t, :], cst("ones")[:, 0:1], start=True, stop=True)
                    mm.then_inc(s["mixed"], 1)

                @block.scalar
                def _(act):
                    act.wait_ge(s["vec"], 2)
                    act.activation(WW, WW, ACT.Tanh).then_inc(s["exped"], 1)
                    act.wait_ge(s["exped"], 1)
                    act.activation(WW, WW, ACT.Exp).then_inc(s["exped"], 1)

                @block.vector
                def _(dve):
                    c = Chain(dve, s["vec"])
                    dve.wait_ge(s["scored"], 1)
                    for h in range(2):
                        c.mark(dve.tensor_tensor(ww[:, 4 * h:4 * h + 4, :], PS[:, h, :].rearrange("p (t k) -> p t k", t=4),
                                                 quad(cst("lw")), ALU.mult))
                    dve.wait_ge(s["exped"], 2)
                    dve.tensor_tensor(ww, ww, cst("off").unsqueeze(1).broadcast_to([P, TILES, P]), ALU.mult)\
                        .then_inc(s["weighed"], 1)
                    dve.wait_ge(s["mixed"], 1)
                    c.step(dve.tensor_scalar(SM, PS[:, 4, 0:TILES], 1e-7, None, ALU.add))
                    c.step(dve.reciprocal(SM, SM))
                    for t in range(TILES):
                        c.mark(dve.scalar_tensor_tensor(out=X[:, t, :], in0=PS[:, 2 + t // 4, (t % 4) * P:(t % 4 + 1) * P],
                                                        scalar=SM[:, t:t + 1], in1=X[:, t, :], op0=ALU.mult, op1=ALU.add))
                    c.join()

        def l0_ffn():
            normalize(X, XN, HT, 1e-5)
            route(HT, w("L0f_router"), 64, 6, "sigmoid", 48)
            G2 = BIG[1][:, 0:TOK]
            GA = BIG[0][:, 3072:3584].bitcast(BF16)
            GB = BIG[0][:, 3584:4096].bitcast(BF16)
            GF = BIG[1][:, TOK:2 * TOK]
            R1 = BIG[1][:, 2 * TOK:3 * TOK]
            T3 = BIG[1][:, 3 * TOK:3 * TOK + 512].bitcast(BF16)
            T1 = BIG[1][:, 3 * TOK + 512:4 * TOK].bitcast(BF16)
            with phase("vec", "turned", "pool") as (block, s):
                @block.tensor
                def _(pe):
                    pe.wait_ge(s["vec"], 2)
                    for t in range(TILES):
                        mm = pe.transpose(PS[:, t // 4, (t % 4) * P:(t % 4 + 1) * P], G2[:, t * P:(t + 1) * P], ident)
                    mm.then_inc(s["turned"], 1)

                @block.vector
                def _(dve):
                    c = Chain(dve, s["vec"])
                    g2 = G2.rearrange("p (t c e) -> p t c e", t=TILES, c=2)
                    for k in range(2):
                        c.mark(dve.tensor_copy(g2[:, :, k, :], GATE[:, :, :]))
                    dve.wait_ge(s["turned"], 1)
                    c.step(dve.tensor_copy(GF, PS[:, 0:2, :].rearrange("p a b -> p (a b)")))
                    c.step(dve.tensor_copy(T1, GF))
                    c.step(dve.tensor_tensor(R1, GF, T1, ALU.subtract))
                    c.step(dve.tensor_copy(T3, R1))
                    c.step(dve.tensor_tensor(R1, R1, T3, ALU.subtract))
                    c.mark(dve.memset(GB[:, :], 0.0))
                    c.mark(dve.tensor_copy(GA[0:64, :], T1[0:64, :]))
                    c.mark(dve.tensor_copy(GA[64:128, :], T3[64:128, :]))
                    c.join()
                    c.step(dve.tensor_copy(GB[0:64, :], R1[0:64, :]))

            n = 4 * P
            W1 = [BIG[0][:, u * 512:u * 512 + n] for u in range(2)]
            W2 = [BIG[0][:, 1024 + u * 512:1024 + u * 512 + n] for u in range(2)]
            HID = [BIG[2][:, c * TOK:(c + 1) * TOK] for c in range(2)]
            SH = [BIG[3][:, c * TOK:(c + 1) * TOK] for c in range(2)]
            YT = BIG[1][:, 0:TOK]
            halves = lambda a: a.rearrange("p (a b) -> p a b", a=2)
            with phase("loaded_even", "loaded_odd", "made", "hfree", "acted", "picked", "ready", "ymade", "shared",
                       "copied", "turned", "added") as (block, s):
                loaded = (s["loaded_even"], s["loaded_odd"])
                UNITS, PAIRS = 8, 4

                @block.sync
                def _(sp):
                    with sp.Fori(0, UNITS // 2) as i:
                        for u in range(2):
                            e = i * 2 + u
                            sp.wait_ge(s["ymade"], e * 8 + 8)
                            for name, buf in (("L0f_w1", W1), ("L0f_w2", W2)):
                                sp.dma_start(buf[u], d[name][:, bass.ts(e, n)]).then_inc(loaded[u], 16)

                @block.tensor
                def _(pe):
                    pe.sem_inc(s["ymade"], 16)
                    for c in range(2):
                        for h in range(2):
                            mm = pe.matmul(PS[:, 2 * c + h, :], w("L0f_sw1")[:, c * P:(c + 1) * P],
                                           HT[:, h * HALF:(h + 1) * HALF], start=True, stop=True)
                        mm.then_inc(s["made"], 1)
                    pe.wait_ge(s["shared"], 2)
                    for c in range(2):
                        for h in range(2):
                            pe.matmul(PS[:, 6 + h, :], w("L0f_sw2")[:, c * P:(c + 1) * P], SH[c][:, h * HALF:(h + 1) * HALF],
                                      start=c == 0, stop=False, skip_group_check=True)

                    def outputs(u, c):
                        for h in range(2):
                            pe.matmul(PS[:, 6 + h, :], W2[u][:, c * P:(c + 1) * P], HID[c % 2][:, h * HALF:(h + 1) * HALF],
                                      start=False, stop=False, skip_group_check=True).then_inc(s["ymade"], 1)

                    def step(i, u, c, before=None):
                        pair = (i * 2 + u) * PAIRS + c
                        if c == 0:
                            pe.wait_ge(loaded[u], i * 32 + 32)
                        pe.wait_ge(s["hfree"], pair + 1)
                        for h in range(2):
                            mm = pe.matmul(PS[:, 2 * (c % 2) + h, :], W1[u][:, c * P:(c + 1) * P],
                                           HT[:, h * HALF:(h + 1) * HALF], start=True, stop=True)
                        mm.then_inc(s["made"], 1)
                        pe.wait_ge(s["ready"], pair + 1)
                        if before is not None:
                            outputs(*before)
                        for h in range(2):
                            for k, G in enumerate((GA, GB)):
                                mm = pe.matmul(PS[:, 4 + h, :], pickb[:, bass.ts(pair, P)],
                                               G[:, h * HALF:(h + 1) * HALF], start=k == 0, stop=k == 1)
                        mm.then_inc(s["picked"], 1)

                    step(0, 0, 0)
                    order = [(u, c) for u in range(2) for c in range(PAIRS)]
                    with pe.Fori(0, UNITS // 2 - 1) as i:
                        for a, b in zip(order, order[1:]):
                            step(i, *b, before=a)
                        step(i + 1, 0, 0, before=order[-1])
                    for a, b in zip(order, order[1:]):
                        step(UNITS // 2 - 1, *b, before=a)
                    pe.wait_ge(s["ready"], UNITS * PAIRS + 1)
                    outputs(*order[-1])
                    for t in range(TILES):
                        if t == 0:
                            pe.wait_ge(s["copied"], 1)
                        mm = pe.transpose(PS[:, t // 4, (t % 4) * P:(t % 4 + 1) * P], YT[:, t * P:(t + 1) * P], ident)
                    mm.then_inc(s["turned"], 1)

                @block.scalar
                def _(act):
                    for c in range(2):
                        act.wait_ge(s["made"], c + 1)
                        act.activation(halves(SH[c]), PS[:, 2 * c:2 * c + 2, :], ACT.Gelu_apprx_tanh).then_inc(s["shared"], 1)
                        act.wait_ge(s["shared"], c + 1)
                        act.sem_inc(s["hfree"], 1)
                    with act.Fori(0, 16) as i:
                        for c in range(2):
                            pair = i * 2 + c
                            act.wait_ge(s["made"], pair + 3)
                            act.wait_ge(s["ymade"], pair * 2 + 14)
                            act.activation(halves(HID[c]), PS[:, 2 * c:2 * c + 2, :], ACT.Gelu_apprx_tanh)\
                               .then_inc(s["acted"], 1)
                            act.wait_ge(s["acted"], pair + 1)
                            act.sem_inc(s["hfree"], 1)

                @block.vector
                def _(dve):
                    dve.sem_inc(s["ready"], 1)
                    with dve.Fori(0, 16) as i:
                        for c in range(2):
                            pair = i * 2 + c
                            dve.wait_ge(s["acted"], pair + 1)
                            dve.wait_ge(s["picked"], pair + 1)
                            dve.tensor_tensor(halves(HID[c]), halves(HID[c]), PS[:, 4:6, :], ALU.mult)\
                                .then_inc(s["ready"], 1)
                    dve.wait_ge(s["ymade"], 16 + 2 * 32)
                    dve.tensor_copy(halves(YT), PS[:, 6:8, :]).then_inc(s["copied"], 1)
                    dve.wait_ge(s["turned"], 1)
                    x = X[:, :, :].rearrange("p (a t) f -> p a (t f)", a=2)
                    dve.tensor_tensor(x, x, PS[:, 0:2, :], ALU.add).then_inc(s["added"], 1)
                    dve.wait_ge(s["added"], 1)

        def l1_xattn():
            normalize(X, XN, HT, 1e-5)
            with phase("zeroed") as (block, s):
                @block.gpsimd
                def _(pool):
                    pool.memset(XR[:, :, :], 0.0).then_inc(s["zeroed"], 1)
            project([(QT, w("L1xs_q"), HT, w("c_L1xs_bq"), HD ** -0.5), (KT, w("L1xs_k"), CT, w("c_L1xs_bk"), 1.0)],
                    (CT, w("L1xs_v"), row("L1xs_v")))
            attend(w("L1xs_o"), XR, "src", row("L1xs_o"))
            project([(QT, w("L1xt_q"), HT, w("c_L1xt_bq"), HD ** -0.5), (KT, w("L1xt_k"), HT, w("c_L1xt_bk"), 1.0)],
                    (HT, w("L1xt_v"), row("L1xt_v")))
            attend(w("L1xt_o"), XR, "tgt", row("L1xt_o"))
            turn(XR, QT)
            N = 4 * BATCH
            GX = BIG[0]
            gx = GX[:, :].rearrange("p (s g b) -> p g b s", s=SEQ, g=4)
            HS = BIG[1][:, 0:(SEQ + 1) * BATCH]
            G = [BIG[1][:, 1280 + i * 128:1280 + i * 128 + 5 * BATCH] for i in range(2)]
            T = BIG[1][:, 1600:1600 + 2 * BATCH]
            TC = BIG[1][:, 1664:1664 + BATCH]
            WH = BIG[1][:, 2048:2560]
            with phase("made", "evac", "zeroed") as (block, s):
                @block.tensor
                def _(pe):
                    for g in range(4):
                        for h in range(2):
                            cols = slice(h * HALF, (h + 1) * HALF)
                            o = PS[:, 2 * g + h, :]
                            pe.matmul(o, w("L1x_wx")[:, g * P:(g + 1) * P], HT[:, cols], start=True, stop=False)
                            pe.matmul(o, w("L1x_wc")[:, g * P:(g + 1) * P], QT[:, cols], start=False, stop=True)\
                              .then_inc(s["made"], 1)

                @block.gpsimd
                def _(pool):
                    pool.memset(HS[:, 0:BATCH], 0.0).then_inc(s["zeroed"], 1)
                    pool.memset(G[0][:, 64:80], 0.0).then_inc(s["zeroed"], 1)
                    pool.tensor_scalar(WH[:, 0:3 * P], w("L1x_wh")[:, 0:3 * P], 0.5, None, ALU.mult).then_inc(s["zeroed"], 1)
                    pool.tensor_copy(WH[:, 3 * P:4 * P], w("L1x_wh")[:, 3 * P:4 * P]).then_inc(s["zeroed"], 1)

                @block.vector
                def _(dve):
                    for g in range(4):
                        for h in range(2):
                            dve.wait_ge(s["made"], 2 * g + h + 1)
                            dve.tensor_scalar(gx[:, g, h * 8:h * 8 + 8, :],
                                              PS[:, 2 * g + h, :].rearrange("p (b s) -> p b s", b=8),
                                              w("c_L1x_lstm_b")[:, g:g + 1], 2.0 if g == 3 else 1.0, ALU.add, ALU.mult)\
                                .then_inc(s["evac"], 1)
                    dve.wait_ge(s["evac"], 8)

            with phase("gates", "gfree", "acted", "cell", "tanhed", "hidden") as (block, s):
                @block.tensor
                def _(pe):
                    with pe.Fori(0, SEQ // 2) as i:
                        for u in range(2):
                            step = i * 2 + u
                            o = PS[:, u, 0:N]
                            pe.wait_ge(s["gfree"], step + 1)
                            pe.matmul(o, ident, GX[:, bass.ts(step, N)], start=True, stop=False, skip_group_check=True)
                            pe.wait_ge(s["hidden"], step + 1)
                            for g in range(4):
                                mm = pe.matmul(o[:, g * BATCH:(g + 1) * BATCH], WH[:, g * P:(g + 1) * P],
                                               HS[:, bass.ts(step, BATCH)], start=False, stop=g == 3,
                                               skip_group_check=True)
                            mm.then_inc(s["gates"], 1)

                @block.scalar
                def _(act):
                    act.sem_inc(s["gfree"], 2)
                    with act.Fori(0, SEQ // 2) as i:
                        for u in range(2):
                            step = i * 2 + u
                            act.wait_ge(s["gates"], step + 1)
                            act.activation(G[u][:, 0:64], PS[:, u, 0:64], ACT.Tanh, scale=0.5).then_inc(s["acted"], 1)
                            act.wait_ge(s["acted"], step + 1)
                            act.sem_inc(s["gfree"], 1)
                            act.wait_ge(s["cell"], step * 2 + 2)
                            act.activation(TC, G[1 - u][:, 64:80], ACT.Tanh, scale=0.5).then_inc(s["tanhed"], 1)

                @block.vector
                def _(dve):
                    dve.sem_inc(s["hidden"], 1)
                    with dve.Fori(0, SEQ // 2) as i:
                        for u in range(2):
                            step = i * 2 + u
                            dve.wait_ge(s["acted"], step + 1)
                            dve.scalar_tensor_tensor(out=T, in0=G[u][:, 0:32], scalar=1.0, in1=G[u][:, 48:80],
                                                     op0=ALU.add, op1=ALU.mult).then_inc(s["cell"], 1)
                            dve.wait_ge(s["cell"], step * 2 + 1)
                            dve.scalar_tensor_tensor(out=G[1 - u][:, 64:80], in0=T[:, BATCH:2 * BATCH], scalar=0.5,
                                                     in1=T[:, 0:BATCH], op0=ALU.mult, op1=ALU.add)\
                                .then_inc(s["cell"], 1)
                            dve.wait_ge(s["tanhed"], step + 1)
                            dve.scalar_tensor_tensor(out=HS[:, bass.ts(step + 1, BATCH)], in0=G[u][:, 32:48],
                                                     scalar=1.0, in1=TC, op0=ALU.add, op1=ALU.mult)\
                                .then_inc(s["hidden"], 1)

            RR = [BIG[2][:, c * TOK:(c + 1) * TOK] for c in range(4)]
            with phase("made", "evac", "ymade", "based", "added") as (block, s):
                @block.tensor
                def _(pe):
                    for c in range(4):
                        if c >= 2:
                            pe.wait_ge(s["evac"], 2 * (c - 1))
                        for h in range(2):
                            pe.matmul(PS[:, 2 * (c % 2) + h, :], w("L1x_w1")[:, c * P:(c + 1) * P],
                                      HS[:, BATCH + h * HALF:BATCH + (h + 1) * HALF], start=True, stop=True)\
                              .then_inc(s["made"], 1)
                    pe.wait_ge(s["evac"], 8)
                    for t in range(TILES):
                        for c in range(4):
                            mm = pe.matmul(PS[:, 4 + t // 4, (t % 4) * P:(t % 4 + 1) * P], RR[c][:, t * P:(t + 1) * P],
                                           w("L1x_w2")[:, c * P:(c + 1) * P], start=c == 0, stop=c == 3)
                        mm.then_inc(s["ymade"], 1)

                @block.scalar
                def _(act):
                    for c in range(4):
                        for h in range(2):
                            act.wait_ge(s["made"], 2 * c + h + 1)
                            o = RR[c].rearrange("p (b s) -> p s b", b=BATCH)[:, h * 32:(h + 1) * 32, :]
                            act.activation(o, PS[:, 2 * (c % 2) + h, :].rearrange("p (s b) -> p s b", b=BATCH), ACT.Relu,
                                           scale=0.5, bias=w("c_L1x_b1")[:, c:c + 1]).then_inc(s["evac"], 1)

                @block.gpsimd
                def _(pool):
                    pool.tensor_tensor(X[:, :, :], X[:, :, :],
                                       row("L1x_b2").unsqueeze(1).broadcast_to([P, TILES, P]), ALU.add)\
                        .then_inc(s["based"], 1)

                @block.vector
                def _(dve):
                    dve.wait_ge(s["based"], 1)
                    for h in range(2):
                        dve.wait_ge(s["ymade"], 4 * h + 4)
                        x = X[:, 4 * h:4 * h + 4, :].rearrange("p t f -> p (t f)")
                        dve.tensor_tensor(x, x, PS[:, 4 + h, :], ALU.add).then_inc(s["added"], 1)
                    dve.wait_ge(s["added"], 2)


        EXTRA = sb("EXTRA", [P, 6 * TOK])
        tiles = lambda a: a.rearrange("p (t f) -> p t f", t=TILES)
        halves = lambda a: a.rearrange("p (a b) -> p a b", a=2)
        half = lambda a, g: a[:, g * HALF:(g + 1) * HALF]
        square = lambda g, t: PS[:, g, (t % 4) * P:(t % 4 + 1) * P]
        each = lambda a: a.unsqueeze(1).broadcast_to([P, TILES, P])

        def delta_heads():
            H, LV = 8, 5
            W4 = BIG[3]
            part = lambda buf, i: buf[:, i * TOK:(i + 1) * TOK]
            SIL = BIG[0][:, :].rearrange("p (t n f) -> p t n f", t=TILES, n=4)
            QH, KH, KBH, GAM = (part(BIG[1], i) for i in range(4))
            LT, AT, XX, XXT = (part(BIG[2], i) for i in range(4))
            WO, YY, CC, KB, GU, GW = (part(EXTRA, i) for i in range(6))
            OO = XN[:, :, :]
            small = CS[:, C_AT["pick"][0]:C_AT["pick"][0] + 4096]
            steps = lambda a: a.rearrange("p (t h) -> p t h", t=TILES)
            LG = small[:, 0:128].rearrange("p (t n) -> p t n", t=TILES)
            BETA, G, Z, E1, NA, U, SP, T1 = (steps(small[:, 128 + 64 * i:192 + 64 * i]) for i in range(8))
            RS = small[:, 700:716].rearrange("p (t n) -> p t n", t=TILES)
            RO = small[:, 720:728]
            EA = small[:, 730:738]
            SQ2 = small[:, 1024:3072].rearrange("p (t n f) -> p t n f", t=TILES, n=2)
            with phase("loaded", "made", "vec", "acted") as (block, s):
                @block.sync
                def _(sp):
                    sp.dma_start(W4[:, :], d["L3a_w"]).then_inc(s["loaded"], 16)
                    sp.dma_start(WO, d["L3a_wo"]).then_inc(s["loaded"], 16)
                    sp.wait_ge(s["loaded"], 32)

                @block.tensor
                def _(pe):
                    for t in range(TILES):
                        a = W_AT["L3a_b"][0]
                        mm = pe.matmul(PS[:, 0, t * 16:(t + 1) * 16], HT[:, t * P:(t + 1) * P], WT[:, a:a + 16],
                                       start=True, stop=True)
                    mm.then_inc(s["made"], 1)

                @block.scalar
                def _(act):
                    act.wait_ge(s["made"], 1)
                    act.activation(LG, PS[:, 0, 0:128].rearrange("p (t n) -> p t n", t=TILES), ACT.Copy).then_inc(s["acted"], 1)
                    act.wait_ge(s["acted"], 1)
                    act.activation(BETA, LG[:, :, 0:8], ACT.Sigmoid).then_inc(s["acted"], 1)
                    act.activation(EA, row("L3a_Alog"), ACT.Exp).then_inc(s["acted"], 1)
                    act.wait_ge(s["vec"], 2)
                    act.activation(E1, NA, ACT.Exp).then_inc(s["acted"], 1)
                    act.wait_ge(s["vec"], 3)
                    act.activation(SP, U, ACT.Ln).then_inc(s["acted"], 1)

                @block.vector
                def _(dve):
                    c = Chain(dve, s["vec"])
                    wide = lambda a: a.unsqueeze(1).broadcast_to([P, TILES, 8])
                    dve.wait_ge(s["acted"], 1)
                    c.step(dve.tensor_tensor(Z, LG[:, :, 8:16], wide(row("L3a_dt")), ALU.add))
                    c.step(dve.scalar_tensor_tensor(out=NA, in0=Z, scalar=-1.0, in1=Z, op0=ALU.mult, op1=ALU.min))
                    dve.wait_ge(s["acted"], 4)
                    c.step(dve.tensor_scalar(U, E1, 1.0, None, ALU.add))
                    dve.wait_ge(s["acted"], 5)
                    c.step(dve.tensor_scalar(T1, E1, -0.25, 1.0 / 3.0, ALU.mult, ALU.add))
                    c.step(dve.tensor_tensor(T1, T1, E1, ALU.mult))
                    c.step(dve.tensor_scalar(T1, T1, -0.5, None, ALU.add))
                    c.step(dve.tensor_tensor(T1, T1, E1, ALU.mult))
                    c.step(dve.scalar_tensor_tensor(out=T1, in0=T1, scalar=1.0, in1=E1, op0=ALU.add, op1=ALU.mult))
                    c.step(dve.tensor_scalar(U, E1, 0.01, None, ALU.is_lt))
                    c.step(dve.tensor_tensor(T1, T1, U, ALU.mult))
                    c.step(dve.tensor_scalar(U, U, -1.0, 1.0, ALU.mult, ALU.add))
                    c.step(dve.tensor_tensor(SP, SP, U, ALU.mult))
                    c.step(dve.tensor_tensor(SP, SP, T1, ALU.add))
                    c.step(dve.scalar_tensor_tensor(out=SP, in0=Z, scalar=0.0, in1=SP, op0=ALU.max, op1=ALU.add))
                    c.step(dve.scalar_tensor_tensor(out=G, in0=SP, scalar=-1.0, in1=wide(EA), op0=ALU.mult, op1=ALU.mult))

            per = dict(projected=8, silued=8, squared=1, summed=1, qk_rooted=1, q_scaled=1, k_scaled=1, beta_k=1,
                       spread=1, pairs=1, decayed=1, turned=3, tcopied=3, inner=2, lower=1, level0=1, other=1,
                       xcopied=1, attn=1, masked=LV, ymade=8, ycopied=8, x_corrected=6, t_corrected=8, x_subbed=6,
                       t_subbed=8, zmade=2, zcopied=2, wmade=2, wcopied=2, vmade=2, delta=2, mixed=2, gated=1,
                       mean_squares=1, o_rooted=1, onormed=2, oturned=2, ocopied=2, out=2, added=2)
            FRONT, REST = 4, 20
            with phase(*per, "vec") as (block, s):
                def waits(eng, h):
                    return lambda name, n: eng.wait_ge(s[name], h * per[name] + n)

                def all_heads(eng, head):
                    with eng.Fori(0, H - 1) as h:
                        head(h, True)
                    head(H - 1, False)

                @block.tensor
                def _(pe):
                    def project_tile(h, t):
                        if t >= 2:
                            waits(pe, h)("silued", t - 1)
                        pe.matmul(PS[:, 6 + t % 2, :], HT[:, t * P:(t + 1) * P], W4[:, bass.ts(h, HALF)],
                                  start=True, stop=True).then_inc(s["projected"], 1)

                    def pairs(h):
                        waits(pe, h)("spread", 1)
                        waits(pe, h)("silued", TILES)
                        for g in range(2):
                            mm = pe.matmul(PS[:, 6 + g, :], cst("tri_str"), half(GU, g), start=True, stop=True)
                        mm.then_inc(s["pairs"], 1)

                    def head(h, more):
                        at = waits(pe, h)
                        for n, ready in enumerate(("q_scaled", "k_scaled", "beta_k")):
                            at(ready, 1)
                            for t in range(TILES):
                                src = tiles(KB)[:, t, :] if n == 2 else SIL[:, t, n, :]
                                mm = pe.transpose(square(2 * n + t // 4, t), src, ident)
                            mm.then_inc(s["turned"], 1)
                        at("tcopied", 3)
                        at("decayed", 1)
                        for bank, o in ((6, KBH), (0, QH)):
                            for t in range(TILES):
                                c = slice(t * P, (t + 1) * P)
                                mm = pe.matmul(square(bank + t // 4, t), KH[:, c], o[:, c], start=True, stop=True)
                            mm.then_inc(s["inner"], 1)
                        at("level0", 1)
                        for t in range(TILES):
                            mm = pe.transpose(square(2 + t // 4, t), tiles(XXT)[:, t, :], ident)
                        mm.then_inc(s["other"], 1)
                        at("xcopied", 1)
                        at("attn", 1)
                        for l in range(1, LV):
                            at("masked", l)
                            for g in range(2):
                                if l > 1:
                                    at("x_subbed", 2 * (l - 2) + g + 1)
                                for t in range(4 * g, 4 * g + 4):
                                    mm = pe.matmul(square(g, t), tiles(CC)[:, t, :], tiles(XX)[:, t, :],
                                                   start=True, stop=True)
                                mm.then_inc(s["ymade"], 1)
                            for g in range(2):
                                at("ycopied", 2 * (l - 1) + g + 1)
                                if l > 1:
                                    at("t_subbed", 2 * (l - 2) + g + 1)
                                if l < LV - 1:
                                    for t in range(4 * g, 4 * g + 4):
                                        mm = pe.matmul(square(2 + g, t), tiles(XXT)[:, t, :], tiles(YY)[:, t, :],
                                                       start=True, stop=True)
                                    mm.then_inc(s["x_corrected"], 1)
                                for t in range(4 * g, 4 * g + 4):
                                    mm = pe.matmul(square(4 + g, t), tiles(YY)[:, t, :], tiles(XXT)[:, t, :],
                                                   start=True, stop=True)
                                mm.then_inc(s["t_corrected"], 1)
                        for g in range(2):
                            at("t_subbed", 2 * (LV - 2) + g + 1)
                            for t in range(4 * g, 4 * g + 4):
                                mm = pe.matmul(square(g, t), tiles(XXT)[:, t, :], SIL[:, t, 2, :], start=True, stop=True)
                            mm.then_inc(s["zmade"], 1)
                        if more:
                            project_tile(h + 1, 0)
                            project_tile(h + 1, 1)
                        at("masked", LV)
                        for g in range(2):
                            at("zcopied", g + 1)
                            for t in range(4 * g, 4 * g + 4):
                                mm = pe.matmul(square(2 + g, t), tiles(CC)[:, t, :], tiles(YY)[:, t, :],
                                               start=True, stop=True)
                            mm.then_inc(s["wmade"], 1)
                        if more:
                            project_tile(h + 1, 2)
                            project_tile(h + 1, 3)
                        for g in range(2):
                            at("wcopied", g + 1)
                            for t in range(4 * g, 4 * g + 4):
                                mm = pe.matmul(square(4 + g, t), tiles(XXT)[:, t, :], tiles(XX)[:, t, :],
                                               start=True, stop=True)
                            mm.then_inc(s["vmade"], 1)
                        if more:
                            project_tile(h + 1, 4)
                            project_tile(h + 1, 5)
                        for g in range(2):
                            at("delta", g + 1)
                            for t in range(4 * g, 4 * g + 4):
                                mm = pe.matmul(square(g, t), tiles(AT)[:, t, :], tiles(YY)[:, t, :], start=True, stop=True)
                            mm.then_inc(s["mixed"], 1)
                        if more:
                            project_tile(h + 1, 6)
                            project_tile(h + 1, 7)
                            pairs(h + 1)
                        for g in range(2):
                            at("onormed", g + 1)
                            for t in range(4 * g, 4 * g + 4):
                                mm = pe.transpose(square(2 + g, t), OO[:, t, :], ident)
                            mm.then_inc(s["oturned"], 1)
                        for g in range(2):
                            at("ocopied", g + 1)
                            for t in range(4 * g, 4 * g + 4):
                                mm = pe.matmul(square(4 + g, t), tiles(XX)[:, t, :], WO[:, bass.ts(h, P)],
                                               start=True, stop=True)
                            mm.then_inc(s["out"], 1)

                    for t in range(TILES):
                        project_tile(0, t)
                    pairs(0)
                    all_heads(pe, head)

                @block.scalar
                def _(act):
                    def silu(h, first, last):
                        for t in range(first, last):
                            waits(act, h)("projected", t + 1)
                            act.activation(BIG[0][:, t * HALF:(t + 1) * HALF], PS[:, 6 + t % 2, :], ACT.Silu)\
                                .then_inc(s["silued"], 1)

                    def root_and_decay(h):
                        waits(act, h)("summed", 1)
                        act.activation(RS, RS, ACT.Sqrt).then_inc(s["qk_rooted"], 1)
                        waits(act, h)("pairs", 1)
                        act.activation(halves(GAM), PS[:, 6:8, :], ACT.Exp).then_inc(s["decayed"], 1)

                    def head(h, more):
                        at = waits(act, h)
                        for n, o in enumerate((QH, KH, KBH)):
                            at("turned", n + 1)
                            act.activation(halves(o), PS[:, 2 * n:2 * n + 2, :], ACT.Copy).then_inc(s["tcopied"], 1)
                        at("other", 1)
                        act.activation(halves(XX), PS[:, 2:4, :], ACT.Copy).then_inc(s["xcopied"], 1)
                        for l in range(1, LV):
                            for g in range(2):
                                at("ymade", 2 * (l - 1) + g + 1)
                                act.activation(half(YY, g), PS[:, g, :], ACT.Copy).then_inc(s["ycopied"], 1)
                        for g in range(2):
                            at("zmade", g + 1)
                            act.activation(half(YY, g), PS[:, g, :], ACT.Copy).then_inc(s["zcopied"], 1)
                        if more:
                            silu(h + 1, 0, 2)
                        for g in range(2):
                            at("wmade", g + 1)
                            act.activation(half(XX, g), PS[:, 2 + g, :], ACT.Copy).then_inc(s["wcopied"], 1)
                        if more:
                            silu(h + 1, 2, TILES)
                        at("mean_squares", 1)
                        act.activation(RO, RO, ACT.Sqrt).then_inc(s["o_rooted"], 1)
                        for g in range(2):
                            at("oturned", g + 1)
                            act.activation(half(XX, g), PS[:, 2 + g, :], ACT.Copy).then_inc(s["ocopied"], 1)
                        if more:
                            root_and_decay(h + 1)

                    silu(0, 0, TILES)
                    root_and_decay(0)
                    all_heads(act, head)

                @block.gpsimd
                def _(pool):
                    def spread(h):
                        pool.tensor_tensor(tiles(GU), each(cst("tri_inc")),
                                           G[:, :, bass.ds(h, 1)].broadcast_to([P, TILES, P]), ALU.mult)\
                            .then_inc(s["spread"], 1)

                    def square_low(h):
                        waits(pool, h)("silued", 4)
                        pool.tensor_tensor(SQ2[:, 0:4], SIL[:, 0:4, 0:2, :], SIL[:, 0:4, 0:2, :], ALU.mult)\
                            .then_inc(s["squared"], 1)

                    def gates(h):
                        waits(pool, h)("silued", TILES)
                        pool.tensor_tensor(tiles(GW), SIL[:, :, 3, :], each(row("L3a_norm")), ALU.mult)\
                            .then_inc(s["gated"], 1)

                    def head(h, more):
                        at = waits(pool, h)
                        for l in range(1, LV + 1):
                            if l == 1:
                                at("lower", 1)
                            else:
                                at("ymade", 2 * (l - 1))
                            a = C_AT["level"][0] + l * P
                            pool.tensor_tensor(tiles(CC), tiles(LT), each(CS[:, a:a + P]), ALU.mult)\
                                .then_inc(s["masked"], 1)
                        if more:
                            spread(h + 1)
                            square_low(h + 1)
                            at("onormed", 2)
                            gates(h + 1)

                    spread(0)
                    square_low(0)
                    gates(0)
                    all_heads(pool, head)

                @block.vector
                def _(dve):
                    col = lambda a: a.broadcast_to([P, TILES, P])
                    beta = lambda h: col(BETA[:, :, bass.ds(h, 1)])

                    def square_high(h):
                        waits(dve, h)("silued", TILES)
                        return dve.tensor_tensor(SQ2[:, 4:8], SIL[:, 4:8, 0:2, :], SIL[:, 4:8, 0:2, :], ALU.mult)

                    def scale(h, c):
                        at = waits(dve, h)
                        at("squared", 1)
                        c.step(dve.tensor_reduce(RS, SQ2, AX.X, ALU.add))
                        dve.tensor_scalar(RS, RS, 1e-6, None, ALU.add).then_inc(s["summed"], 1)
                        at("qk_rooted", 1)
                        c.step(dve.reciprocal(RS, RS))
                        dve.scalar_tensor_tensor(out=SIL[:, :, 0, :], in0=SIL[:, :, 0, :], scalar=float(P) ** -0.5,
                                                 in1=col(RS[:, :, 0:1]), op0=ALU.mult, op1=ALU.mult)\
                            .then_inc(s["q_scaled"], 1)
                        dve.tensor_tensor(SIL[:, :, 1, :], SIL[:, :, 1, :], col(RS[:, :, 1:2]), ALU.mult)\
                            .then_inc(s["k_scaled"], 1)

                    def weigh(h, c):
                        waits(dve, h)("k_scaled", 1)
                        dve.tensor_tensor(tiles(KB), SIL[:, :, 1, :], beta(h), ALU.mult).then_inc(s["beta_k"], 1)
                        c.mark(dve.tensor_tensor(SIL[:, :, 2, :], SIL[:, :, 2, :], beta(h), ALU.mult))

                    def head(h, more):
                        at = waits(dve, h)
                        c = Chain(dve, s["vec"], h * (FRONT + REST) + FRONT)
                        at("decayed", 1)
                        c.step(dve.tensor_tensor(tiles(GAM), tiles(GAM), each(cst("tri_inc")), ALU.mult))
                        at("inner", 1)
                        dve.tensor_tensor(halves(LT), PS[:, 6:8, :], halves(GAM), ALU.mult).then_inc(s["lower"], 1)
                        at("lower", 1)
                        a = C_AT["level"][0]
                        c.step(dve.tensor_tensor(tiles(XXT), tiles(LT), each(CS[:, a:a + P]), ALU.mult))
                        dve.tensor_tensor(tiles(XXT), each(ident), tiles(XXT), ALU.subtract).then_inc(s["level0"], 1)
                        at("inner", 2)
                        dve.tensor_tensor(halves(AT), PS[:, 0:2, :], halves(GAM), ALU.mult).then_inc(s["attn"], 1)
                        at("level0", 1)
                        at("xcopied", 1)
                        for l in range(1, LV):
                            for g in range(2):
                                n = 2 * (l - 1) + g
                                if l < LV - 1:
                                    at("x_corrected", n + 1)
                                    if l > 1:
                                        at("x_subbed", n - 1)
                                    dve.tensor_tensor(half(XX, g), half(XX, g), PS[:, 2 + g, :], ALU.subtract)\
                                        .then_inc(s["x_subbed"], 1)
                                at("t_corrected", n + 1)
                                if l > 1:
                                    at("t_subbed", n - 1)
                                dve.tensor_tensor(half(XXT, g), half(XXT, g), PS[:, 4 + g, :], ALU.subtract)\
                                    .then_inc(s["t_subbed"], 1)
                        for g in range(2):
                            at("vmade", g + 1)
                            dve.tensor_tensor(half(YY, g), half(YY, g), PS[:, 4 + g, :], ALU.subtract).then_inc(s["delta"], 1)
                        for g in range(2):
                            at("mixed", g + 1)
                            for t in range(4 * g, 4 * g + 4):
                                c.mark(dve.bn_stats(stats[:, t, :], square(t // 4, t)))
                        c.join()
                        dve.memset(small[:, 740:741], 0.0)
                        for t in range(TILES):
                            c.mark(dve.bn_aggr(mv[:, t, :], stats[:, t, :]))
                        c.join()
                        c.step(dve.tensor_tensor(RO, mv[:, :, 0], mv[:, :, 0], ALU.mult))
                        dve.scalar_tensor_tensor(out=RO, in0=mv[:, :, 1], scalar=1e-6, in1=RO,
                                                 op0=ALU.add, op1=ALU.add).then_inc(s["mean_squares"], 1)
                        if more:
                            c.mark(square_high(h + 1))
                        at("o_rooted", 1)
                        c.step(dve.reciprocal(RO, RO))
                        at("gated", 1)
                        for g in range(2):
                            for t in range(4 * g, 4 * g + 4):
                                ins = dve.scalar_tensor_tensor(out=OO[:, t, :], in0=square(g, t), scalar=RO[:, t:t + 1],
                                                               in1=tiles(GW)[:, t, :], op0=ALU.mult, op1=ALU.mult)
                            ins.then_inc(s["onormed"], 1)
                        if more:
                            scale(h + 1, c)
                        for g in range(2):
                            at("out", g + 1)
                            x = XR[:, 4 * g:4 * g + 4, :].rearrange("p t f -> p (t f)")
                            dve.tensor_tensor(x, x, PS[:, 4 + g, :], ALU.add).then_inc(s["added"], 1)
                        at("added", 2)
                        if more:
                            weigh(h + 1, c)
                        assert c.n == REST + (FRONT if more else 0)

                    c = Chain(dve, s["vec"])
                    c.step(square_high(0))
                    scale(0, c)
                    weigh(0, c)
                    assert c.n == FRONT
                    all_heads(dve, head)

        def l3_attn():
            normalize(X, XR, HT, 1e-5)
            normalize(XR, XN, HT, 1e-6, rms=True)
            delta_heads()
            normalize(XR, XN, HT, 1e-6, rms=True)
            RR = [BIG[2][:, c * TOK:(c + 1) * TOK] for c in range(4)]
            with phase("made", "rect", "evac", "ymade", "added") as (block, s):
                @block.tensor
                def _(pe):
                    for c in range(4):
                        if c >= 2:
                            pe.wait_ge(s["rect"], c - 1)
                        for h in range(2):
                            mm = pe.matmul(PS[:, 2 * (c % 2) + h, :], w("L3a_fc")[:, c * P:(c + 1) * P],
                                           HT[:, h * HALF:(h + 1) * HALF], start=True, stop=True)
                        mm.then_inc(s["made"], 1)
                    pe.wait_ge(s["evac"], 4)
                    for t in range(TILES):
                        for c in range(4):
                            mm = pe.matmul(square(4 + t // 4, t), RR[c][:, t * P:(t + 1) * P],
                                           w("L3a_proj")[:, c * P:(c + 1) * P], start=c == 0, stop=c == 3)
                        mm.then_inc(s["ymade"], 1)

                @block.scalar
                def _(act):
                    for c in range(4):
                        act.wait_ge(s["made"], c + 1)
                        act.activation(halves(RR[c]), PS[:, 2 * (c % 2):2 * (c % 2) + 2, :], ACT.Relu).then_inc(s["rect"], 1)
                        act.wait_ge(s["rect"], c + 1)
                        act.activation(RR[c], RR[c], ACT.Square).then_inc(s["evac"], 1)

                @block.vector
                def _(dve):
                    whole = lambda a: a[:, :, :].rearrange("p t f -> p (t f)")
                    dve.tensor_tensor(whole(X), whole(X), whole(XR), ALU.add).then_inc(s["added"], 1)
                    dve.wait_ge(s["added"], 1)
                    for h in range(2):
                        dve.wait_ge(s["ymade"], 4 * h + 4)
                        x = X[:, 4 * h:4 * h + 4, :].rearrange("p t f -> p (t f)")
                        dve.tensor_tensor(x, x, PS[:, 4 + h, :], ALU.add).then_inc(s["added"], 1)
                    dve.wait_ge(s["added"], 3)

        def l3_ffn():
            normalize(X, XN, HT, 1e-5)
            QMAX = 32767.0
            inv_q = float(np.float32(1.0) / np.float32(QMAX))
            WQ = EXTRA[:, 0:1152].rearrange("p (n i) -> p n i", n=36)
            WF = EXTRA[:, 0:1152]
            WD = EXTRA[:, 1152:2304]
            MB = EXTRA[:, 2304:2340]
            IB = EXTRA[:, 2340:2376]
            SC = EXTRA[:, 2400:2412]
            UP, GT, SG = BIG[0][:, 0:3072], BIG[1][:, 0:3072], BIG[2][:, 0:3072]
            blocks32 = lambda a: a.unsqueeze(2).broadcast_to([P, 36, 32])
            with phase("vec", "turned", "copied") as (block, s):
                @block.vector
                def _(dve):
                    c = Chain(dve, s["vec"])
                    src = w("L3f_w").rearrange("p (n i) -> p n i", n=36)
                    c.step(dve.tensor_reduce(MB, src, AX.X, ALU.max, apply_absolute_value=True))
                    c.step(dve.tensor_scalar(MB, MB, float(np.float32(1) / np.float32(7)), 1e-12, ALU.mult, ALU.max))
                    c.step(dve.reciprocal(IB, MB))
                    c.step(dve.tensor_tensor(WQ, src, blocks32(IB), ALU.mult))
                    c.step(dve.tensor_scalar(WF, WF, MAGIC, None, ALU.add))
                    c.step(dve.tensor_scalar(WF, WF, -MAGIC, -8.0, ALU.add, ALU.max))
                    c.step(dve.tensor_scalar(WF, WF, 7.0, None, ALU.min))
                    c.step(dve.tensor_tensor(WQ, WQ, blocks32(MB), ALU.mult))

                @block.tensor
                def _(pe):
                    pe.wait_ge(s["vec"], 8)
                    for n in range(9):
                        mm = pe.transpose(PS[:, n // 4, (n % 4) * P:(n % 4 + 1) * P], WF[:, n * P:(n + 1) * P], ident)
                    mm.then_inc(s["turned"], 1)

                @block.scalar
                def _(act):
                    act.wait_ge(s["turned"], 1)
                    act.activation(WD[:, 0:1024].rearrange("p (a b) -> p a b", a=2), PS[:, 0:2, :], ACT.Copy)\
                        .then_inc(s["copied"], 1)
                    act.activation(WD[:, 1024:1152], PS[:, 2, 0:P], ACT.Copy).then_inc(s["copied"], 1)

            def quantize(items, after=None):
                with phase("vec", "pooled") as (block, s):
                    @block.gpsimd
                    def _(pool):
                        pool.wait_ge(s["vec"], 1)
                        n = len(items)
                        a = items[0][2]
                        pool.partition_all_reduce(SC[:, 6:6 + n], SC[:, a:a + n], P, bass.bass_isa.ReduceOp.max)\
                            .then_inc(s["pooled"], 1)

                    @block.vector
                    def _(dve):
                        c = Chain(dve, s["vec"])
                        n = len(items)
                        a = items[0][2]
                        for k, (src, dst, col) in enumerate(items):
                            ins = dve.tensor_reduce(SC[:, col:col + 1], src, AX.X, ALU.max, apply_absolute_value=True)
                            if k == n - 1:
                                c.mark(ins)
                        dve.wait_ge(s["pooled"], 1)
                        c.step(dve.tensor_scalar(SC[:, a:a + n], SC[:, 6:6 + n], inv_q, 1e-12, ALU.mult, ALU.max))
                        c.step(dve.reciprocal(SC[:, 8:8 + n], SC[:, a:a + n]))
                        for k, (src, dst, col) in enumerate(items):
                            c.step(dve.tensor_scalar(dst, src, SC[:, 8 + k:9 + k], MAGIC, ALU.mult, ALU.add))
                            c.step(dve.tensor_scalar(dst, dst, -MAGIC, -QMAX - 1.0, ALU.add, ALU.max))
                            c.step(dve.tensor_scalar(dst, dst, QMAX, SC[:, col:col + 1], ALU.min, ALU.mult))

            quantize([(HT[:, :], QT[:, :], 0)])
            with phase("made", "copied") as (block, s):
                @block.tensor
                def _(pe):
                    for n in range(6):
                        if n >= 4:
                            pe.wait_ge(s["copied"], n - 3)
                        for h in range(2):
                            mm = pe.matmul(PS[:, 2 * (n % 4) + h, :], WD[:, n * P:(n + 1) * P],
                                           QT[:, h * HALF:(h + 1) * HALF], start=True, stop=True)
                        mm.then_inc(s["made"], 1)

                @block.scalar
                def _(act):
                    for n in range(6):
                        act.wait_ge(s["made"], n + 1)
                        o = (GT if n < 3 else UP)[:, (n % 3) * TOK:(n % 3 + 1) * TOK]
                        act.activation(halves(o), PS[:, 2 * (n % 4):2 * (n % 4) + 2, :], ACT.Copy).then_inc(s["copied"], 1)
            quantize([(GT, GT, 0), (UP, UP, 1)])
            with phase("signed", "vec") as (block, s):
                @block.scalar
                def _(act):
                    act.activation(SG, GT, ACT.Sigmoid).then_inc(s["signed"], 1)

                @block.vector
                def _(dve):
                    c = Chain(dve, s["vec"])
                    dve.wait_ge(s["signed"], 1)
                    c.step(dve.tensor_scalar(SG, SG, 65536.0, MAGIC, ALU.mult, ALU.add))
                    c.step(dve.tensor_scalar(SG, SG, -MAGIC, 0.0, ALU.add, ALU.max))
                    c.step(dve.tensor_scalar(SG, SG, 65535.0, 1.0 / 65536.0, ALU.min, ALU.mult))
                    c.step(dve.tensor_tensor(GT, GT, SG, ALU.mult))
            quantize([(GT, GT, 0)])
            with phase("vec") as (block, s):
                @block.vector
                def _(dve):
                    dve.tensor_tensor(UP, UP, GT, ALU.mult).then_inc(s["vec"], 1)
            quantize([(UP, UP, 0)])
            with phase("ymade", "added") as (block, s):
                @block.tensor
                def _(pe):
                    for t in range(TILES):
                        for c in range(3):
                            mm = pe.matmul(square(t // 4, t), UP[:, c * TOK + t * P:c * TOK + (t + 1) * P],
                                           WD[:, (6 + c) * P:(7 + c) * P], start=c == 0, stop=c == 2)
                    mm.then_inc(s["ymade"], 1)

                @block.vector
                def _(dve):
                    dve.wait_ge(s["ymade"], 1)
                    x = X[:, :, :].rearrange("p (a t) f -> p a (t f)", a=2)
                    dve.tensor_tensor(x, x, PS[:, 0:2, :], ALU.add).then_inc(s["added"], 1)

        def store():
            with phase("stored") as (block, s):
                @block.sync
                def _(sp):
                    sp.dma_start(out, X[:, :, :]).then_inc(s["stored"], 16)
                    sp.wait_ge(s["stored"], 16)

        def l0_attn():
            normalize(X, XN, HT, 1e-5)
            qkv = w("L0a_qkv")
            token_qk(qkv[:, 0:P], qkv[:, P:2 * P], True, HD ** -0.5)
            project([], (HT, qkv[:, 2 * P:3 * P], None))
            attend(w("L0a_o"), X, None, row("L0a_o"))

        def l0_xattn():
            normalize(X, XN, HT, 1e-5)
            project([(QT, w("L0x_q"), HT, None, HD ** -0.5), (KT, w("L0x_k"), CT, None, 1.0)],
                    (CT, w("L0x_v"), None))
            with phase("rel") as (block, s):
                @block.sync
                def _(sp):
                    for b in range(PER):
                        sp.dma_start(REL[b * SEQ:(b + 1) * SEQ, :, :], d["rel"]).then_inc(s["rel"], 16)
                    sp.wait_ge(s["rel"], 32)
            attend(w("L0x_o"), X, "rel", row("L0x_o"))

        def l1_attn():
            normalize(X, XN, HT, 1e-5)
            project([(QT, w("L1a_q"), HT, None, w("c_L1a_scale")), (KT, w("L1a_k"), HT, None, 1.0)],
                    (HT, w("L1a_v"), None))
            attend(w("L1a_o"), X, "strict", row("L1a_o"))

        def l2_xattn():
            normalize(X, XN, HT, 1e-5)
            project([(QT, w("L2x_q"), HT, None, HD ** -0.5), (KT, w("L2x_k"), CT, None, 1.0)],
                    (CT, w("L2x_v"), None))
            attend(w("L2x_o"), X)

        def l3_xattn():
            normalize(X, XN, HT, 1e-5)
            project([(QT, w("L3x_q"), HT, w("c_L3x_bq"), HD ** -0.5), (KT, w("L3x_k"), CT, w("c_L3x_bk"), 1.0)],
                    (CT, w("L3x_v"), row("L3x_v")))
            attend(w("L3x_o"), X, None, row("L3x_o"))

        blocks = [l0_attn, l0_xattn, l0_ffn, l1_attn, l1_xattn, l1_ffn, l2_attn, l2_xattn, l2_ffn, l3_attn, l3_xattn, l3_ffn]
        for f in blocks[first:last]:
            f()
        store()
        nc.clear_and_free_semaphores(used.pop())


def pack(inputs):
    g = {k: np.asarray(v) for k, v in inputs.items()}
    W = {}
    W["L0a_qkv"] = g["L0_attn_w_qkv"].T
    W["L0a_o"] = g["L0_attn_w_proj"].T
    W["L0x_q"], W["L0x_k"], W["L0x_v"], W["L0x_o"] = (g["L0_xattn_" + n].T for n in ("wq", "wk", "wv", "fc_w"))
    W["L0f_router"] = g["L0_ffn_router_weight"].T
    W["L0f_sw1"] = g["L0_ffn_sw1"].T
    W["L0f_sw2"] = g["L0_ffn_sw2"].T.reshape(2, P, P).transpose(1, 0, 2)
    q3 = g["L1_attn_w_qkv"]
    W["L1a_q"], W["L1a_k"], W["L1a_v"] = q3[:, 0:P], q3[:, P:2 * P], q3[:, 2 * P:]
    W["L1a_o"] = g["L1_attn_w_out"]
    for a, b in (("L1xs_", "L1_xattn_src_w"), ("L1xt_", "L1_xattn_tgt_w")):
        for n in "qkvo":
            W[a + n] = g[b + n]
    lw = g["L1_xattn_lstm_w"].reshape(3, P, 4, P)[:, :, [0, 2, 3, 1], :]
    W["L1x_wx"], W["L1x_wc"], W["L1x_wh"] = lw[0], lw[1], lw[2]
    W["L1x_w1"] = g["L1_xattn_ffn_w1"]
    W["L1x_w2"] = g["L1_xattn_ffn_w2"].reshape(4, P, P).transpose(1, 0, 2)
    q3 = g["L1_ffn_Wqkv"].reshape(P, HEADS, 3, HD)
    W["L1f_q"], W["L1f_k"], W["L1f_v"] = q3[:, :, 0], q3[:, :, 1], q3[:, :, 2]
    W["L1f_o"], W["L1f_gate"] = g["L1_ffn_Wproj"], g["L1_ffn_Wgate"]
    W["L2a_w"] = g["L2_attn_W"]
    W["L2x_q"], W["L2x_k"], W["L2x_v"], W["L2x_o"] = (g["L2_xattn_w_" + n].T for n in "qkvo")
    W["L2f_gate"] = g["L2_ffn_gate_w"]
    W["L3a_b"], W["L3a_a"], W["L3a_fc"] = g["L3_attn_Wb"], g["L3_attn_Wa"], g["L3_attn_W_fc"]
    W["L3a_proj"] = g["L3_attn_W_proj"].reshape(4, P, P).transpose(1, 0, 2)
    W["L3x_q"], W["L3x_k"], W["L3x_v"], W["L3x_o"] = (g["L3_xattn_W" + n].T for n in "qkvo")
    W["L3f_w"] = np.concatenate([g["L3_ffn_w_gate"].reshape(3, P, P), g["L3_ffn_w_up"].reshape(3, P, P),
                                 g["L3_ffn_w_down"].reshape(P, 3, P).transpose(1, 0, 2)]).transpose(1, 0, 2)
    W["c_L1a_scale"] = np.repeat(g["L1_attn_scale"].reshape(-1), HD)
    for a, b in (("L1xs_b", "L1_xattn_src_b"), ("L1xt_b", "L1_xattn_tgt_b"), ("L3x_b", "L3_xattn_b")):
        for n in "qk":
            W["c_" + a + n] = g[b + n]
    W["c_L1x_lstm_b"] = g["L1_xattn_lstm_b"].reshape(4, P)[[0, 2, 3, 1]].T
    W["c_L1x_b1"] = g["L1_xattn_ffn_b1"].reshape(4, P).T
    for n in ("ln1_g", "ln1_b", "ln2_g", "ln2_b"):
        W["c_" + n] = g["L1_ffn_" + n]
    W["c_L1f_b1"] = g["L1_ffn_b1"].reshape(32, P).T
    W["c_L2a_b"] = g["L2_attn_b"]
    W["c_tgt_bias"] = np.concatenate([g["L1_xattn_tgt_bias"].reshape(SEQ, SEQ)] * 2)
    R = {"L0a_o": g["L0_attn_b_proj"], "L0a_gamma": np.concatenate([g["L0_attn_q_gamma"], g["L0_attn_k_gamma"]]),
         "L0a_beta": np.concatenate([g["L0_attn_q_beta"], g["L0_attn_k_beta"]]), "L0x_o": g["L0_xattn_fc_b"],
         "L0f_bias": g["L0_ffn_expert_bias"], "L1a_o": g["L1_attn_b_out"], "L1xs_v": g["L1_xattn_src_bv"],
         "L1xt_v": g["L1_xattn_tgt_bv"], "L1xs_o": g["L1_xattn_src_bo"], "L1xt_o": g["L1_xattn_tgt_bo"],
         "L1x_b2": g["L1_xattn_ffn_b2"], "L2f_b": g["L2_ffn_gate_b"], "L3a_Alog": g["L3_attn_A_log"],
         "L3a_dt": g["L3_attn_dt_bias"], "L3a_norm": g["L3_attn_o_norm_w"], "L3x_v": g["L3_xattn_bv"],
         "L3x_o": g["L3_xattn_bo"]}
    a = {}
    a["x"] = g["x"].reshape(TILES, P, P).transpose(1, 0, 2)
    a["ctxT"] = g["ctx_1024"].reshape(TOK, P).T
    a["weights"] = np.concatenate([W[n].reshape(P, m) for n, m in WEIGHTS], 1)
    a["rows"] = np.concatenate([R[n].reshape(1, m) for n, m in ROWS], 1)
    a["consts"] = shape_constants()
    a["src_bias"] = g["mask_Bx1x1xS2_ff0"].reshape(TILES, PER, SEQ).transpose(1, 0, 2)
    q, k = np.arange(SEQ)[:, None], np.arange(SEQ)[None, :]
    a["rel"] = g["L0_xattn_rel_table"][k - q + 255].transpose(0, 2, 1)
    a["L0f_w1"] = g["L0_ffn_w1"].transpose(1, 0, 2).reshape(P, 4096)
    a["L0f_w2"] = g["L0_ffn_w2"].reshape(32, P, P).transpose(1, 0, 2).reshape(P, 4096)
    a["L1f_w1"] = g["L1_ffn_W1"].transpose(1, 0, 2).reshape(P, 4096)
    a["L1f_w2"] = g["L1_ffn_W2"].reshape(32, P, P).transpose(1, 0, 2).reshape(P, 4096)
    a["L1f_b2"] = g["L1_ffn_b2"]
    both = lambda e, s: np.concatenate([g["L2_ffn_" + e], g["L2_ffn_" + s]])
    a["L2f_w1"] = both("ew1", "sw1").transpose(1, 0, 2).reshape(P, 18 * 256)
    a["L2f_w3"] = both("ew3", "sw3").transpose(1, 0, 2).reshape(P, 18 * 256)
    a["L2f_w2"] = both("ew2", "sw2").reshape(36, P, P).transpose(1, 0, 2).reshape(P, 36 * P)
    a["L3a_w"] = np.concatenate([g["L3_attn_W" + n].reshape(P, 8, 1, P) for n in "qkvg"], 2).reshape(P, 4096)
    a["L3a_wo"] = g["L3_attn_Wo"].reshape(8, P, P).transpose(1, 0, 2).reshape(P, 1024)
    return {k: np.ascontiguousarray(v) for k, v in a.items()}


def kernel(**inputs):
    import concourse.bacc as _bacc
    from concourse.bass_utils import run_bass_kernel_spmd as _run

    nc = _bacc.Bacc("TRN2", target_bir_lowering=False, num_devices=1)
    arrays = pack(inputs)
    d = {k: nc.dram_tensor(k + "_dram", v.shape, F32, kind="ExternalInput").ap() for k, v in arrays.items()}
    out = nc.dram_tensor("out_dram", (P, TILES, P), F32, kind="ExternalOutput").ap()
    decoder_kernel(nc, d, out)
    r = _run(nc, [{k + "_dram": v for k, v in arrays.items()}], core_ids=[0])
    return r.results[0]["out_dram"].transpose(1, 0, 2).reshape(BATCH, SEQ, P)
```

```python
from contextlib import ExitStack, contextmanager

import numpy as np
import concourse.bass as bass
from concourse import mybir

ALU = mybir.AluOpType
ACT = mybir.ActivationFunctionType
AX = mybir.AxisListType
F32 = mybir.dt.float32
BF16 = mybir.dt.bfloat16

P = 128
SEQ = 64
BATCH = 16
TOK = BATCH * SEQ
TILES = TOK // P
PER = P // SEQ
HEADS = 16
HD = P // HEADS
GROUPS = 4
HALF = 512
MAGIC = 12582912.0
NEVER = -3.0e38

WEIGHTS = [
    ("L0a_qkv", 384), ("L0a_o", 128), ("L0x_q", 128), ("L0x_k", 128), ("L0x_v", 128), ("L0x_o", 128),
    ("L0f_router", 64), ("L0f_sw1", 256), ("L0f_sw2", 256),
    ("L1a_q", 128), ("L1a_k", 128), ("L1a_v", 128), ("L1a_o", 128),
    ("L1xs_q", 128), ("L1xs_k", 128), ("L1xs_v", 128), ("L1xs_o", 128),
    ("L1xt_q", 128), ("L1xt_k", 128), ("L1xt_v", 128), ("L1xt_o", 128),
    ("L1x_wx", 512), ("L1x_wc", 512), ("L1x_wh", 512), ("L1x_w1", 512), ("L1x_w2", 512),
    ("L1f_q", 128), ("L1f_k", 128), ("L1f_v", 128), ("L1f_o", 128), ("L1f_gate", 8),
    ("L2a_w", 128), ("L2x_q", 128), ("L2x_k", 128), ("L2x_v", 128), ("L2x_o", 128), ("L2f_gate", 16),
    ("L3a_b", 8), ("L3a_a", 8), ("L3a_fc", 512), ("L3a_proj", 512),
    ("L3x_q", 128), ("L3x_k", 128), ("L3x_v", 128), ("L3x_o", 128),
    ("L3f_w", 1152),
    ("c_L1a_scale", 1), ("c_L1xs_bq", 1), ("c_L1xs_bk", 1), ("c_L1xt_bq", 1), ("c_L1xt_bk", 1),
    ("c_L1x_lstm_b", 4), ("c_L1x_b1", 4), ("c_ln1_g", 1), ("c_ln1_b", 1), ("c_ln2_g", 1), ("c_ln2_b", 1),
    ("c_L1f_b1", 32), ("c_L2a_b", 1), ("c_L3x_bq", 1), ("c_L3x_bk", 1),
    ("c_tgt_bias", 64),
]
ROWS = [
    ("L0a_o", 128), ("L0a_gamma", 16), ("L0a_beta", 16), ("L0x_o", 128), ("L0f_bias", 64), ("L1a_o", 128),
    ("L1xs_v", 128), ("L1xt_v", 128), ("L1xs_o", 128), ("L1xt_o", 128), ("L1x_b2", 128), ("L2f_b", 16),
    ("L3a_Alog", 8), ("L3a_dt", 8), ("L3a_norm", 128), ("L3x_v", 128), ("L3x_o", 128),
]
CONSTS = [
    ("ident", 128), ("gmask", GROUPS), ("rope_c", 8), ("rope_s", 8), ("causal", 64),
    ("strict", 64), ("notfirst", 1), ("upper", 128), ("ones", 128), ("two", 128),
    ("tri_inc", 128), ("tri_str", 128), ("level", 6 * 128), ("lw", 128), ("off", 128), ("pick", 32 * 128),
]


def offsets(table):
    at, out = 0, {}
    for name, n in table:
        out[name] = (at, n)
        at += n
    return out, at


W_AT, W_COLS = offsets(WEIGHTS)
R_AT, R_COLS = offsets(ROWS)
C_AT, C_COLS = offsets(CONSTS)


def shape_constants():
    p = np.arange(P)
    q = p % SEQ
    same = (p[:, None] // SEQ) == (p[None, :] // SEQ)
    c = {}
    c["ident"] = np.eye(P)
    c["gmask"] = (p[:, None] // HD) % 4 == np.arange(GROUPS)[None, :]
    c["tri_inc"] = same & (p[:, None] <= p[None, :])
    c["tri_str"] = same & (p[:, None] > p[None, :])
    c["ones"] = np.ones((P, P))
    levels = []
    for l in range(6):
        m = 2 ** l
        levels.append((p[:, None] // (2 * m) == p[None, :] // (2 * m))
                      & (p[:, None] // m % 2 == 1) & (p[None, :] // m % 2 == 0))
    c["level"] = np.concatenate(levels, 1)
    d = np.abs(q[:, None] - q[None, :]).astype(np.float32)
    c["lw"] = np.where(same & (d != 0), np.float32(1) / (d + np.float32(1e-7)), 0)
    c["off"] = same & (d != 0)
    inv = (1.0 / 10000.0 ** (np.arange(4, dtype=np.float32) / 4)).astype(np.float32)
    ang = (q[:, None].astype(np.float32) * inv[None, :]).astype(np.float32)
    c["rope_c"] = np.concatenate([np.cos(ang), np.cos(ang)], 1)
    c["rope_s"] = np.concatenate([-np.sin(ang), np.sin(ang)], 1)
    k = np.arange(SEQ)
    c["causal"] = np.where(k[None, :] > q[:, None], -1e9, 0)
    c["strict"] = np.where(k[None, :] >= q[:, None], -1e30, 0)
    c["notfirst"] = (q != 0)[:, None]
    c["upper"] = p[:, None] < p[None, :]
    pick = np.zeros((P, 32, P))
    for i in range(32):
        for r in range(P):
            if r % 64 // 2 == i:
                pick[r, i, (r % 2) * 64:(r % 2) * 64 + 64] = 1
    c["pick"] = pick.reshape(P, 32 * P)
    two = np.zeros((P, P))
    two[0, :SEQ] = 1
    two[1, SEQ:] = 1
    c["two"] = two
    return np.concatenate([np.asarray(c[n], np.float32) for n, _ in CONSTS], 1)


class Chain:

    def __init__(self, eng, sem, base=0):
        self.eng, self.sem, self.base, self.n = eng, sem, base, 0

    def mark(self, ins):
        ins.then_inc(self.sem, 1)
        self.n += 1

    def join(self):
        self.eng.wait_ge(self.sem, self.base + self.n)

    def step(self, ins):
        self.mark(ins)
        self.join()


def decoder_kernel(nc, d, out, first=0, last=12):
    ctx = ExitStack()
    uid = [0]
    used = []

    def sb(name, shape, dt=F32):
        return ctx.enter_context(nc.sbuf_tensor(name, shape, dt))

    @contextmanager
    def phase(*names):
        uid[0] += 1
        sems = [nc.alloc_semaphore(f"{n}_{uid[0]}") for n in names]
        if used and used[-1]:
            nc.clear_and_free_semaphores(used[-1])
        with nc.Block() as block:
            yield block, dict(zip(names, sems))
        used[:] = [sems]

    with ctx:
        PS = ctx.enter_context(nc.psum_tensor("PS", [P, 8, HALF], F32))
        WT = sb("WT", [P, W_COLS])
        RW = sb("RW", [P, R_COLS])
        CS = sb("CS", [P, C_COLS])
        X = sb("X", [P, TILES, P])
        XN = sb("XN", [P, TILES, P])
        XR = sb("XR", [P, TILES, P])
        HT = sb("HT", [P, TOK])
        CT = sb("CT", [P, TOK])
        QT = sb("QT", [P, TOK])
        KT = sb("KT", [P, TOK])
        VD = sb("VD", [P, BATCH, 2, P])
        identb = sb("identb", [P, P], BF16)
        causalb = sb("causalb", [P, SEQ], BF16)
        strictb = sb("strictb", [P, SEQ], BF16)
        upperb = sb("upperb", [P, P], BF16)
        onesb = sb("onesb", [P, P], BF16)
        pickb = sb("pickb", [P, 32 * P], BF16)
        stats = sb("stats", [P, TILES, 6])
        mv = sb("mv", [P, TILES, 2])
        rstd = sb("rstd", [P, TILES])
        idle = sb("idle", [P, 1])
        SRC = sb("SRC", [2, TILES, SEQ])
        BIG = [sb(f"BIG{i}", [P, 4096]) for i in range(4)]
        REL = BIG[3][:, 0:1024].rearrange("p (h k) -> p h k", h=HEADS)

        def w(name):
            a, n = W_AT[name]
            return WT[:, a:a + n]

        def row(name):
            a, n = R_AT[name]
            return RW[:, a:a + n]

        def cst(name):
            a, n = C_AT[name]
            return CS[:, a:a + n]

        ident = cst("ident")

        rest_loaded = nc.alloc_semaphore("rest_loaded")
        EARLY_W, EARLY_R, EARLY_C = W_AT["L0x_q"][0], R_AT["L0x_o"][0], C_AT["tri_inc"][0]
        with phase("loaded", "made", "zeroed") as (block, s):
            @block.sync
            def _(sp):
                sp.dma_start(X[:, :, :], d["x"]).then_inc(s["loaded"], 16)
                sp.dma_start(CS[:, 0:EARLY_C], d["consts"][:, 0:EARLY_C]).then_inc(s["loaded"], 16)
                sp.dma_start(CT[:, :], d["ctxT"]).then_inc(rest_loaded, 16)
                sp.dma_start(CS[:, EARLY_C:], d["consts"][:, EARLY_C:]).then_inc(rest_loaded, 16)
                sp.dma_start(SRC[:, :, :], d["src_bias"]).then_inc(rest_loaded, 16)

            @block.scalar
            def _(act):
                act.dma_start(WT[:, 0:EARLY_W], d["weights"][:, 0:EARLY_W]).then_inc(s["loaded"], 16)
                act.dma_start(RW[:, 0:EARLY_R], d["rows"][0:1, 0:EARLY_R].broadcast_to([P, EARLY_R]))\
                   .then_inc(s["loaded"], 16)
                act.dma_start(WT[:, EARLY_W:], d["weights"][:, EARLY_W:]).then_inc(rest_loaded, 16)
                act.dma_start(RW[:, EARLY_R:], d["rows"][0:1, EARLY_R:].broadcast_to([P, R_COLS - EARLY_R]))\
                   .then_inc(rest_loaded, 16)

            @block.vector
            def _(dve):
                dve.wait_ge(s["loaded"], 64)
                for dst, name in ((identb, "ident"), (causalb, "causal"), (strictb, "strict"),
                                  (upperb, "upper"), (onesb, "ones")):
                    dve.tensor_copy(dst[:, :], cst(name)).then_inc(s["made"], 1)
                dve.memset(idle[:, :], 0.0).then_inc(s["made"], 1)
                dve.wait_ge(s["made"], 6)

            @block.gpsimd
            def _(pool):
                pool.memset(VD[:, :, :, :], 0.0).then_inc(s["zeroed"], 1)

        def rest():
            with phase("made") as (block, s):
                @block.vector
                def _(dve):
                    dve.wait_ge(rest_loaded, 80)
                    dve.tensor_copy(pickb[:, :], cst("pick")).then_inc(s["made"], 1)

        def norm_factors(dve, c, rooted, src, eps, rms, counted):
            if not counted:
                for t in range(TILES):
                    c.mark(dve.bn_stats(stats[:, t, :], src[:, t, :]))
                c.join()
            for t in range(TILES):
                c.mark(dve.bn_aggr(mv[:, t, :], stats[:, t, :]))
            c.join()
            if rms:
                c.step(dve.tensor_tensor(rstd[:, :], mv[:, :, 0], mv[:, :, 0], ALU.mult))
                c.step(dve.tensor_tensor(mv[:, :, 1], mv[:, :, 1], rstd[:, :], ALU.add))
                c.step(dve.memset(mv[:, :, 0], 0.0))
            c.step(dve.tensor_scalar(rstd[:, :], mv[:, :, 1], eps, None, ALU.add))
            dve.wait_ge(rooted, 1)
            c.step(dve.reciprocal(rstd[:, :], rstd[:, :]))

        def normalize(src, dst, dstT, eps, gain=None, shift=None, rms=False, counted=False):
            with phase("stat", "rooted", "normed", "turned", "copied") as (block, s):
                @block.vector
                def _(dve):
                    norm_factors(dve, Chain(dve, s["stat"]), s["rooted"], src, eps, rms, counted)
                    for t in range(TILES):
                        dve.tensor_scalar(dst[:, t, :], src[:, t, :], mv[:, t, 0:1], rstd[:, t:t + 1],
                                          ALU.subtract, ALU.mult).then_inc(s["normed"], 1)

                @block.tensor
                def _(pe):
                    for t in range(TILES):
                        pe.wait_ge(s["normed"], t + 1)
                        pe.transpose(PS[:, t // 4, (t % 4) * P:(t % 4 + 1) * P], dst[:, t, :], ident)\
                          .then_inc(s["turned"], 1)

                @block.scalar
                def _(act):
                    act.activation(idle[:, :], idle[:, :], ACT.Sqrt)
                    act.wait_ge(s["stat"], (1 if counted else 2) * TILES + (4 if rms else 1))
                    act.activation(rstd[:, :], rstd[:, :], ACT.Sqrt).then_inc(s["rooted"], 1)
                    for h in range(2):
                        act.wait_ge(s["turned"], 4 * h + 4)
                        o = dstT[:, h * HALF:(h + 1) * HALF]
                        if gain is None:
                            act.activation(o, PS[:, h, :], ACT.Copy).then_inc(s["copied"], 1)
                        else:
                            act.activation(o, PS[:, h, :], ACT.Identity, bias=shift, scale=gain)\
                               .then_inc(s["copied"], 1)
                    act.wait_ge(s["copied"], 2)

        TWICE = BIG[3][:, 1024:3072]

        def copy_twice(act, src):
            return act.activation(TWICE.rearrange("p (b c k) -> p b c k", b=BATCH, c=2),
                                  src[:, :].rearrange("p (b k) -> p b k", b=BATCH).unsqueeze(2)
                                  .broadcast_to([P, BATCH, 2, SEQ]), ACT.Copy)

        def value_product(pe, b, wv, brow):
            o = PS[:, 4 + b // 4, (b % 4) * P:(b % 4 + 1) * P]
            mm = pe.matmul(o, TWICE[:, b * P:(b + 1) * P], wv, start=True, stop=brow is None)
            if brow is not None:
                mm = pe.matmul(o, cst("ones")[0:1, :], brow[0:1, :], start=False, stop=True)
            return mm

        def move_values(half, copy, parts=(0, 1)):
            rows = slice(half * SEQ, (half + 1) * SEQ)
            for k in parts:
                for pair in range(2):
                    src = PS[rows, 4 + 2 * k:6 + 2 * k, :].rearrange("p k (b g r e) -> p (k b) g r e", b=4, g=4, r=4)
                    dst = VD[rows, 8 * k:8 * k + 8, pair, :].rearrange("p b (g r e) -> p b g r e", g=4, r=4)
                    r = 2 * pair + half
                    copy(8 * k + 8, dst[:, :, :, r, :], src[:, :, :, r, :])

        def normalize_and_project(q_item, k_item, values, counted):
            with phase("stat", "rooted", "normed", "turned", "copied", "twice", "made", "evac", "vmade", "vevac") as (block, s):
                @block.tensor
                def _(pe):
                    def products(item, h):
                        pe.matmul(PS[:, 2 + h, :], item[1], item[2][:, h * HALF:(h + 1) * HALF], start=True, stop=True)\
                          .then_inc(s["made"], 1)

                    def some_values(first, last):
                        for b in range(first, last):
                            value_product(pe, b, values[1], values[2]).then_inc(s["vmade"], 1)

                    for h in range(2):
                        products(k_item, h)
                    pe.wait_ge(s["twice"], 1)
                    some_values(0, 4)
                    for t in range(TILES):
                        pe.wait_ge(s["normed"], t + 1)
                        pe.transpose(PS[:, t // 4, (t % 4) * P:(t % 4 + 1) * P], XN[:, t, :], ident).then_inc(s["turned"], 1)
                    some_values(4, 8)
                    pe.wait_ge(s["evac"], 1)
                    for h in range(2):
                        pe.wait_ge(s["copied"], h + 1)
                        products(q_item, h)
                    some_values(8, BATCH)

                @block.scalar
                def _(act):
                    def copy(made, dst, src):
                        act.wait_ge(s["vmade"], made)
                        act.activation(dst, src, ACT.Copy).then_inc(s["vevac"], 1)

                    act.activation(idle[:, :], idle[:, :], ACT.Sqrt)
                    copy_twice(act, values[0]).then_inc(s["twice"], 1)
                    act.wait_ge(s["stat"], (1 if counted else 2) * TILES + 1)
                    act.activation(rstd[:, :], rstd[:, :], ACT.Sqrt).then_inc(s["rooted"], 1)
                    for h in range(2):
                        act.wait_ge(s["turned"], 4 * h + 4)
                        act.activation(HT[:, h * HALF:(h + 1) * HALF], PS[:, h, :], ACT.Copy).then_inc(s["copied"], 1)
                    move_values(1, copy)

                @block.vector
                def _(dve):
                    def copy(made, dst, src):
                        dve.wait_ge(s["vmade"], made)
                        dve.tensor_copy(dst, src).then_inc(s["vevac"], 1)

                    def evacuate(item, made):
                        dst, _, _, bias, factor = item
                        dve.wait_ge(s["made"], made)
                        dve.tensor_scalar(dst[:, :].rearrange("p (a b) -> p a b", a=2), PS[:, 2:4, :],
                                          0.0 if bias is None else bias, factor, ALU.add, ALU.mult).then_inc(s["evac"], 1)

                    c = Chain(dve, s["stat"])
                    norm_factors(dve, c, s["rooted"], X, 1e-5, False, counted)
                    for t in range(TILES):
                        dve.tensor_scalar(XN[:, t, :], X[:, t, :], mv[:, t, 0:1], rstd[:, t:t + 1],
                                          ALU.subtract, ALU.mult).then_inc(s["normed"], 1)
                    evacuate(k_item, 2)
                    move_values(0, copy, (0,))
                    evacuate(q_item, 4)
                    move_values(0, copy, (1,))
                    dve.wait_ge(s["vevac"], 8)
                    dve.wait_ge(s["evac"], 2)

        def project(items, values=None):
            with phase("made", "evac", "twice", "vmade", "vevac") as (block, s):
                @block.scalar
                def _(act):
                    if values:
                        copy_twice(act, values[0]).then_inc(s["twice"], 1)

                        def copy(made, dst, src):
                            act.wait_ge(s["vmade"], made)
                            act.activation(dst, src, ACT.Copy).then_inc(s["vevac"], 1)
                        move_values(1, copy)

                @block.tensor
                def _(pe):
                    for n, (dst, wt, src, bias, factor) in enumerate(items):
                        if n >= 2:
                            pe.wait_ge(s["evac"], n - 1)
                        for h in range(2):
                            pe.matmul(PS[:, 2 * (n % 2) + h, :], wt, src[:, h * HALF:(h + 1) * HALF],
                                      start=True, stop=True).then_inc(s["made"], 1)
                    if values:
                        src, wv, brow = values
                        pe.wait_ge(s["twice"], 1)
                        for b in range(BATCH):
                            value_product(pe, b, wv, brow).then_inc(s["vmade"], 1)

                def evacuate(eng, n):
                    dst, wt, src, bias, factor = items[n]
                    eng.wait_ge(s["made"], 2 * n + 2)
                    view = dst[:, :].rearrange("p (a b) -> p a b", a=2)
                    return view, PS[:, 2 * (n % 2):2 * (n % 2) + 2, :], bias, factor

                @block.vector
                def _(dve):
                    for n in range(len(items)):
                        o, i, bias, factor = evacuate(dve, n)
                        dve.tensor_scalar(o, i, 0.0 if bias is None else bias, factor, ALU.add, ALU.mult)\
                           .then_inc(s["evac"], 1)
                    dve.wait_ge(s["evac"], len(items)) if items else None
                    if values:
                        def copy(made, dst, src):
                            dve.wait_ge(s["vmade"], made)
                            dve.tensor_copy(dst, src).then_inc(s["vevac"], 1)
                        move_values(0, copy)
                        dve.wait_ge(s["vevac"], 8)

        def token_qk(wq, wk, wv, rotate_norm, factor):
            QK = BIG[0][:, 0:2048]
            A = BIG[1][:, 0:2048]
            B = BIG[2][:, 0:2048]
            G = 2 * TILES * HEADS
            grp = lambda a: a.rearrange("p (g e) -> p g e", e=HD)
            sm = BIG[3][:, 0:G]
            va = BIG[3][:, 512:512 + G]
            rs = BIG[3][:, 768:768 + G]
            wide = lambda a: a.unsqueeze(2).broadcast_to([P, G, HD])
            with phase("made", "copied", "vec", "rooted", "ready", "turned", "evac", "twice", "vmade", "vevac") as (block, s):
                @block.tensor
                def _(pe):
                    for t in range(TILES):
                        ht = HT[:, t * P:(t + 1) * P]
                        o = PS[:, t // 2, (t % 2) * 256:(t % 2) * 256 + 256]
                        pe.matmul(o[:, 0:P], ht, wq, start=True, stop=True)
                        pe.matmul(o[:, P:2 * P], ht, wk, start=True, stop=True).then_inc(s["made"], 1)
                    pe.wait_ge(s["twice"], 1)
                    for b in range(BATCH):
                        value_product(pe, b, wv, None).then_inc(s["vmade"], 1)
                    pe.wait_ge(s["vevac"], 8)
                    pe.wait_ge(s["ready"], 1)
                    for n in range(2):
                        for t in range(TILES):
                            pe.transpose(PS[:, 4 + 2 * n + t // 4, (t % 4) * P:(t % 4 + 1) * P],
                                         QK[:, (2 * t + n) * P:(2 * t + n + 1) * P], ident).then_inc(s["turned"], 1)

                @block.scalar
                def _(act):
                    copy_twice(act, HT).then_inc(s["twice"], 1)
                    act.wait_ge(s["made"], TILES)
                    act.activation(QK.rearrange("p (a b) -> p a b", a=4), PS[:, 0:4, :], ACT.Copy).then_inc(s["copied"], 1)

                    def copy(made, dst, src):
                        act.wait_ge(s["vmade"], made)
                        act.activation(dst, src, ACT.Copy).then_inc(s["vevac"], 1)

                    for half in range(2):
                        move_values(half, copy)
                    if rotate_norm:
                        act.wait_ge(s["vec"], 6)
                        act.activation(rs, va, ACT.Sqrt).then_inc(s["rooted"], 1)
                    for n in range(2):
                        act.wait_ge(s["turned"], TILES * (n + 1))
                        dst = (QT, KT)[n]
                        act.activation(dst[:, :].rearrange("p (a b) -> p a b", a=2), PS[:, 4 + 2 * n:6 + 2 * n, :],
                                       ACT.Copy, scale=factor if n == 0 else 1.0).then_inc(s["evac"], 1)
                    act.wait_ge(s["evac"], 2)

                @block.vector
                def _(dve):
                    c = Chain(dve, s["vec"])
                    dve.wait_ge(s["copied"], 1)
                    if rotate_norm:
                        c.step(dve.tensor_reduce(sm, grp(QK), AX.X, ALU.add))
                        c.step(dve.tensor_scalar(sm, sm, 1.0 / HD, None, ALU.mult))
                        c.step(dve.tensor_tensor(grp(QK), grp(QK), wide(sm), ALU.subtract))
                        c.step(dve.tensor_tensor(A, QK, QK, ALU.mult))
                        c.step(dve.tensor_reduce(va, grp(A), AX.X, ALU.add))
                        c.step(dve.tensor_scalar(va, va, 1.0 / HD, 1e-6, ALU.mult, ALU.add))
                        dve.wait_ge(s["rooted"], 1)
                        c.step(dve.reciprocal(rs, rs))
                        c.step(dve.tensor_tensor(grp(QK), grp(QK), wide(rs), ALU.mult))
                        four = QK.rearrange("p (t n h e) -> p t n h e", t=TILES, n=2, e=HD)
                        for name, op in (("L0a_gamma", ALU.mult), ("L0a_beta", ALU.add)):
                            for n in range(2):
                                r = row(name)[:, n * HD:(n + 1) * HD].unsqueeze(1).unsqueeze(1)\
                                    .broadcast_to([P, TILES, HEADS, HD])
                                c.mark(dve.tensor_tensor(four[:, :, n], four[:, :, n], r, op))
                            c.join()
                    rc = cst("rope_c").unsqueeze(1).broadcast_to([P, G, HD])
                    h4 = HD // 2
                    c.mark(dve.tensor_tensor(grp(A), grp(QK), rc, ALU.mult))
                    for x in range(2):
                        sn = cst("rope_s")[:, x * h4:(x + 1) * h4].unsqueeze(1).broadcast_to([P, G, h4])
                        c.mark(dve.tensor_tensor(grp(B)[:, :, x * h4:(x + 1) * h4],
                                                 grp(QK)[:, :, (1 - x) * h4:(2 - x) * h4], sn, ALU.mult))
                    c.join()
                    dve.tensor_tensor(QK, A, B, ALU.add).then_inc(s["ready"], 1)

        KM = [BIG[1][:, t * 512:(t + 1) * 512].rearrange("p (r k) -> p r k", r=GROUPS) for t in range(TILES)]
        EX = [BIG[2][:, 0:1024], BIG[2][:, 1024:2048], BIG[0][:, 0:1024]]
        PT = [BIG[2][:, 2048 + i * 1024:3072 + i * 1024].rearrange("p (j q) -> p j q", j=8) for i in range(2)]
        OT = [BIG[0][:, 2304 + i * 128:2432 + i * 128] for i in range(2)]
        MX = [BIG[0][:, 2560 + i * 16:2576 + i * 16] for i in range(2)]
        RI = [BIG[0][:, 2592 + i * 16:2608 + i * 16] for i in range(2)]
        SB = BIG[0][:, 3072:3584].rearrange("p (t k) -> p t k", t=TILES)

        def attend(wo, dst, bias=None, bias_row=None):
            LAST = TILES + 4
            added_bias = bias in ("tgt", "src", "rel")
            ENDS = (0, TILES - 1)
            with phase("masked", "scored", "vec", "subbed", "exped", "summed", "weighed", "weighed_ends", "turned", "copied", "mixed",
                       "ocopied", "projected", "added", "based", "rowed", "spread") as (block, s):
                four = lambda a: a.rearrange("p (g r k) -> p g r k", g=4, r=4)
                by_head = lambda a: a.rearrange("p (h k) -> p h k", h=HEADS)

                def stages(*order):
                    for step in range(LAST):
                        for stage, lag in order:
                            if 0 <= step - lag < TILES:
                                stage(step - lag)

                @block.gpsimd
                def _(pool):
                    def mask_keys(t):
                        pool.tensor_tensor(
                            KM[t], KT[:, t * P:(t + 1) * P].unsqueeze(1).broadcast_to([P, GROUPS, P]),
                            cst("gmask").unsqueeze(2).broadcast_to([P, GROUPS, P]), ALU.mult).then_inc(s["masked"], 1)

                    def weigh(t):
                        if t == 1 and bias_row is not None:
                            pool.tensor_tensor(dst[:, :, :], dst[:, :, :],
                                               bias_row.unsqueeze(1).broadcast_to([P, TILES, P]), ALU.add)\
                                .then_inc(s["based"], 1)
                        pool.wait_ge(s["summed"], t)
                        e = by_head(EX[t % 3])
                        pool.tensor_tensor(e, e, RI[t % 2].unsqueeze(2).broadcast_to([P, HEADS, SEQ]), ALU.mult)\
                            .then_inc(s["weighed"], 1)

                    mask_keys(0)
                    mask_keys(1)
                    for t in range(TILES):
                        if t + 2 < TILES:
                            mask_keys(t + 2)
                        if t not in ENDS:
                            weigh(t)

                @block.tensor
                def _(pe):
                    if bias == "src":
                        pe.matmul(PS[:, 7, :], cst("two")[0:2, :], SRC[:, :, :], start=True, stop=True)\
                          .then_inc(s["rowed"], 1)

                    def scores(t):
                        pe.wait_ge(s["masked"], t + 1)
                        if t > 0:
                            pe.wait_ge(s["subbed"], t)
                        for g in range(4):
                            if bias in ("causal", "strict"):
                                m = (causalb if bias == "causal" else strictb)[:, :]
                                pe.matmul(PS[:, g, 0:256].rearrange("p (r k) -> p r k", r=4), identb[:, :],
                                          m.unsqueeze(1).broadcast_to([P, 4, SEQ]), start=True, stop=False)
                        for b in range(PER):
                            q = slice(b * SEQ, (b + 1) * SEQ)
                            for g in range(4):
                                rows = slice(32 * g, 32 * g + 32)
                                mm = pe.matmul(PS[q, g, 0:256].rearrange("p (r k) -> p r k", r=4),
                                               QT[rows, t * P + b * SEQ:t * P + (b + 1) * SEQ], KM[t][rows, :, q],
                                               start=bias is None or added_bias, stop=True)
                        mm.then_inc(s["scored"], 1)

                    def turn_probs(t):
                        if t in ENDS:
                            pe.wait_ge(s["weighed_ends"], 1 + ENDS.index(t))
                        else:
                            pe.wait_ge(s["weighed"], t)
                        if t > 0:
                            pe.wait_ge(s["copied"], t)
                        for j in range(8):
                            mm = pe.transpose(PS[:, 4 + j // 4, (j % 4) * P:(j % 4 + 1) * P],
                                              EX[t % 3][:, j * P:(j + 1) * P], ident)
                        mm.then_inc(s["turned"], 1)

                    def mix(t):
                        pe.wait_ge(s["copied"], t + 1)
                        if t > 0:
                            pe.wait_ge(s["ocopied"], t)
                        for b in range(PER):
                            q = slice(b * SEQ, (b + 1) * SEQ)
                            for j in range(8):
                                rows = slice(32 * (j // 2), 32 * (j // 2) + 32)
                                mm = pe.matmul(PS[rows, 6, q], VD[:, PER * t + b, j % 2, rows], PT[t % 2][:, j, q],
                                               start=j % 2 == 0, stop=j % 2 == 1)
                        mm.then_inc(s["mixed"], 1)

                    def project_out(t):
                        pe.wait_ge(s["ocopied"], t + 1)
                        if t > 0:
                            pe.wait_ge(s["added"], t)
                        elif bias == "src":
                            pe.wait_ge(s["spread"], 1)
                        pe.matmul(PS[:, 7, 0:P], OT[t % 2], wo, start=True, stop=True).then_inc(s["projected"], 1)

                    stages((scores, 0), (turn_probs, 2), (mix, 3), (project_out, 4))

                @block.vector
                def _(dve):
                    c = Chain(dve, s["vec"])
                    if bias == "src":
                        dve.wait_ge(s["rowed"], 1)
                        dve.tensor_copy(SB, PS[:, 7, :].rearrange("p (t k) -> p t k", t=TILES)).then_inc(s["spread"], 1)
                        dve.wait_ge(s["spread"], 1)

                    def shift(t):
                        S = PS[:, 0:4, 0:256].rearrange("p g (r k) -> p g r k", r=4)
                        E = four(EX[t % 3])
                        dve.wait_ge(s["scored"], t + 1)
                        if t > 2:
                            dve.wait_ge(s["turned"], t - 2)
                        m = MX[t % 2].rearrange("p (g r) -> p g r", g=4)
                        if added_bias:
                            if bias == "rel":
                                a = REL.rearrange("p (g r) k -> p g r k", g=4)
                            else:
                                a = w("c_tgt_bias") if bias == "tgt" else SB[:, t, :]
                                a = a.unsqueeze(1).unsqueeze(1).broadcast_to([P, 4, 4, SEQ])
                            c.step(dve.tensor_tensor(E, S, a, ALU.add))
                            S = E
                        c.step(dve.tensor_reduce(m, S, AX.X, ALU.max))
                        dve.tensor_tensor(E, S, m.unsqueeze(3).broadcast_to([P, 4, 4, SEQ]), ALU.subtract)\
                            .then_inc(s["subbed"], 1)

                    def add_up(t):
                        dve.wait_ge(s["exped"], t + 1)
                        if t > 2:
                            dve.wait_ge(s["weighed"], t - 2)
                        r = RI[t % 2]
                        c.step(dve.tensor_reduce(r, by_head(EX[t % 3]), AX.X, ALU.add))
                        last = dve.reciprocal(r, r)
                        if bias == "strict":
                            c.step(last)
                            last = dve.tensor_scalar(r, r, cst("notfirst"), None, ALU.mult)
                        if t in ENDS:
                            c.step(last)
                            e = by_head(EX[t % 3])
                            dve.tensor_tensor(e, e, r.unsqueeze(2).broadcast_to([P, HEADS, SEQ]), ALU.mult)\
                               .then_inc(s["weighed_ends"], 1)
                        else:
                            last.then_inc(s["summed"], 1)

                    def add(t):
                        if t == 0 and bias_row is not None:
                            dve.wait_ge(s["based"], 1)
                        dve.wait_ge(s["projected"], t + 1)
                        dve.tensor_tensor(dst[:, t, :], dst[:, t, :], PS[:, 7, 0:P], ALU.add).then_inc(s["added"], 1)
                        if t > 0:
                            count(t - 1)

                    def count(t):
                        dve.wait_ge(s["added"], t + 1)
                        c.mark(dve.bn_stats(stats[:, t, :], dst[:, t, :]))

                    stages((add_up, 1), (shift, 0), (add, 4))
                    count(TILES - 1)
                    c.join()

                @block.scalar
                def _(act):
                    def copy_probs(t):
                        act.wait_ge(s["turned"], t + 1)
                        if t > 1:
                            act.wait_ge(s["mixed"], t - 1)
                        act.activation(PT[t % 2].rearrange("p (a b) q -> p a (b q)", a=2), PS[:, 4:6, :], ACT.Copy)\
                            .then_inc(s["copied"], 1)

                    def exponent(t):
                        act.wait_ge(s["subbed"], t + 1)
                        act.activation(EX[t % 3], EX[t % 3], ACT.Exp).then_inc(s["exped"], 1)

                    def copy_out(t):
                        act.wait_ge(s["mixed"], t + 1)
                        if t > 1:
                            act.wait_ge(s["projected"], t - 1)
                        act.activation(OT[t % 2], PS[:, 6, 0:P], ACT.Copy).then_inc(s["ocopied"], 1)

                    stages((copy_probs, 2), (exponent, 0), (copy_out, 3))

        def turn(src, dstT):
            with phase("turned", "copied") as (block, s):
                @block.tensor
                def _(pe):
                    for t in range(TILES):
                        pe.transpose(PS[:, t // 4, (t % 4) * P:(t % 4 + 1) * P], src[:, t, :], ident)\
                          .then_inc(s["turned"], 1)

                @block.scalar
                def _(act):
                    for h in range(2):
                        act.wait_ge(s["turned"], 4 * h + 4)
                        act.activation(dstT[:, h * HALF:(h + 1) * HALF], PS[:, h, :], ACT.Copy).then_inc(s["copied"], 1)
                    act.wait_ge(s["copied"], 2)

        GATE = sb("GATE", [P, TILES, 64])

        def route(srcT, wg, E, K, kind, capacity):
            V = E + 8 - K
            n = TILES * E
            cut = lambda i, m: BIG[0][:, i * 512:i * 512 + TILES * m].rearrange("p (t e) -> p t e", t=TILES)
            LG, SCORE, MASK, PROB, TOP = cut(0, E), cut(1, E), cut(2, E), cut(3, E), cut(4, 8)
            VAL = BIG[1][:, 0:TILES * V].rearrange("p (t e) -> p t e", t=TILES)
            REP = BIG[1][:, 1024:1024 + TILES * V].rearrange("p (t e) -> p t e", t=TILES)
            RED = BIG[1][:, 2048:2048 + TILES]
            MASKB = BIG[1][:, 2304:2304 + n // 2].bitcast(BF16).rearrange("p (t e) -> p t e", t=TILES)
            WM = BIG[2][0:16, 0:TOK]
            WR = BIG[2][0:16, TOK:2 * TOK]
            KEPT = BIG[2][0:16, 2 * TOK:3 * TOK]
            W8 = BIG[2][0:16, 3 * TOK:3 * TOK + 8]
            TAKEN, LEAST = -3.2e38, NEVER
            wide = lambda a: a.unsqueeze(2).broadcast_to([P, TILES, E])
            logits = PS[:, 0, 0:n].rearrange("p (t e) -> p t e", t=TILES)
            before = PS[:, 1, 0:n].rearrange("p (t e) -> p t e", t=TILES)
            rounds = capacity // 8
            CHUNKS = 2
            PAIRS = (E, 0)
            columns = 2 * CHUNKS * P
            SW = [[BIG[0][:, 2560 + i * columns:2560 + (i + 1) * columns] for i in range(3)],
                  [QT[:, 0:columns], QT[:, columns:2 * columns], KT[:, 0:columns]]]
            SHID = [BIG[3][:, c * TOK:(c + 1) * TOK] for c in range(2 * CHUNKS)]
            SGATE = [EXTRA[:, c * TOK:(c + 1) * TOK] for c in range(2 * CHUNKS)]
            STEPS = 4 * CHUNKS
            with phase("logits", "scored", "vec", "masked", "counted", "turned", "kept", "back",
                       "sloaded", "smade", "sacted", "sgated", "sout", "ssaved") as (block, s):
                if kind == "logit":
                    @block.sync
                    def _(sp):
                        for W, unit in zip(SW, PAIRS):
                            for dst, name in zip(W, ("L2f_w1", "L2f_w3", "L2f_w2")):
                                sp.dma_start(dst, d[name][:, unit * CHUNKS * P:unit * CHUNKS * P + columns])\
                                    .then_inc(s["sloaded"], 16)

                    @block.gpsimd
                    def _(pool):
                        for c in range(4 * CHUNKS):
                            hid, gate = SHID[c % (2 * CHUNKS)], SGATE[c % (2 * CHUNKS)]
                            pool.wait_ge(s["sacted"], 2 * c + 2)
                            pool.tensor_tensor(hid, hid, gate, ALU.mult).then_inc(s["sgated"], 1)

                @block.tensor
                def _(pe):
                    for t in range(TILES):
                        pe.matmul(logits[:, t, :], srcT[:, t * P:(t + 1) * P], wg, start=True, stop=True)\
                          .then_inc(s["logits"], 1)
                    pe.wait_ge(s["masked"], 1)
                    if kind != "logit":
                        for t in range(TILES):
                            for b in range(t + 1):
                                mm = pe.matmul(before[:, t, :], (upperb if b == t else onesb)[:, :], MASKB[:, b, :],
                                               start=b == 0, stop=b == t)
                        mm.then_inc(s["counted"], 1)
                    else:
                        for t in range(TILES):
                            mm = pe.transpose(PS[0:16, 2 + t // 4, (t % 4) * P:(t % 4 + 1) * P], PROB[:, t, :], ident)
                        mm.then_inc(s["turned"], 1)
                        pe.wait_ge(s["sloaded"], 96)
                        for pair, W in enumerate(SW):
                            for n in range(STEPS):
                                c, h = n // 2, n % 2
                                if n >= 2:
                                    pe.wait_ge(s["sacted"], pair * STEPS + n - 1)
                                elif pair == 1:
                                    pe.wait_ge(s["ssaved"], 1)
                                for k in range(2):
                                    mm = pe.matmul(PS[:, 4 + 2 * h + k, :], W[k][:, c * P:(c + 1) * P],
                                                   srcT[:, h * HALF:(h + 1) * HALF], start=True, stop=True)
                                mm.then_inc(s["smade"], 1)
                            pe.wait_ge(s["sgated"], (pair + 1) * 2 * CHUNKS)
                            for first in (range(2) if pair == 1 else range(1)):
                                mine = range(first * CHUNKS, (first + 1) * CHUNKS) if pair == 1 else range(2 * CHUNKS)
                                for t in range(TILES):
                                    for c in mine:
                                        mm = pe.matmul(PS[:, 4 + 2 * first + t // 4, (t % 4) * P:(t % 4 + 1) * P],
                                                       SHID[c][:, t * P:(t + 1) * P], W[2][:, c * P:(c + 1) * P],
                                                       start=c == mine[0], stop=c == mine[-1])
                            mm.then_inc(s["sout"], 1)
                        pe.wait_ge(s["kept"], 1)
                        for t in range(TILES):
                            mm = pe.transpose(before[:, t, :], KEPT[:, t * P:(t + 1) * P], ident[0:16, 0:16])
                        mm.then_inc(s["back"], 1)

                @block.scalar
                def _(act):
                    if kind == "sigmoid":
                        act.wait_ge(s["logits"], TILES)
                        act.activation(SCORE, logits, ACT.Sigmoid).then_inc(s["scored"], 1)
                    else:
                        act.wait_ge(s["vec"], 3)
                        act.activation(SCORE, SCORE, ACT.Exp).then_inc(s["scored"], 1)
                    if kind == "logit":
                        for pair in range(2):
                            for n in range(STEPS):
                                c, h = n // 2, n % 2
                                act.wait_ge(s["smade"], pair * STEPS + n + 1)
                                cols = slice(h * HALF, (h + 1) * HALF)
                                act.activation(SHID[c][:, cols], PS[:, 4 + 2 * h, :], ACT.Silu)
                                act.activation(SGATE[c][:, cols], PS[:, 5 + 2 * h, :], ACT.Copy).then_inc(s["sacted"], 1)
                            if pair == 0:
                                act.wait_ge(s["sout"], 1)
                                act.activation(XR[:, :, :].rearrange("p (a t) f -> p a (t f)", a=2), PS[:, 4:6, :],
                                               ACT.Copy, scale=0.5).then_inc(s["ssaved"], 1)

                @block.vector
                def _(dve):
                    c = Chain(dve, s["vec"])
                    if kind != "sigmoid":
                        dve.wait_ge(s["logits"], TILES)
                        c.mark(dve.tensor_copy(LG, logits))
                        c.step(dve.tensor_reduce(RED, logits, AX.X, ALU.max))
                        c.step(dve.tensor_tensor(SCORE, LG, wide(RED), ALU.subtract))
                    dve.wait_ge(s["scored"], 1)
                    if kind != "sigmoid":
                        c.step(dve.tensor_reduce(RED, SCORE, AX.X, ALU.add))
                        c.step(dve.reciprocal(RED, RED))
                        c.step(dve.tensor_tensor(SCORE, SCORE, wide(RED), ALU.mult))
                    c.mark(dve.memset(VAL[:, :, E:V], NEVER))
                    if kind == "softmax":
                        c.step(dve.tensor_copy(VAL[:, :, 0:E], SCORE))
                    else:
                        b = row("L0f_bias" if kind == "sigmoid" else "L2f_b")
                        c.step(dve.tensor_tensor(VAL[:, :, 0:E], SCORE,
                                                 b.unsqueeze(1).broadcast_to([P, TILES, E]), ALU.add))
                    for t in range(TILES):
                        c.mark(dve.max(TOP[:, t, :], VAL[:, t, :]))
                    c.join()
                    c.step(dve.memset(TOP[:, :, K:8], NEVER))
                    for t in range(TILES):
                        c.mark(dve.match_replace(REP[:, t, :], TOP[:, t, :], VAL[:, t, :], -2.0e38))
                    c.join()
                    c.step(dve.tensor_tensor(MASK, REP[:, :, 0:E], VAL[:, :, 0:E], ALU.not_equal))
                    if kind == "logit":
                        c.step(dve.tensor_tensor(PROB, LG, MASK, ALU.mult))
                        c.step(dve.tensor_scalar(SCORE, MASK, -NEVER, NEVER, ALU.mult, ALU.add))
                        c.mark(dve.tensor_tensor(PROB, PROB, SCORE, ALU.add))
                        c.join()
                        dve.sem_inc(s["masked"], 1)
                        dve.wait_ge(s["turned"], 1)
                        c.mark(dve.tensor_copy(WM, PS[0:16, 2:4, :].rearrange("p a b -> p (a b)")))
                        c.step(dve.tensor_copy(WR, PS[0:16, 2:4, :].rearrange("p a b -> p (a b)")))
                        for r in range(rounds):
                            c.step(dve.max(W8, WR))
                            c.step(dve.match_replace(WR, W8, WR, TAKEN))
                        c.mark(dve.tensor_tensor(KEPT, WR, WM, ALU.not_equal))
                        c.join()
                        dve.sem_inc(s["kept"], 1)
                        dve.wait_ge(s["back"], 1)
                        c.step(dve.tensor_tensor(MASK, MASK, before, ALU.mult))
                        c.step(dve.tensor_tensor(GATE[:, :, 0:E], LG, MASK, ALU.mult))
                        dve.wait_ge(s["ssaved"], 1)
                        c.step(dve.tensor_tensor(X[:, :, :], X[:, :, :], XR[:, :, :], ALU.add))
                        dve.wait_ge(s["sout"], 2)
                        for e in range(2):
                            for t in range(TILES):
                                c.mark(dve.scalar_tensor_tensor(
                                    out=X[:, t, :], in0=PS[:, 4 + 2 * e + t // 4, (t % 4) * P:(t % 4 + 1) * P],
                                    scalar=GATE[:, t, e:e + 1], in1=X[:, t, :], op0=ALU.mult, op1=ALU.add))
                            if e == 0:
                                c.join()
                        c.join()
                        return
                    dve.tensor_copy(MASKB, MASK).then_inc(s["masked"], 1)
                    if kind == "sigmoid":
                        c.step(dve.tensor_tensor(PROB, SCORE, MASK, ALU.mult))
                        c.step(dve.tensor_reduce(RED, PROB, AX.X, ALU.add))
                        c.step(dve.tensor_scalar(RED, RED, 1e-20, None, ALU.add))
                        c.step(dve.reciprocal(RED, RED))
                        c.step(dve.tensor_tensor(PROB, PROB, wide(RED), ALU.mult))
                    else:
                        c.step(dve.tensor_tensor(PROB, SCORE, MASK, ALU.mult))
                    dve.wait_ge(s["counted"], 1)
                    c.step(dve.scalar_tensor_tensor(out=GATE[:, :, 0:E], in0=before, scalar=float(capacity), in1=PROB,
                                                    op0=ALU.is_lt, op1=ALU.mult))

        def experts(srcT, names, begin, units, chunks, func, bias, dst):
            n = chunks * P
            W1 = [BIG[0][:, u * 512:u * 512 + n] for u in range(2)]
            W3 = [BIG[0][:, 1024 + u * 512:1024 + u * 512 + n] for u in range(2)]
            W2 = [BIG[0][:, 2048 + u * 512:2048 + u * 512 + n] for u in range(2)]
            HID = [[BIG[2 + u][:, c * TOK:(c + 1) * TOK] for c in range(chunks)] for u in range(2)]
            gated = len(names) == 3
            STEPS = 4
            assert chunks * (2 if gated else 1) == STEPS

            def where(step, u):
                c = step // 2 if gated else step
                o = HID[u][c].rearrange("p (a b) -> p a b", a=2)
                return c, (o[:, step % 2, :] if gated else o)

            def pipeline(eng, hidden, output):
                def both(h, y):
                    for n in range(2):
                        if h is not None:
                            for step in (2 * n, 2 * n + 1):
                                hidden(*h, step)
                        if y is not None:
                            output(*y, n)
                both((0, 0), None)
                with eng.Fori(0, units // 2 - 1) as i:
                    both((i, 1), (i, 0))
                    both((i + 1, 0), (i, 1))
                last = units // 2 - 1
                both((last, 1), (last, 0))
                both(None, (last, 1))

            with phase("w1_even", "w1_odd", "w2_even", "w2_odd", "made", "acted", "ready", "ymade", "added") as (block, s):
                w1_loaded, w2_loaded = (s["w1_even"], s["w1_odd"]), (s["w2_even"], s["w2_odd"])

                @block.sync
                def _(sp):
                    with sp.Fori(0, units // 2) as i:
                        for u in range(2):
                            e = i * 2 + u
                            sp.wait_ge(s["made"], e * STEPS + STEPS)
                            sp.dma_start(W1[u], d[names[0]][:, bass.ts(e + begin, n)]).then_inc(w1_loaded[u], 16)
                            if gated:
                                sp.dma_start(W3[u], d[names[1]][:, bass.ts(e + begin, n)]).then_inc(w1_loaded[u], 16)
                            sp.wait_ge(s["ymade"], e * 2 + 2)
                            sp.dma_start(W2[u], d[names[-1]][:, bass.ts(e + begin, n)]).then_inc(w2_loaded[u], 16)

                @block.tensor
                def _(pe):
                    pe.sem_inc(s["made"], 2 * STEPS)
                    pe.sem_inc(s["ymade"], 4)

                    def hidden(i, u, step):
                        e = i * 2 + u
                        c, _ = where(step, u)
                        if step == 0:
                            pe.wait_ge(w1_loaded[u], (i + 1) * (16 * (len(names) - 1)))
                        pe.wait_ge(s["ready"], e * STEPS + (step + 1))
                        wc = slice(c * P, (c + 1) * P)
                        for k in range(2):
                            W, h = ((W1, W3)[k], step % 2) if gated else (W1, k)
                            mm = pe.matmul(PS[:, 2 * (step % 2) + k, :], W[u][:, wc], srcT[:, h * HALF:(h + 1) * HALF],
                                           start=True, stop=True)
                        mm.then_inc(s["made"], 1)

                    def output(i, u, h):
                        e = i * 2 + u
                        if h == 0:
                            pe.wait_ge(s["ready"], e * STEPS + (STEPS + 2))
                            pe.wait_ge(w2_loaded[u], i * 16 + 16)
                        pe.wait_ge(s["added"], e * 2 + (h + 1))
                        for t in range(4 * h, 4 * h + 4):
                            for c in range(chunks):
                                mm = pe.matmul(PS[:, 4 + h, (t % 4) * P:(t % 4 + 1) * P],
                                               HID[u][c][:, t * P:(t + 1) * P], W2[u][:, c * P:(c + 1) * P],
                                               start=c == 0, stop=c == chunks - 1)
                        mm.then_inc(s["ymade"], 1)

                    pipeline(pe, hidden, output)

                @block.scalar
                def _(act):
                    if not gated:
                        act.sem_inc(s["ready"], 2)
                    with act.Fori(0, units // 2) as i:
                        for u in range(2):
                            e = i * 2 + u
                            act.wait_ge(s["ymade"], e * 2 + 2)
                            for step in range(STEPS):
                                act.wait_ge(s["made"], e * STEPS + (2 * STEPS + step + 1))
                                c, o = where(step, u)
                                b = 2 * (step % 2)
                                src = PS[:, b, :] if gated else PS[:, b:b + 2, :]
                                if bias is None:
                                    ins = act.activation(o, src, func)
                                else:
                                    ins = act.activation(o, src, func, bias=bias[:, bass.ds(e * chunks + c, 1)])
                                ins.then_inc(s["acted"] if gated else s["ready"], 1)

                @block.vector
                def _(dve):
                    dve.sem_inc(s["added"], 2)
                    if gated:
                        dve.sem_inc(s["ready"], 2)

                    def hidden(i, u, step):
                        if gated:
                            dve.wait_ge(s["acted"], (i * 2 + u) * STEPS + (step + 1))
                            _, o = where(step, u)
                            dve.tensor_tensor(o, o, PS[:, 2 * (step % 2) + 1, :], ALU.mult).then_inc(s["ready"], 1)

                    def output(i, u, h):
                        e = i * 2 + u
                        dve.wait_ge(s["ymade"], e * 2 + (h + 5))
                        dve.wait_ge(s["added"], e * 2 + (h + 1))
                        for t in range(4 * h, 4 * h + 4):
                            ins = dve.scalar_tensor_tensor(
                                out=dst[:, t, :], in0=PS[:, 4 + h, (t % 4) * P:(t % 4 + 1) * P],
                                scalar=GATE[:, t, bass.ds(e + begin, 1)], in1=dst[:, t, :], op0=ALU.mult, op1=ALU.add)
                        ins.then_inc(s["added"], 1)

                    pipeline(dve, hidden, output)
                    dve.wait_ge(s["added"], 2 * units + 2)

        def l1_ffn(counted):
            normalize(X, XR, HT, 1e-5)
            normalize(XR, XN, HT, 1e-5, w("c_ln1_g"), w("c_ln1_b"))
            token_qk(w("L1f_q"), w("L1f_k"), w("L1f_v"), False, HD ** -0.5)
            attend(w("L1f_o"), XR, "causal")
            normalize(XR, XN, HT, 1e-5, w("c_ln2_g"), w("c_ln2_b"), counted=True)
            route(HT, w("L1f_gate"), 8, 2, "softmax", 256)
            B2 = BIG[1][0:8, 0:P]
            GT = BIG[1][0:8, P:P + TOK]
            with phase("loaded", "turned", "copied", "made", "vec") as (block, s):
                @block.sync
                def _(sp):
                    sp.dma_start(B2, d["L1f_b2"]).then_inc(s["loaded"], 16)

                @block.tensor
                def _(pe):
                    for t in range(TILES):
                        mm = pe.transpose(PS[0:8, t // 4, (t % 4) * P:(t % 4 + 1) * P], GATE[:, t, 0:8], ident)
                    mm.then_inc(s["turned"], 1)
                    pe.wait_ge(s["loaded"], 16)
                    pe.wait_ge(s["copied"], 1)
                    for t in range(TILES):
                        mm = pe.matmul(PS[:, 2 + t // 4, (t % 4) * P:(t % 4 + 1) * P], GT[:, t * P:(t + 1) * P], B2,
                                       start=True, stop=True)
                    mm.then_inc(s["made"], 1)

                @block.scalar
                def _(act):
                    act.wait_ge(s["turned"], 1)
                    act.activation(GT.rearrange("p (a b) -> p a b", a=2), PS[0:8, 0:2, :], ACT.Copy).then_inc(s["copied"], 1)

                @block.vector
                def _(dve):
                    c = Chain(dve, s["vec"])
                    both = lambda a: a[:, :, :].rearrange("p (a t) f -> p a (t f)", a=2)
                    c.step(dve.tensor_tensor(both(X), both(X), both(XR), ALU.add))
                    dve.wait_ge(s["made"], 1)
                    c.step(dve.tensor_tensor(both(X), both(X), PS[:, 2:4, :], ALU.add))
            experts(HT, ("L1f_w1", "L1f_w2"), 0, 8, 4, ACT.Gelu, w("c_L1f_b1"), X)

        def l2_ffn(counted):
            normalize(X, XN, HT, 1e-5, counted=counted)
            route(HT, w("L2f_gate"), 16, 2, "logit", 160)
            experts(HT, ("L2f_w1", "L2f_w3", "L2f_w2"), 2, 14, 2, ACT.Silu, None, X)

        def l2_attn(counted):
            normalize(X, XN, HT, 1e-5)
            project([(QT, w("L2a_w"), HT, w("c_L2a_b"), 1.0)])
            WW = BIG[0][:, 0:TOK]
            SM = BIG[0][:, TOK:TOK + TILES]
            ww = WW.rearrange("p (t k) -> p t k", t=TILES)
            two = lambda a: a.rearrange("p (a b) -> p a b", a=2)
            quad = lambda a: a.unsqueeze(1).broadcast_to([P, 4, P])
            with phase("scored", "vec", "exped", "weighed", "mixed") as (block, s):
                @block.tensor
                def _(pe):
                    for t in range(TILES):
                        cols = slice(t * P, (t + 1) * P)
                        mm = pe.matmul(PS[:, t // 4, (t % 4) * P:(t % 4 + 1) * P], HT[:, cols], QT[:, cols],
                                       start=True, stop=True)
                    mm.then_inc(s["scored"], 1)
                    pe.wait_ge(s["weighed"], 1)
                    for t in range(TILES):
                        pe.matmul(PS[:, 2 + t // 4, (t % 4) * P:(t % 4 + 1) * P], ww[:, t, :], XN[:, t, :],
                                  start=True, stop=True)
                        mm = pe.matmul(PS[:, 4, t:t + 1], ww[:, t, :], cst("ones")[:, 0:1], start=True, stop=True)
                    mm.then_inc(s["mixed"], 1)

                @block.scalar
                def _(act):
                    act.wait_ge(s["vec"], 2)
                    act.activation(WW, WW, ACT.Tanh).then_inc(s["exped"], 1)
                    act.wait_ge(s["exped"], 1)
                    act.activation(WW, WW, ACT.Exp).then_inc(s["exped"], 1)

                @block.vector
                def _(dve):
                    c = Chain(dve, s["vec"])
                    dve.wait_ge(s["scored"], 1)
                    for h in range(2):
                        c.mark(dve.tensor_tensor(ww[:, 4 * h:4 * h + 4, :], PS[:, h, :].rearrange("p (t k) -> p t k", t=4),
                                                 quad(cst("lw")), ALU.mult))
                    dve.wait_ge(s["exped"], 2)
                    dve.tensor_tensor(ww, ww, cst("off").unsqueeze(1).broadcast_to([P, TILES, P]), ALU.mult)\
                        .then_inc(s["weighed"], 1)
                    dve.wait_ge(s["mixed"], 1)
                    c.step(dve.tensor_scalar(SM, PS[:, 4, 0:TILES], 1e-7, None, ALU.add))
                    c.step(dve.reciprocal(SM, SM))
                    for t in range(TILES):
                        c.mark(dve.scalar_tensor_tensor(out=X[:, t, :], in0=PS[:, 2 + t // 4, (t % 4) * P:(t % 4 + 1) * P],
                                                        scalar=SM[:, t:t + 1], in1=X[:, t, :], op0=ALU.mult, op1=ALU.add))
                    c.join()

        def l0_ffn(counted):
            normalize(X, XN, HT, 1e-5, counted=counted)
            route(HT, w("L0f_router"), 64, 6, "sigmoid", 48)
            G2 = BIG[1][:, 0:TOK]
            GA = BIG[0][:, 3072:3584].bitcast(BF16)
            GB = BIG[0][:, 3584:4096].bitcast(BF16)
            GF = BIG[1][:, TOK:2 * TOK]
            R1 = BIG[1][:, 2 * TOK:3 * TOK]
            T3 = BIG[1][:, 3 * TOK:3 * TOK + 512].bitcast(BF16)
            T1 = BIG[1][:, 3 * TOK + 512:4 * TOK].bitcast(BF16)
            n = 4 * P
            W1 = [BIG[0][:, u * 512:u * 512 + n] for u in range(2)]
            W2 = [BIG[0][:, 1024 + u * 512:1024 + u * 512 + n] for u in range(2)]
            HID = [BIG[2][:, c * TOK:(c + 1) * TOK] for c in range(2)]
            SH = [BIG[3][:, c * TOK:(c + 1) * TOK] for c in range(2)]
            YT = BIG[1][:, 0:TOK]
            halves = lambda a: a.rearrange("p (a b) -> p a b", a=2)
            with phase("vec", "turned", "loaded", "made", "shared", "opened") as (block, s):
                @block.sync
                def _(sp):
                    for u in range(2):
                        for name, buf in (("L0f_w1", W1), ("L0f_w2", W2)):
                            sp.dma_start(buf[u], d[name][:, u * n:(u + 1) * n]).then_inc(s["loaded"], 16)
                    sp.wait_ge(s["loaded"], 64)

                @block.scalar
                def _(act):
                    for c in range(2):
                        act.wait_ge(s["made"], c + 1)
                        act.activation(halves(SH[c]), PS[:, 2 + 2 * c:4 + 2 * c, :], ACT.Gelu_apprx_tanh)\
                           .then_inc(s["shared"], 1)

                @block.tensor
                def _(pe):
                    pe.wait_ge(s["vec"], 2)
                    for t in range(TILES):
                        mm = pe.transpose(PS[:, t // 4, (t % 4) * P:(t % 4 + 1) * P], G2[:, t * P:(t + 1) * P], ident)
                    mm.then_inc(s["turned"], 1)
                    for c in range(2):
                        for h in range(2):
                            mm = pe.matmul(PS[:, 2 + 2 * c + h, :], w("L0f_sw1")[:, c * P:(c + 1) * P],
                                           HT[:, h * HALF:(h + 1) * HALF], start=True, stop=True)
                        mm.then_inc(s["made"], 1)
                    for c in range(2):
                        pe.wait_ge(s["shared"], c + 1)
                        for h in range(2):
                            pe.matmul(PS[:, 6 + h, :], w("L0f_sw2")[:, c * P:(c + 1) * P], SH[c][:, h * HALF:(h + 1) * HALF],
                                      start=c == 0, stop=False, skip_group_check=True).then_inc(s["opened"], 1)
                    pe.wait_ge(s["opened"], 4)

                @block.vector
                def _(dve):
                    c = Chain(dve, s["vec"])
                    g2 = G2.rearrange("p (t c e) -> p t c e", t=TILES, c=2)
                    for k in range(2):
                        c.mark(dve.tensor_copy(g2[:, :, k, :], GATE[:, :, :]))
                    dve.wait_ge(s["turned"], 1)
                    c.step(dve.tensor_copy(GF, PS[:, 0:2, :].rearrange("p a b -> p (a b)")))
                    c.step(dve.tensor_copy(T1, GF))
                    c.step(dve.tensor_tensor(R1, GF, T1, ALU.subtract))
                    c.step(dve.tensor_copy(T3, R1))
                    c.step(dve.tensor_tensor(R1, R1, T3, ALU.subtract))
                    c.mark(dve.memset(GB[:, :], 0.0))
                    c.mark(dve.tensor_copy(GA[0:64, :], T1[0:64, :]))
                    c.mark(dve.tensor_copy(GA[64:128, :], T3[64:128, :]))
                    c.join()
                    c.step(dve.tensor_copy(GB[0:64, :], R1[0:64, :]))

            with phase("loaded_even", "loaded_odd", "made", "hfree", "acted", "picked", "ready", "ymade",
                       "copied", "turned", "added") as (block, s):
                loaded = (s["loaded_even"], s["loaded_odd"])
                UNITS, PAIRS = 8, 4

                @block.sync
                def _(sp):
                    for u in range(2):
                        sp.sem_inc(loaded[u], 32)
                    with sp.Fori(1, UNITS // 2) as i:
                        for u in range(2):
                            e = i * 2 + u
                            sp.wait_ge(s["ymade"], e * 8 + 8)
                            for name, buf in (("L0f_w1", W1), ("L0f_w2", W2)):
                                sp.dma_start(buf[u], d[name][:, bass.ts(e, n)]).then_inc(loaded[u], 16)

                @block.tensor
                def _(pe):
                    pe.sem_inc(s["ymade"], 16)
                    def outputs(u, c):
                        for h in range(2):
                            pe.matmul(PS[:, 6 + h, :], W2[u][:, c * P:(c + 1) * P], HID[c % 2][:, h * HALF:(h + 1) * HALF],
                                      start=False, stop=False, skip_group_check=True).then_inc(s["ymade"], 1)

                    def step(i, u, c, before=None):
                        pair = (i * 2 + u) * PAIRS + c
                        if c == 0:
                            pe.wait_ge(loaded[u], i * 32 + 32)
                        pe.wait_ge(s["hfree"], pair + 1)
                        for h in range(2):
                            mm = pe.matmul(PS[:, 2 * (c % 2) + h, :], W1[u][:, c * P:(c + 1) * P],
                                           HT[:, h * HALF:(h + 1) * HALF], start=True, stop=True)
                        mm.then_inc(s["made"], 1)
                        pe.wait_ge(s["ready"], pair + 1)
                        if before is not None:
                            outputs(*before)
                        for h in range(2):
                            for k, G in enumerate((GA, GB)):
                                mm = pe.matmul(PS[:, 4 + h, :], pickb[:, bass.ts(pair, P)],
                                               G[:, h * HALF:(h + 1) * HALF], start=k == 0, stop=k == 1)
                        mm.then_inc(s["picked"], 1)

                    step(0, 0, 0)
                    order = [(u, c) for u in range(2) for c in range(PAIRS)]
                    with pe.Fori(0, UNITS // 2 - 1) as i:
                        for a, b in zip(order, order[1:]):
                            step(i, *b, before=a)
                        step(i + 1, 0, 0, before=order[-1])
                    for a, b in zip(order, order[1:]):
                        step(UNITS // 2 - 1, *b, before=a)
                    pe.wait_ge(s["ready"], UNITS * PAIRS + 1)
                    outputs(*order[-1])
                    for t in range(TILES):
                        if t == 0:
                            pe.wait_ge(s["copied"], 1)
                        mm = pe.transpose(PS[:, t // 4, (t % 4) * P:(t % 4 + 1) * P], YT[:, t * P:(t + 1) * P], ident)
                    mm.then_inc(s["turned"], 1)

                @block.scalar
                def _(act):
                    act.sem_inc(s["hfree"], 2)
                    with act.Fori(0, 16) as i:
                        for c in range(2):
                            pair = i * 2 + c
                            act.wait_ge(s["made"], pair + 1)
                            act.wait_ge(s["ymade"], pair * 2 + 14)
                            act.activation(halves(HID[c]), PS[:, 2 * c:2 * c + 2, :], ACT.Gelu_apprx_tanh)\
                               .then_inc(s["acted"], 1)
                            act.wait_ge(s["acted"], pair + 1)
                            act.sem_inc(s["hfree"], 1)

                @block.vector
                def _(dve):
                    dve.sem_inc(s["ready"], 1)
                    with dve.Fori(0, 16) as i:
                        for c in range(2):
                            pair = i * 2 + c
                            dve.wait_ge(s["acted"], pair + 1)
                            dve.wait_ge(s["picked"], pair + 1)
                            dve.tensor_tensor(halves(HID[c]), halves(HID[c]), PS[:, 4:6, :], ALU.mult)\
                                .then_inc(s["ready"], 1)
                    dve.wait_ge(s["ymade"], 16 + 2 * 32)
                    dve.tensor_copy(halves(YT), PS[:, 6:8, :]).then_inc(s["copied"], 1)
                    dve.wait_ge(s["turned"], 1)
                    x = X[:, :, :].rearrange("p (a t) f -> p a (t f)", a=2)
                    dve.tensor_tensor(x, x, PS[:, 0:2, :], ALU.add).then_inc(s["added"], 1)
                    dve.wait_ge(s["added"], 1)

        def l1_xattn(counted):
            with phase("zeroed") as (block, s):
                @block.gpsimd
                def _(pool):
                    pool.memset(XR[:, :, :], 0.0).then_inc(s["zeroed"], 1)
            normalize_and_project((QT, w("L1xs_q"), HT, w("c_L1xs_bq"), HD ** -0.5),
                                  (KT, w("L1xs_k"), CT, w("c_L1xs_bk"), 1.0), (CT, w("L1xs_v"), row("L1xs_v")), counted)
            attend(w("L1xs_o"), XR, "src", row("L1xs_o"))
            project([(QT, w("L1xt_q"), HT, w("c_L1xt_bq"), HD ** -0.5), (KT, w("L1xt_k"), HT, w("c_L1xt_bk"), 1.0)],
                    (HT, w("L1xt_v"), row("L1xt_v")))
            attend(w("L1xt_o"), XR, "tgt", row("L1xt_o"))
            turn(XR, QT)
            N = 4 * BATCH
            GX = BIG[0]
            gx = GX[:, :].rearrange("p (s g b) -> p g b s", s=SEQ, g=4)
            HS = BIG[1][:, 0:(SEQ + 1) * BATCH]
            G = [BIG[1][:, 1280 + i * 128:1280 + i * 128 + 5 * BATCH] for i in range(2)]
            T = BIG[1][:, 1600:1600 + 2 * BATCH]
            TC = BIG[1][:, 1664:1664 + BATCH]
            WH = BIG[1][:, 2048:2560]
            with phase("made", "evac", "zeroed") as (block, s):
                @block.tensor
                def _(pe):
                    for g in range(4):
                        for h in range(2):
                            cols = slice(h * HALF, (h + 1) * HALF)
                            o = PS[:, 2 * g + h, :]
                            pe.matmul(o, w("L1x_wx")[:, g * P:(g + 1) * P], HT[:, cols], start=True, stop=False)
                            pe.matmul(o, w("L1x_wc")[:, g * P:(g + 1) * P], QT[:, cols], start=False, stop=True)\
                              .then_inc(s["made"], 1)

                @block.gpsimd
                def _(pool):
                    pool.memset(HS[:, 0:BATCH], 0.0).then_inc(s["zeroed"], 1)
                    pool.memset(G[0][:, 48:64], 0.0).then_inc(s["zeroed"], 1)
                    for g in range(4):
                        cols = slice(g * P, (g + 1) * P)
                        pool.tensor_scalar(WH[:, cols], w("L1x_wh")[:, cols], 1.0 if g == 2 else 0.5, None, ALU.mult)\
                            .then_inc(s["zeroed"], 1)

                @block.vector
                def _(dve):
                    for g in range(4):
                        for h in range(2):
                            dve.wait_ge(s["made"], 2 * g + h + 1)
                            dve.tensor_scalar(gx[:, g, h * 8:h * 8 + 8, :],
                                              PS[:, 2 * g + h, :].rearrange("p (b s) -> p b s", b=8),
                                              w("c_L1x_lstm_b")[:, g:g + 1], 2.0 if g == 2 else 1.0, ALU.add, ALU.mult)\
                                .then_inc(s["evac"], 1)
                    dve.wait_ge(s["evac"], 8)

            with phase("gates", "gfree", "acted", "out_gate", "opened", "cell", "tanhed", "hidden") as (block, s):
                @block.tensor
                def _(pe):
                    with pe.Fori(0, SEQ // 2) as i:
                        for u in range(2):
                            step = i * 2 + u
                            first, last = PS[:, 2 * u, 0:3 * BATCH], PS[:, 2 * u + 1, 0:BATCH]
                            pe.wait_ge(s["gfree"], step + 1)
                            pe.matmul(first, ident, GX[:, bass.ds(step * N, 3 * BATCH)], start=True, stop=False,
                                      skip_group_check=True)
                            pe.matmul(last, ident, GX[:, bass.ds(step * N + 3 * BATCH, BATCH)], start=True, stop=False,
                                      skip_group_check=True)
                            pe.wait_ge(s["hidden"], step + 1)
                            for g in range(4):
                                o = first[:, g * BATCH:(g + 1) * BATCH] if g < 3 else last
                                mm = pe.matmul(o, WH[:, g * P:(g + 1) * P], HS[:, bass.ts(step, BATCH)],
                                               start=False, stop=g >= 2, skip_group_check=True)
                                if g == 2:
                                    mm.then_inc(s["gates"], 1)
                            mm.then_inc(s["out_gate"], 1)

                @block.scalar
                def _(act):
                    act.sem_inc(s["gfree"], 2)
                    with act.Fori(0, SEQ // 2) as i:
                        for u in range(2):
                            step = i * 2 + u
                            act.wait_ge(s["gates"], step + 1)
                            act.activation(G[u][:, 0:48], PS[:, 2 * u, 0:48], ACT.Tanh, scale=0.5).then_inc(s["acted"], 1)
                            act.wait_ge(s["out_gate"], step + 1)
                            act.activation(G[u][:, 64:80], PS[:, 2 * u + 1, 0:BATCH], ACT.Tanh, scale=0.5)\
                                .then_inc(s["opened"], 1)
                            act.wait_ge(s["cell"], step * 2 + 2)
                            act.activation(TC, G[1 - u][:, 48:64], ACT.Tanh, scale=0.5).then_inc(s["tanhed"], 1)
                            act.wait_ge(s["opened"], step + 1)
                            act.sem_inc(s["gfree"], 1)

                @block.vector
                def _(dve):
                    dve.sem_inc(s["hidden"], 1)
                    with dve.Fori(0, SEQ // 2) as i:
                        for u in range(2):
                            step = i * 2 + u
                            dve.wait_ge(s["acted"], step + 1)
                            dve.scalar_tensor_tensor(out=T, in0=G[u][:, 0:32], scalar=1.0, in1=G[u][:, 32:64],
                                                     op0=ALU.add, op1=ALU.mult).then_inc(s["cell"], 1)
                            dve.wait_ge(s["cell"], step * 2 + 1)
                            dve.scalar_tensor_tensor(out=G[1 - u][:, 48:64], in0=T[:, BATCH:2 * BATCH], scalar=0.5,
                                                     in1=T[:, 0:BATCH], op0=ALU.mult, op1=ALU.add)\
                                .then_inc(s["cell"], 1)
                            dve.wait_ge(s["tanhed"], step + 1)
                            dve.scalar_tensor_tensor(out=HS[:, bass.ts(step + 1, BATCH)], in0=G[u][:, 64:80],
                                                     scalar=1.0, in1=TC, op0=ALU.add, op1=ALU.mult)\
                                .then_inc(s["hidden"], 1)

            RR = [BIG[2][:, c * TOK:(c + 1) * TOK] for c in range(4)]
            with phase("made", "evac", "ymade", "based", "added") as (block, s):
                @block.tensor
                def _(pe):
                    for c in range(4):
                        if c >= 2:
                            pe.wait_ge(s["evac"], 2 * (c - 1))
                        for h in range(2):
                            pe.matmul(PS[:, 2 * (c % 2) + h, :], w("L1x_w1")[:, c * P:(c + 1) * P],
                                      HS[:, BATCH + h * HALF:BATCH + (h + 1) * HALF], start=True, stop=True)\
                              .then_inc(s["made"], 1)
                    pe.wait_ge(s["evac"], 8)
                    for t in range(TILES):
                        for c in range(4):
                            mm = pe.matmul(PS[:, 4 + t // 4, (t % 4) * P:(t % 4 + 1) * P], RR[c][:, t * P:(t + 1) * P],
                                           w("L1x_w2")[:, c * P:(c + 1) * P], start=c == 0, stop=c == 3)
                        mm.then_inc(s["ymade"], 1)

                @block.scalar
                def _(act):
                    for c in range(4):
                        for h in range(2):
                            act.wait_ge(s["made"], 2 * c + h + 1)
                            o = RR[c].rearrange("p (b s) -> p s b", b=BATCH)[:, h * 32:(h + 1) * 32, :]
                            act.activation(o, PS[:, 2 * (c % 2) + h, :].rearrange("p (s b) -> p s b", b=BATCH), ACT.Relu,
                                           scale=0.5, bias=w("c_L1x_b1")[:, c:c + 1]).then_inc(s["evac"], 1)

                @block.gpsimd
                def _(pool):
                    pool.tensor_tensor(X[:, :, :], X[:, :, :],
                                       row("L1x_b2").unsqueeze(1).broadcast_to([P, TILES, P]), ALU.add)\
                        .then_inc(s["based"], 1)

                @block.vector
                def _(dve):
                    dve.wait_ge(s["based"], 1)
                    for h in range(2):
                        dve.wait_ge(s["ymade"], 4 * h + 4)
                        x = X[:, 4 * h:4 * h + 4, :].rearrange("p t f -> p (t f)")
                        dve.tensor_tensor(x, x, PS[:, 4 + h, :], ALU.add).then_inc(s["added"], 1)
                    dve.wait_ge(s["added"], 2)


        EXTRA = sb("EXTRA", [P, 4 * TOK])
        W4 = BIG[3]
        delta_loaded = nc.alloc_semaphore("delta_loaded")
        tiles = lambda a: a.rearrange("p (t f) -> p t f", t=TILES)
        halves = lambda a: a.rearrange("p (a b) -> p a b", a=2)
        half = lambda a, g: a[:, g * HALF:(g + 1) * HALF]
        square = lambda g, t: PS[:, g, (t % 4) * P:(t % 4 + 1) * P]
        each = lambda a: a.unsqueeze(1).broadcast_to([P, TILES, P])

        def delta_heads():
            H, LV = 8, 5
            part = lambda buf, i: buf[:, i * TOK:(i + 1) * TOK]
            SIL = BIG[0][:, :].rearrange("p (t n f) -> p t n f", t=TILES, n=4)
            QH, KH, DL, DA = (part(BIG[1], i) for i in range(4))
            LL, AT, XX, XXT = (part(BIG[2], i) for i in range(4))
            WO, YY, CC, WW = (part(EXTRA, i) for i in range(4))
            GU, GW = QT[:, :], KT[:, :]
            OO = XN[:, :, :]
            small = CS[:, C_AT["pick"][0]:C_AT["pick"][0] + 4096]
            steps = lambda a: a.rearrange("p (t h) -> p t h", t=TILES)
            LG = small[:, 0:128].rearrange("p (t n) -> p t n", t=TILES)
            BETA, G, Z, E1, NA, U, SP, T1 = (steps(small[:, 128 + 64 * i:192 + 64 * i]) for i in range(8))
            RS = small[:, 700:716].rearrange("p (t n) -> p t n", t=TILES)
            RO = small[:, 720:728]
            EA = small[:, 730:738]
            SQ2 = small[:, 1024:3072].rearrange("p (t n f) -> p t n f", t=TILES, n=2)
            TABLE_STEPS = 15

            def table_logits(pe, s):
                for t in range(TILES):
                    a = W_AT["L3a_b"][0]
                    mm = pe.matmul(PS[:, 0, t * 16:(t + 1) * 16], HT[:, t * P:(t + 1) * P], WT[:, a:a + 16],
                                   start=True, stop=True)
                mm.then_inc(s["table_logits"], 1)

            def table_functions(act, s):
                act.wait_ge(s["table_logits"], 1)
                act.activation(LG, PS[:, 0, 0:128].rearrange("p (t n) -> p t n", t=TILES), ACT.Copy)\
                   .then_inc(s["table_act"], 1)
                act.wait_ge(s["table_act"], 1)
                act.activation(BETA, LG[:, :, 0:8], ACT.Sigmoid).then_inc(s["table_act"], 1)
                act.activation(EA, row("L3a_Alog"), ACT.Exp).then_inc(s["table_act"], 1)
                act.wait_ge(s["table_vec"], 2)
                act.activation(E1, NA, ACT.Exp).then_inc(s["table_act"], 1)
                act.wait_ge(s["table_vec"], 3)
                act.activation(SP, U, ACT.Ln).then_inc(s["table_act"], 1)

            def table_decays(dve, s):
                c = Chain(dve, s["table_vec"])
                wide = lambda a: a.unsqueeze(1).broadcast_to([P, TILES, 8])
                dve.wait_ge(s["table_act"], 1)
                c.step(dve.tensor_tensor(Z, LG[:, :, 8:16], wide(row("L3a_dt")), ALU.add))
                c.step(dve.scalar_tensor_tensor(out=NA, in0=Z, scalar=-1.0, in1=Z, op0=ALU.mult, op1=ALU.min))
                dve.wait_ge(s["table_act"], 4)
                c.step(dve.tensor_scalar(U, E1, 1.0, None, ALU.add))
                dve.wait_ge(s["table_act"], 5)
                c.step(dve.tensor_scalar(T1, E1, -0.25, 1.0 / 3.0, ALU.mult, ALU.add))
                c.step(dve.tensor_tensor(T1, T1, E1, ALU.mult))
                c.step(dve.tensor_scalar(T1, T1, -0.5, None, ALU.add))
                c.step(dve.tensor_tensor(T1, T1, E1, ALU.mult))
                c.step(dve.scalar_tensor_tensor(out=T1, in0=T1, scalar=1.0, in1=E1, op0=ALU.add, op1=ALU.mult))
                c.step(dve.tensor_scalar(U, E1, 0.01, None, ALU.is_lt))
                c.step(dve.tensor_tensor(T1, T1, U, ALU.mult))
                c.step(dve.tensor_scalar(U, U, -1.0, 1.0, ALU.mult, ALU.add))
                c.step(dve.tensor_tensor(SP, SP, U, ALU.mult))
                c.step(dve.tensor_tensor(SP, SP, T1, ALU.add))
                c.step(dve.scalar_tensor_tensor(out=SP, in0=Z, scalar=0.0, in1=SP, op0=ALU.max, op1=ALU.add))
                c.step(dve.scalar_tensor_tensor(out=G, in0=SP, scalar=-1.0, in1=wide(EA), op0=ALU.mult, op1=ALU.mult))
                assert c.n == TABLE_STEPS

            per = dict(projected=8, silued=8, squared=1, summed=1, qk_rooted=1, q_scaled=1, k_scaled=1,
                       spread=1, pairs=2, decayed=2, turned=2, tcopied=2, weighed=2, gram=2, lower=2, level0=2,
                       other=2, xcopied=2, inner=1, attn=1, attn_masked=1, masked=LV, ymade=8, ycopied=8,
                       x_corrected=6, t_corrected=8, x_subbed=6, t_subbed=8, zmade=2, zcopied=2, wmade=2, wcopied=2,
                       vmade=2, delta=2, mixed=2, gated=1, mean_squares=1, o_rooted=1, onormed=2, oturned=2,
                       ocopied=2, out=2, added=2)
            FRONT, REST = 5, 20
            with phase(*per, "vec", "table_logits", "table_act", "table_vec") as (block, s):
                def waits(eng, h):
                    return lambda name, n: eng.wait_ge(s[name], h * per[name] + n)

                def all_heads(eng, head):
                    with eng.Fori(0, H - 1) as h:
                        head(h, True)
                    head(H - 1, False)

                @block.tensor
                def _(pe):
                    def project_tile(h, t):
                        if t >= 2:
                            waits(pe, h)("silued", t - 1)
                        pe.matmul(PS[:, 6 + t % 2, :], HT[:, t * P:(t + 1) * P], W4[:, bass.ts(h, HALF)],
                                  start=True, stop=True).then_inc(s["projected"], 1)

                    def pairs(h):
                        waits(pe, h)("spread", 1)
                        waits(pe, h)("silued", TILES)
                        for t in range(TILES):
                            mm = pe.matmul(square(6 + t // 4, t), tiles(GU)[:, t, :], cst("tri_str"), start=True, stop=True)
                        mm.then_inc(s["pairs"], 1)

                    def head(h, more):
                        at = waits(pe, h)
                        at("k_scaled", 1)
                        for t in range(TILES):
                            mm = pe.transpose(square(t // 4, t), SIL[:, t, 1, :], ident)
                        mm.then_inc(s["turned"], 1)
                        at("decayed", 1)
                        for g in range(2):
                            mm = pe.matmul(PS[:, 6 + g, :], cst("tri_str"), half(GU, g), start=True, stop=True)
                        mm.then_inc(s["pairs"], 1)
                        at("tcopied", 1)
                        at("q_scaled", 1)
                        for g in range(2):
                            for t in range(4 * g, 4 * g + 4):
                                c = slice(t * P, (t + 1) * P)
                                mm = pe.matmul(square(4 + g, t), KH[:, c], KH[:, c], start=True, stop=True)
                            mm.then_inc(s["gram"], 1)
                        for t in range(TILES):
                            mm = pe.transpose(square(2 + t // 4, t), SIL[:, t, 0, :], ident)
                        mm.then_inc(s["turned"], 1)
                        for g in range(2):
                            at("level0", g + 1)
                            for t in range(4 * g, 4 * g + 4):
                                mm = pe.transpose(square(g, t), tiles(XX)[:, t, :], ident)
                            mm.then_inc(s["other"], 1)
                        at("decayed", 2)
                        at("tcopied", 2)
                        for t in range(TILES):
                            c = slice(t * P, (t + 1) * P)
                            mm = pe.matmul(square(6 + t // 4, t), KH[:, c], QH[:, c], start=True, stop=True)
                        mm.then_inc(s["inner"], 1)
                        for l in range(1, LV):
                            at("masked", l)
                            for g in range(2):
                                if l > 1:
                                    at("t_subbed", 2 * (l - 2) + g + 1)
                                else:
                                    at("xcopied", g + 1)
                                for t in range(4 * g, 4 * g + 4):
                                    mm = pe.matmul(square(g, t), tiles(CC)[:, t, :], tiles(XXT)[:, t, :],
                                                   start=True, stop=True)
                                mm.then_inc(s["ymade"], 1)
                            for g in range(2):
                                at("ycopied", 2 * (l - 1) + g + 1)
                                if l > 1:
                                    at("x_subbed", 2 * (l - 2) + g + 1)
                                for t in range(4 * g, 4 * g + 4):
                                    mm = pe.matmul(square(4 + g, t), tiles(XX)[:, t, :], tiles(YY)[:, t, :],
                                                   start=True, stop=True)
                                mm.then_inc(s["t_corrected"], 1)
                                if l < LV - 1:
                                    for t in range(4 * g, 4 * g + 4):
                                        mm = pe.matmul(square(2 + g, t), tiles(YY)[:, t, :], tiles(XX)[:, t, :],
                                                       start=True, stop=True)
                                    mm.then_inc(s["x_corrected"], 1)
                        for g in range(2):
                            at("t_subbed", 2 * (LV - 2) + g + 1)
                            for t in range(4 * g, 4 * g + 4):
                                mm = pe.matmul(square(g, t), tiles(XXT)[:, t, :], SIL[:, t, 2, :], start=True, stop=True)
                            mm.then_inc(s["zmade"], 1)
                        at("masked", LV)
                        for g in range(2):
                            for t in range(4 * g, 4 * g + 4):
                                mm = pe.matmul(square(2 + g, t), tiles(CC)[:, t, :], tiles(XXT)[:, t, :],
                                               start=True, stop=True)
                            mm.then_inc(s["wmade"], 1)
                        if more:
                            at("attn", 1)
                            for t in range(3):
                                project_tile(h + 1, t)
                        for g in range(2):
                            at("zcopied", g + 1)
                            at("wcopied", g + 1)
                            for t in range(4 * g, 4 * g + 4):
                                mm = pe.matmul(square(4 + g, t), tiles(WW)[:, t, :], tiles(YY)[:, t, :],
                                               start=True, stop=True)
                            mm.then_inc(s["vmade"], 1)
                        if more:
                            project_tile(h + 1, 3)
                            project_tile(h + 1, 4)
                        at("attn_masked", 1)
                        for g in range(2):
                            at("delta", g + 1)
                            for t in range(4 * g, 4 * g + 4):
                                mm = pe.matmul(square(g, t), tiles(AT)[:, t, :], tiles(YY)[:, t, :], start=True, stop=True)
                            mm.then_inc(s["mixed"], 1)
                        if more:
                            for t in range(5, TILES):
                                project_tile(h + 1, t)
                            pairs(h + 1)
                        for g in range(2):
                            at("onormed", g + 1)
                            for t in range(4 * g, 4 * g + 4):
                                mm = pe.transpose(square(2 + g, t), OO[:, t, :], ident)
                            mm.then_inc(s["oturned"], 1)
                        for g in range(2):
                            at("ocopied", g + 1)
                            for t in range(4 * g, 4 * g + 4):
                                mm = pe.matmul(square(4 + g, t), tiles(XX)[:, t, :], WO[:, bass.ts(h, P)],
                                               start=True, stop=True)
                            mm.then_inc(s["out"], 1)

                    table_logits(pe, s)
                    pe.wait_ge(delta_loaded, 32)
                    for t in range(TILES):
                        project_tile(0, t)
                    pairs(0)
                    all_heads(pe, head)

                @block.scalar
                def _(act):
                    def silu(h, first, last):
                        for t in range(first, last):
                            waits(act, h)("projected", t + 1)
                            act.activation(BIG[0][:, t * HALF:(t + 1) * HALF], PS[:, 6 + t % 2, :], ACT.Silu)\
                                .then_inc(s["silued"], 1)

                    def root_and_decay(h):
                        waits(act, h)("summed", 1)
                        act.activation(RS, RS, ACT.Sqrt).then_inc(s["qk_rooted"], 1)
                        waits(act, h)("pairs", 1)
                        act.activation(halves(DL), PS[:, 6:8, :], ACT.Exp).then_inc(s["decayed"], 1)

                    def head(h, more):
                        at = waits(act, h)
                        at("turned", 1)
                        act.activation(halves(KH), PS[:, 0:2, :], ACT.Copy).then_inc(s["tcopied"], 1)
                        at("pairs", 2)
                        act.activation(halves(DA), PS[:, 6:8, :], ACT.Exp).then_inc(s["decayed"], 1)
                        at("turned", 2)
                        act.activation(halves(QH), PS[:, 2:4, :], ACT.Copy).then_inc(s["tcopied"], 1)
                        for g in range(2):
                            at("other", g + 1)
                            act.activation(half(XXT, g), PS[:, g, :], ACT.Copy).then_inc(s["xcopied"], 1)
                        for l in range(1, LV):
                            for g in range(2):
                                at("ymade", 2 * (l - 1) + g + 1)
                                act.activation(half(YY, g), PS[:, g, :], ACT.Copy).then_inc(s["ycopied"], 1)
                        if more:
                            act.activation(idle[:, :], idle[:, :], ACT.Silu)
                        for g in range(2):
                            at("zmade", g + 1)
                            act.activation(half(YY, g), PS[:, g, :], ACT.Copy).then_inc(s["zcopied"], 1)
                        for g in range(2):
                            at("wmade", g + 1)
                            act.activation(half(WW, g), PS[:, 2 + g, :], ACT.Copy).then_inc(s["wcopied"], 1)
                        if more:
                            silu(h + 1, 0, TILES)
                        at("mean_squares", 1)
                        act.activation(RO, RO, ACT.Sqrt).then_inc(s["o_rooted"], 1)
                        for g in range(2):
                            at("oturned", g + 1)
                            act.activation(half(XX, g), PS[:, 2 + g, :], ACT.Copy).then_inc(s["ocopied"], 1)
                        if more:
                            root_and_decay(h + 1)

                    table_functions(act, s)
                    silu(0, 0, TILES)
                    root_and_decay(0)
                    all_heads(act, head)

                @block.gpsimd
                def _(pool):
                    def spread(h):
                        pool.tensor_tensor(tiles(GU), each(cst("tri_inc")),
                                           G[:, :, bass.ds(h, 1)].broadcast_to([P, TILES, P]), ALU.mult)\
                            .then_inc(s["spread"], 1)

                    def square_low(h):
                        waits(pool, h)("silued", 4)
                        pool.tensor_tensor(SQ2[:, 0:4], SIL[:, 0:4, 0:2, :], SIL[:, 0:4, 0:2, :], ALU.mult)\
                            .then_inc(s["squared"], 1)

                    def gates(h):
                        waits(pool, h)("silued", TILES)
                        pool.tensor_tensor(tiles(GW), SIL[:, :, 3, :], each(row("L3a_norm")), ALU.mult)\
                            .then_inc(s["gated"], 1)

                    def head(h, more):
                        at = waits(pool, h)
                        at("decayed", 1)
                        for g in range(2):
                            b = BETA[:, 4 * g:4 * g + 4, bass.ds(h, 1)].broadcast_to([P, 4, P])
                            pool.tensor_tensor(tiles(DL)[:, 4 * g:4 * g + 4, :], tiles(DL)[:, 4 * g:4 * g + 4, :], b,
                                               ALU.mult).then_inc(s["weighed"], 1)
                        for l in range(1, LV + 1):
                            if l == 1:
                                at("lower", 2)
                            else:
                                at("ymade", 2 * (l - 1))
                            a = C_AT["level"][0] + l * P
                            pool.tensor_tensor(tiles(CC), tiles(LL), each(CS[:, a:a + P]), ALU.mult)\
                                .then_inc(s["masked"], 1)
                            if l == 2:
                                at("attn", 1)
                                pool.tensor_tensor(tiles(AT), tiles(AT), each(cst("tri_inc")), ALU.mult)\
                                    .then_inc(s["attn_masked"], 1)
                        if more:
                            spread(h + 1)
                            square_low(h + 1)
                            at("onormed", 2)
                            gates(h + 1)

                    pool.wait_ge(s["table_vec"], TABLE_STEPS)
                    spread(0)
                    square_low(0)
                    gates(0)
                    all_heads(pool, head)

                @block.vector
                def _(dve):
                    col = lambda a: a.broadcast_to([P, TILES, P])
                    beta = lambda h: col(BETA[:, :, bass.ds(h, 1)])

                    def square_high(h):
                        waits(dve, h)("silued", TILES)
                        return dve.tensor_tensor(SQ2[:, 4:8], SIL[:, 4:8, 0:2, :], SIL[:, 4:8, 0:2, :], ALU.mult)

                    def sum_low(h, c):
                        waits(dve, h)("squared", 1)
                        c.mark(dve.tensor_reduce(RS[:, 0:4, :], SQ2[:, 0:4], AX.X, ALU.add))

                    def scale(h, c):
                        at = waits(dve, h)
                        c.step(dve.tensor_reduce(RS[:, 4:8, :], SQ2[:, 4:8], AX.X, ALU.add))
                        dve.tensor_scalar(RS, RS, 1e-6, None, ALU.add).then_inc(s["summed"], 1)
                        at("qk_rooted", 1)
                        c.step(dve.reciprocal(RS, RS))
                        dve.tensor_tensor(SIL[:, :, 1, :], SIL[:, :, 1, :], col(RS[:, :, 1:2]), ALU.mult)\
                            .then_inc(s["k_scaled"], 1)

                    def scale_q(h, c):
                        dve.scalar_tensor_tensor(out=SIL[:, :, 0, :], in0=SIL[:, :, 0, :], scalar=float(P) ** -0.5,
                                                 in1=col(RS[:, :, 0:1]), op0=ALU.mult, op1=ALU.mult)\
                            .then_inc(s["q_scaled"], 1)
                        c.mark(dve.tensor_tensor(SIL[:, :, 2, :], SIL[:, :, 2, :], beta(h), ALU.mult))

                    def head(h, more):
                        at = waits(dve, h)
                        c = Chain(dve, s["vec"], h * (FRONT + REST) + FRONT)
                        a = C_AT["level"][0]
                        for g in range(2):
                            at("gram", g + 1)
                            at("weighed", g + 1)
                            dve.tensor_tensor(half(LL, g), PS[:, 4 + g, :], half(DL, g), ALU.mult).then_inc(s["lower"], 1)
                            at("lower", g + 1)
                            quad = lambda m: m.unsqueeze(1).broadcast_to([P, 4, P])
                            four = lambda m: half(m, g).rearrange("p (t f) -> p t f", t=4)
                            c.step(dve.tensor_tensor(four(XX), four(LL), quad(CS[:, a:a + P]), ALU.mult))
                            dve.tensor_tensor(four(XX), quad(ident), four(XX), ALU.subtract).then_inc(s["level0"], 1)
                        at("inner", 1)
                        dve.tensor_tensor(halves(AT), PS[:, 6:8, :], halves(DA), ALU.mult).then_inc(s["attn"], 1)
                        at("level0", 2)
                        at("xcopied", 2)
                        for l in range(1, LV):
                            for g in range(2):
                                n = 2 * (l - 1) + g
                                at("t_corrected", n + 1)
                                if l > 1:
                                    at("t_subbed", n - 1)
                                dve.tensor_tensor(half(XXT, g), half(XXT, g), PS[:, 4 + g, :], ALU.subtract)\
                                    .then_inc(s["t_subbed"], 1)
                                if l < LV - 1:
                                    at("x_corrected", n + 1)
                                    if l > 1:
                                        at("x_subbed", n - 1)
                                    dve.tensor_tensor(half(XX, g), half(XX, g), PS[:, 2 + g, :], ALU.subtract)\
                                        .then_inc(s["x_subbed"], 1)
                        for g in range(2):
                            at("vmade", g + 1)
                            dve.tensor_tensor(half(YY, g), half(YY, g), PS[:, 4 + g, :], ALU.subtract).then_inc(s["delta"], 1)
                        if more:
                            sum_low(h + 1, c)
                        for g in range(2):
                            at("mixed", g + 1)
                            for t in range(4 * g, 4 * g + 4):
                                c.mark(dve.bn_stats(stats[:, t, :], square(t // 4, t)))
                        c.join()
                        dve.memset(small[:, 740:741], 0.0)
                        for t in range(TILES):
                            c.mark(dve.bn_aggr(mv[:, t, :], stats[:, t, :]))
                        c.join()
                        c.step(dve.tensor_tensor(RO, mv[:, :, 0], mv[:, :, 0], ALU.mult))
                        dve.scalar_tensor_tensor(out=RO, in0=mv[:, :, 1], scalar=1e-6, in1=RO,
                                                 op0=ALU.add, op1=ALU.add).then_inc(s["mean_squares"], 1)
                        if more:
                            c.mark(square_high(h + 1))
                        at("o_rooted", 1)
                        c.step(dve.reciprocal(RO, RO))
                        at("gated", 1)
                        for g in range(2):
                            for t in range(4 * g, 4 * g + 4):
                                ins = dve.scalar_tensor_tensor(out=OO[:, t, :], in0=square(g, t), scalar=RO[:, t:t + 1],
                                                               in1=tiles(GW)[:, t, :], op0=ALU.mult, op1=ALU.mult)
                            ins.then_inc(s["onormed"], 1)
                        if more:
                            scale(h + 1, c)
                        for g in range(2):
                            at("out", g + 1)
                            x = XR[:, 4 * g:4 * g + 4, :].rearrange("p t f -> p (t f)")
                            dve.tensor_tensor(x, x, PS[:, 4 + g, :], ALU.add).then_inc(s["added"], 1)
                        at("added", 2)
                        if more:
                            scale_q(h + 1, c)
                        assert c.n == REST + (FRONT if more else 0)

                    table_decays(dve, s)
                    c = Chain(dve, s["vec"])
                    sum_low(0, c)
                    c.step(square_high(0))
                    scale(0, c)
                    scale_q(0, c)
                    assert c.n == FRONT
                    all_heads(dve, head)

        def l3_attn(counted):
            with phase() as (block, s):
                @block.sync
                def _(sp):
                    sp.dma_start(W4[:, :], d["L3a_w"]).then_inc(delta_loaded, 16)
                    sp.dma_start(EXTRA[:, 0:TOK], d["L3a_wo"]).then_inc(delta_loaded, 16)
            normalize(X, XR, HT, 1e-5)
            normalize(XR, XN, HT, 1e-6, rms=True)
            delta_heads()
            normalize(XR, XN, HT, 1e-6, rms=True)
            RR = [BIG[2][:, c * TOK:(c + 1) * TOK] for c in range(4)]
            with phase("made", "rect", "evac", "ymade", "added") as (block, s):
                @block.tensor
                def _(pe):
                    for c in range(4):
                        if c >= 2:
                            pe.wait_ge(s["rect"], c - 1)
                        for h in range(2):
                            mm = pe.matmul(PS[:, 2 * (c % 2) + h, :], w("L3a_fc")[:, c * P:(c + 1) * P],
                                           HT[:, h * HALF:(h + 1) * HALF], start=True, stop=True)
                        mm.then_inc(s["made"], 1)
                    pe.wait_ge(s["evac"], 4)
                    for t in range(TILES):
                        for c in range(4):
                            mm = pe.matmul(square(4 + t // 4, t), RR[c][:, t * P:(t + 1) * P],
                                           w("L3a_proj")[:, c * P:(c + 1) * P], start=c == 0, stop=c == 3)
                        mm.then_inc(s["ymade"], 1)

                @block.scalar
                def _(act):
                    for c in range(4):
                        act.wait_ge(s["made"], c + 1)
                        act.activation(halves(RR[c]), PS[:, 2 * (c % 2):2 * (c % 2) + 2, :], ACT.Relu).then_inc(s["rect"], 1)
                        act.wait_ge(s["rect"], c + 1)
                        act.activation(RR[c], RR[c], ACT.Square).then_inc(s["evac"], 1)

                @block.vector
                def _(dve):
                    whole = lambda a: a[:, :, :].rearrange("p t f -> p (t f)")
                    dve.tensor_tensor(whole(X), whole(X), whole(XR), ALU.add).then_inc(s["added"], 1)
                    dve.wait_ge(s["added"], 1)
                    for h in range(2):
                        dve.wait_ge(s["ymade"], 4 * h + 4)
                        x = X[:, 4 * h:4 * h + 4, :].rearrange("p t f -> p (t f)")
                        dve.tensor_tensor(x, x, PS[:, 4 + h, :], ALU.add).then_inc(s["added"], 1)
                    dve.wait_ge(s["added"], 3)

        def l3_ffn(counted):
            normalize(X, XN, HT, 1e-5, counted=counted)
            QMAX = 32767.0
            inv_q = float(np.float32(1.0) / np.float32(QMAX))
            WQ = EXTRA[:, 0:1152].rearrange("p (n i) -> p n i", n=36)
            WF = EXTRA[:, 0:1152]
            WD = EXTRA[:, 1152:2304]
            MB = EXTRA[:, 2304:2340]
            IB = EXTRA[:, 2340:2376]
            SC = EXTRA[:, 2400:2412]
            CM = EXTRA[:, 2416:2422]
            UP, GT, SG = BIG[0][:, 0:3072], BIG[1][:, 0:3072], BIG[2][:, 0:3072]
            blocks32 = lambda a: a.unsqueeze(2).broadcast_to([P, 36, 32])
            with phase("vec", "turned", "copied") as (block, s):
                @block.vector
                def _(dve):
                    c = Chain(dve, s["vec"])
                    src = w("L3f_w").rearrange("p (n i) -> p n i", n=36)
                    c.step(dve.tensor_reduce(MB, src, AX.X, ALU.max, apply_absolute_value=True))
                    c.step(dve.tensor_scalar(MB, MB, float(np.float32(1) / np.float32(7)), 1e-12, ALU.mult, ALU.max))
                    c.step(dve.reciprocal(IB, MB))
                    c.step(dve.tensor_tensor(WQ, src, blocks32(IB), ALU.mult))
                    c.step(dve.tensor_scalar(WF, WF, MAGIC, None, ALU.add))
                    c.step(dve.tensor_scalar(WF, WF, -MAGIC, -8.0, ALU.add, ALU.max))
                    c.step(dve.tensor_scalar(WF, WF, 7.0, None, ALU.min))
                    c.step(dve.tensor_tensor(WQ, WQ, blocks32(MB), ALU.mult))

                @block.tensor
                def _(pe):
                    pe.wait_ge(s["vec"], 8)
                    for n in range(9):
                        mm = pe.transpose(PS[:, n // 4, (n % 4) * P:(n % 4 + 1) * P], WF[:, n * P:(n + 1) * P], ident)
                    mm.then_inc(s["turned"], 1)

                @block.scalar
                def _(act):
                    act.wait_ge(s["turned"], 1)
                    act.activation(WD[:, 0:1024].rearrange("p (a b) -> p a b", a=2), PS[:, 0:2, :], ACT.Copy)\
                        .then_inc(s["copied"], 1)
                    act.activation(WD[:, 1024:1152], PS[:, 2, 0:P], ACT.Copy).then_inc(s["copied"], 1)

            def quantize(items, maxima=None, sigmoid=False):
                with phase("vec", "pooled", "signed") as (block, s):
                    if sigmoid:
                        @block.scalar
                        def _(act):
                            act.activation(idle[:, :], idle[:, :], ACT.Sigmoid)
                            act.wait_ge(s["vec"], 6)
                            act.activation(SG, GT, ACT.Sigmoid).then_inc(s["signed"], 1)

                    @block.gpsimd
                    def _(pool):
                        pool.wait_ge(s["vec"], 1)
                        n = len(items)
                        a = items[0][2]
                        pool.partition_all_reduce(SC[:, 6:6 + n], SC[:, a:a + n], P, bass.bass_isa.ReduceOp.max)\
                            .then_inc(s["pooled"], 1)

                    @block.vector
                    def _(dve):
                        c = Chain(dve, s["vec"])
                        n = len(items)
                        a = items[0][2]
                        for k, (src, dst, col) in enumerate(items):
                            ins = dve.tensor_reduce(SC[:, col:col + 1], maxima[k] if maxima else src, AX.X, ALU.max,
                                                    apply_absolute_value=True)
                            if k == n - 1:
                                c.mark(ins)
                        dve.wait_ge(s["pooled"], 1)
                        c.step(dve.tensor_scalar(SC[:, a:a + n], SC[:, 6:6 + n], inv_q, 1e-12, ALU.mult, ALU.max))
                        c.step(dve.reciprocal(SC[:, 8:8 + n], SC[:, a:a + n]))
                        for k, (src, dst, col) in enumerate(items):
                            c.step(dve.tensor_scalar(dst, src, SC[:, 8 + k:9 + k], MAGIC, ALU.mult, ALU.add))
                            c.step(dve.tensor_scalar(dst, dst, -MAGIC, -QMAX - 1.0, ALU.add, ALU.max))
                            c.step(dve.tensor_scalar(dst, dst, QMAX, SC[:, col:col + 1], ALU.min, ALU.mult))

            quantize([(HT[:, :], QT[:, :], 0)])
            with phase("made", "copied", "found") as (block, s):
                @block.vector
                def _(dve):
                    for n in range(6):
                        dve.wait_ge(s["copied"], n + 1)
                        o = (GT if n < 3 else UP)[:, (n % 3) * TOK:(n % 3 + 1) * TOK]
                        dve.tensor_reduce(CM[:, n:n + 1], o, AX.X, ALU.max, apply_absolute_value=True)\
                           .then_inc(s["found"], 1)

                @block.tensor
                def _(pe):
                    for n in range(6):
                        if n >= 4:
                            pe.wait_ge(s["copied"], n - 3)
                        for h in range(2):
                            mm = pe.matmul(PS[:, 2 * (n % 4) + h, :], WD[:, n * P:(n + 1) * P],
                                           QT[:, h * HALF:(h + 1) * HALF], start=True, stop=True)
                        mm.then_inc(s["made"], 1)

                @block.scalar
                def _(act):
                    for n in range(6):
                        act.wait_ge(s["made"], n + 1)
                        o = (GT if n < 3 else UP)[:, (n % 3) * TOK:(n % 3 + 1) * TOK]
                        act.activation(halves(o), PS[:, 2 * (n % 4):2 * (n % 4) + 2, :], ACT.Copy).then_inc(s["copied"], 1)
            quantize([(GT, GT, 0), (UP, UP, 1)], (CM[:, 0:3], CM[:, 3:6]), sigmoid=True)
            with phase("vec") as (block, s):
                @block.vector
                def _(dve):
                    c = Chain(dve, s["vec"])
                    c.step(dve.tensor_scalar(SG, SG, 65536.0, MAGIC, ALU.mult, ALU.add))
                    c.step(dve.tensor_scalar(SG, SG, -MAGIC, 0.0, ALU.add, ALU.max))
                    c.step(dve.tensor_scalar(SG, SG, 65535.0, 1.0 / 65536.0, ALU.min, ALU.mult))
                    c.step(dve.tensor_tensor(GT, GT, SG, ALU.mult))
            quantize([(GT, GT, 0)])
            with phase("vec") as (block, s):
                @block.vector
                def _(dve):
                    dve.tensor_tensor(UP, UP, GT, ALU.mult).then_inc(s["vec"], 1)
            quantize([(UP, UP, 0)])
            with phase("ymade", "added") as (block, s):
                @block.tensor
                def _(pe):
                    for t in range(TILES):
                        for c in range(3):
                            mm = pe.matmul(square(t // 4, t), UP[:, c * TOK + t * P:c * TOK + (t + 1) * P],
                                           WD[:, (6 + c) * P:(7 + c) * P], start=c == 0, stop=c == 2)
                    mm.then_inc(s["ymade"], 1)

                @block.vector
                def _(dve):
                    dve.wait_ge(s["ymade"], 1)
                    x = X[:, :, :].rearrange("p (a t) f -> p a (t f)", a=2)
                    dve.tensor_tensor(x, x, PS[:, 0:2, :], ALU.add).then_inc(s["added"], 1)

        def store():
            with phase("stored") as (block, s):
                @block.sync
                def _(sp):
                    sp.dma_start(out, X[:, :, :]).then_inc(s["stored"], 16)
                    sp.wait_ge(s["stored"], 16)

        def l0_attn(counted):
            normalize(X, XN, HT, 1e-5)
            qkv = w("L0a_qkv")
            token_qk(qkv[:, 0:P], qkv[:, P:2 * P], qkv[:, 2 * P:3 * P], True, HD ** -0.5)
            attend(w("L0a_o"), X, None, row("L0a_o"))

        def l0_xattn(counted):
            normalize_and_project((QT, w("L0x_q"), HT, None, HD ** -0.5), (KT, w("L0x_k"), CT, None, 1.0),
                                  (CT, w("L0x_v"), None), counted)
            with phase("rel") as (block, s):
                @block.sync
                def _(sp):
                    for b in range(PER):
                        sp.dma_start(REL[b * SEQ:(b + 1) * SEQ, :, :], d["rel"]).then_inc(s["rel"], 16)
                    sp.wait_ge(s["rel"], 32)
            attend(w("L0x_o"), X, "rel", row("L0x_o"))

        def l1_attn(counted):
            normalize(X, XN, HT, 1e-5)
            project([(QT, w("L1a_q"), HT, None, w("c_L1a_scale")), (KT, w("L1a_k"), HT, None, 1.0)],
                    (HT, w("L1a_v"), None))
            attend(w("L1a_o"), X, "strict", row("L1a_o"))

        def l2_xattn(counted):
            normalize_and_project((QT, w("L2x_q"), HT, None, HD ** -0.5), (KT, w("L2x_k"), CT, None, 1.0),
                                  (CT, w("L2x_v"), None), counted)
            attend(w("L2x_o"), X)

        def l3_xattn(counted):
            normalize_and_project((QT, w("L3x_q"), HT, w("c_L3x_bq"), HD ** -0.5),
                                  (KT, w("L3x_k"), CT, w("c_L3x_bk"), 1.0), (CT, w("L3x_v"), row("L3x_v")), counted)
            attend(w("L3x_o"), X, None, row("L3x_o"))

        blocks = [l0_attn, l0_xattn, l0_ffn, l1_attn, l1_xattn, l1_ffn, l2_attn, l2_xattn, l2_ffn, l3_attn, l3_xattn, l3_ffn]
        if first > 0:
            rest()
        after_attention = (l0_xattn, l0_ffn, l1_xattn, l2_ffn, l3_ffn)
        for f in blocks[first:last]:
            f(f in after_attention and f is not blocks[first])
            if f is l0_attn:
                rest()
        store()
        nc.clear_and_free_semaphores(used.pop() + [rest_loaded, delta_loaded])


def pack(inputs):
    g = {k: np.asarray(v) for k, v in inputs.items()}
    W = {}
    W["L0a_qkv"] = g["L0_attn_w_qkv"].T
    W["L0a_o"] = g["L0_attn_w_proj"].T
    W["L0x_q"], W["L0x_k"], W["L0x_v"], W["L0x_o"] = (g["L0_xattn_" + n].T for n in ("wq", "wk", "wv", "fc_w"))
    W["L0f_router"] = g["L0_ffn_router_weight"].T
    W["L0f_sw1"] = g["L0_ffn_sw1"].T
    W["L0f_sw2"] = g["L0_ffn_sw2"].T.reshape(2, P, P).transpose(1, 0, 2)
    q3 = g["L1_attn_w_qkv"]
    W["L1a_q"], W["L1a_k"], W["L1a_v"] = q3[:, 0:P], q3[:, P:2 * P], q3[:, 2 * P:]
    W["L1a_o"] = g["L1_attn_w_out"]
    for a, b in (("L1xs_", "L1_xattn_src_w"), ("L1xt_", "L1_xattn_tgt_w")):
        for n in "qkvo":
            W[a + n] = g[b + n]
    lw = g["L1_xattn_lstm_w"].reshape(3, P, 4, P)[:, :, [0, 2, 1, 3], :]
    W["L1x_wx"], W["L1x_wc"], W["L1x_wh"] = lw[0], lw[1], lw[2]
    W["L1x_w1"] = g["L1_xattn_ffn_w1"]
    W["L1x_w2"] = g["L1_xattn_ffn_w2"].reshape(4, P, P).transpose(1, 0, 2)
    q3 = g["L1_ffn_Wqkv"].reshape(P, HEADS, 3, HD)
    W["L1f_q"], W["L1f_k"], W["L1f_v"] = q3[:, :, 0], q3[:, :, 1], q3[:, :, 2]
    W["L1f_o"], W["L1f_gate"] = g["L1_ffn_Wproj"], g["L1_ffn_Wgate"]
    W["L2a_w"] = g["L2_attn_W"]
    W["L2x_q"], W["L2x_k"], W["L2x_v"], W["L2x_o"] = (g["L2_xattn_w_" + n].T for n in "qkvo")
    W["L2f_gate"] = g["L2_ffn_gate_w"]
    W["L3a_b"], W["L3a_a"], W["L3a_fc"] = g["L3_attn_Wb"], g["L3_attn_Wa"], g["L3_attn_W_fc"]
    W["L3a_proj"] = g["L3_attn_W_proj"].reshape(4, P, P).transpose(1, 0, 2)
    W["L3x_q"], W["L3x_k"], W["L3x_v"], W["L3x_o"] = (g["L3_xattn_W" + n].T for n in "qkvo")
    W["L3f_w"] = np.concatenate([g["L3_ffn_w_gate"].reshape(3, P, P), g["L3_ffn_w_up"].reshape(3, P, P),
                                 g["L3_ffn_w_down"].reshape(P, 3, P).transpose(1, 0, 2)]).transpose(1, 0, 2)
    W["c_L1a_scale"] = np.repeat(g["L1_attn_scale"].reshape(-1), HD)
    for a, b in (("L1xs_b", "L1_xattn_src_b"), ("L1xt_b", "L1_xattn_tgt_b"), ("L3x_b", "L3_xattn_b")):
        for n in "qk":
            W["c_" + a + n] = g[b + n]
    W["c_L1x_lstm_b"] = g["L1_xattn_lstm_b"].reshape(4, P)[[0, 2, 1, 3]].T
    W["c_L1x_b1"] = g["L1_xattn_ffn_b1"].reshape(4, P).T
    for n in ("ln1_g", "ln1_b", "ln2_g", "ln2_b"):
        W["c_" + n] = g["L1_ffn_" + n]
    W["c_L1f_b1"] = g["L1_ffn_b1"].reshape(32, P).T
    W["c_L2a_b"] = g["L2_attn_b"]
    W["c_tgt_bias"] = np.concatenate([g["L1_xattn_tgt_bias"].reshape(SEQ, SEQ)] * 2)
    R = {"L0a_o": g["L0_attn_b_proj"], "L0a_gamma": np.concatenate([g["L0_attn_q_gamma"], g["L0_attn_k_gamma"]]),
         "L0a_beta": np.concatenate([g["L0_attn_q_beta"], g["L0_attn_k_beta"]]), "L0x_o": g["L0_xattn_fc_b"],
         "L0f_bias": g["L0_ffn_expert_bias"], "L1a_o": g["L1_attn_b_out"], "L1xs_v": g["L1_xattn_src_bv"],
         "L1xt_v": g["L1_xattn_tgt_bv"], "L1xs_o": g["L1_xattn_src_bo"], "L1xt_o": g["L1_xattn_tgt_bo"],
         "L1x_b2": g["L1_xattn_ffn_b2"], "L2f_b": g["L2_ffn_gate_b"], "L3a_Alog": g["L3_attn_A_log"],
         "L3a_dt": g["L3_attn_dt_bias"], "L3a_norm": g["L3_attn_o_norm_w"], "L3x_v": g["L3_xattn_bv"],
         "L3x_o": g["L3_xattn_bo"]}
    a = {}
    a["x"] = g["x"].reshape(TILES, P, P).transpose(1, 0, 2)
    a["ctxT"] = g["ctx_1024"].reshape(TOK, P).T
    a["weights"] = np.concatenate([W[n].reshape(P, m) for n, m in WEIGHTS], 1)
    a["rows"] = np.concatenate([R[n].reshape(1, m) for n, m in ROWS], 1)
    a["consts"] = shape_constants()
    a["src_bias"] = g["mask_Bx1x1xS2_ff0"].reshape(TILES, PER, SEQ).transpose(1, 0, 2)
    q, k = np.arange(SEQ)[:, None], np.arange(SEQ)[None, :]
    a["rel"] = g["L0_xattn_rel_table"][k - q + 255].transpose(0, 2, 1)
    a["L0f_w1"] = g["L0_ffn_w1"].transpose(1, 0, 2).reshape(P, 4096)
    a["L0f_w2"] = g["L0_ffn_w2"].reshape(32, P, P).transpose(1, 0, 2).reshape(P, 4096)
    a["L1f_w1"] = g["L1_ffn_W1"].transpose(1, 0, 2).reshape(P, 4096)
    a["L1f_w2"] = g["L1_ffn_W2"].reshape(32, P, P).transpose(1, 0, 2).reshape(P, 4096)
    a["L1f_b2"] = g["L1_ffn_b2"]
    both = lambda e, s: np.concatenate([g["L2_ffn_" + e], g["L2_ffn_" + s]])
    a["L2f_w1"] = both("ew1", "sw1").transpose(1, 0, 2).reshape(P, 18 * 256)
    a["L2f_w3"] = both("ew3", "sw3").transpose(1, 0, 2).reshape(P, 18 * 256)
    a["L2f_w2"] = both("ew2", "sw2").reshape(36, P, P).transpose(1, 0, 2).reshape(P, 36 * P)
    a["L3a_w"] = np.concatenate([g["L3_attn_W" + n].reshape(P, 8, 1, P) for n in "qkvg"], 2).reshape(P, 4096)
    a["L3a_wo"] = g["L3_attn_Wo"].reshape(8, P, P).transpose(1, 0, 2).reshape(P, 1024)
    return {k: np.ascontiguousarray(v) for k, v in a.items()}


def kernel(**inputs):
    import concourse.bacc as _bacc
    from concourse.bass_utils import run_bass_kernel_spmd as _run

    nc = _bacc.Bacc("TRN2", target_bir_lowering=False, num_devices=1)
    arrays = pack(inputs)
    d = {k: nc.dram_tensor(k + "_dram", v.shape, F32, kind="ExternalInput").ap() for k, v in arrays.items()}
    out = nc.dram_tensor("out_dram", (P, TILES, P), F32, kind="ExternalOutput").ap()
    decoder_kernel(nc, d, out)
    r = _run(nc, [{k + "_dram": v for k, v in arrays.items()}], core_ids=[0])
    return r.results[0]["out_dram"].transpose(1, 0, 2).reshape(BATCH, SEQ, P)
```
